# Optimizing a Trainium2 kernel written in Bass

```python
import numpy as np
import jax
import jax.numpy as jnp

def _softmax(x, axis=-1):
    return jax.nn.softmax(x, axis=axis)

def _gelu(x):
    return jax.nn.gelu(x, approximate=True)

def _silu(x):
    return jax.nn.silu(x)

def _sigmoid(x):
    return jax.nn.sigmoid(x)

def _layernorm(x, axis=-1, eps=1e-05):
    m = jnp.mean(x, axis=axis, keepdims=True)
    v = jnp.var(x, axis=axis, keepdims=True)
    return (x - m) / jnp.sqrt(v + eps)

def _scatter_add(tgt, idx, src, axis=0):
    return tgt.at[idx].add(src)

def _segment_sum(src, seg, n):
    return jax.ops.segment_sum(src, seg, n)
kernel_name = 'mk_gnn_ffn_d4_gnn_r32_cfc230'

def setup_inputs(seed: int=0):
    np.random.seed(seed)
    _w = jnp.asarray

    def _rec_inputs():
        import jax
        import jax.numpy as jnp
        _gk = jax.random.key(seed)
        x = -0.0003713 + 1 * jax.random.normal(jax.random.fold_in(_gk, 1), (3125, 256), jnp.float32)
        src = jax.random.randint(jax.random.fold_in(_gk, 2), (50000,), 0, 3125, jnp.int32)
        dst = jax.random.randint(jax.random.fold_in(_gk, 3), (50000,), 0, 3125, jnp.int32)
        _o = jnp.argsort(dst, stable=True)
        src = src[_o]
        dst = dst[_o]
        return (x, src, dst)
    x, src, dst = _rec_inputs()

    def _L0_gnn_setup():
        import jax, jax.numpy as jnp
        import numpy as np
        N, IN_CH, HEADS, OUT_CH, E = (50000, 256, 4, 64, 25000)
        key = jax.random.key(seed)
        k1, k2, k3, k4, k5 = jax.random.split(key, 5)
        x = jax.random.normal(k1, (N, IN_CH), dtype=jnp.float32)
        edge_index = jax.random.randint(k2, (2, E), 0, N, dtype=jnp.int64)
        bw = float(np.sqrt(6.0 / (IN_CH + HEADS * OUT_CH)))
        ba = float(np.sqrt(6.0 / (HEADS + OUT_CH)))
        weight = jax.random.uniform(k3, (IN_CH, HEADS * OUT_CH), jnp.float32, -bw, bw)
        attn_l = jax.random.uniform(k4, (HEADS, OUT_CH), jnp.float32, -ba, ba)
        attn_r = jax.random.uniform(k5, (HEADS, OUT_CH), jnp.float32, -ba, ba)
        return {'x': x, 'edge_index': edge_index, 'weight': weight, 'attn_l': attn_l, 'attn_r': attn_r}
    _L0_gnn_all = _L0_gnn_setup()
    _L0_gnn_in = {k: v for k, v in _L0_gnn_all.items() if k in ('weight', 'attn_l', 'attn_r')}
    del _L0_gnn_all

    def _L0_ffn_setup():
        import jax, jax.numpy as jnp
        import numpy as np
        B, S, D = (8, 128, 256)
        H = 4 * D
        CAPACITY = 0.5
        key = jax.random.key(seed)
        ks = jax.random.split(key, 6)
        x = jax.random.normal(ks[0], (B, S, D), dtype=jnp.float32)
        attention_mask = jnp.zeros((B, 1, 1, S), dtype=jnp.float32)
        wr = jax.random.normal(ks[1], (D, 1), dtype=jnp.float32) * 0.02
        br = jnp.zeros((1,), dtype=jnp.float32)
        w1 = jax.random.normal(ks[2], (D, H), dtype=jnp.float32) * 0.02
        b1 = jnp.zeros((H,), dtype=jnp.float32)
        w2 = jax.random.normal(ks[3], (H, D), dtype=jnp.float32) * 0.02
        b2 = jnp.zeros((D,), dtype=jnp.float32)
        return {'x': x, 'attention_mask': attention_mask, 'wr': wr, 'br': br, 'w1': w1, 'b1': b1, 'w2': w2, 'b2': b2}
    _L0_ffn_all = _L0_ffn_setup()
    _L0_ffn_in = {k: v for k, v in _L0_ffn_all.items() if k in ('attention_mask', 'wr', 'br', 'w1', 'b1', 'w2', 'b2')}
    del _L0_ffn_all

    def _L1_gnn_setup():
        import jax, jax.numpy as jnp
        import numpy as np
        N_NODES = 50000
        N_EDGES = 25000
        DIM = 256

        def _gcn_forward(x, W, b, edge_index):
            n = x.shape[0]
            loop = jnp.arange(n, dtype=edge_index.dtype)
            src = jnp.concatenate([edge_index[0], loop])
            dst = jnp.concatenate([edge_index[1], loop])
            h = x @ W
            deg = jax.ops.segment_sum(jnp.ones_like(dst, dtype=h.dtype), dst, num_segments=n)
            dinv = jnp.where(deg > 0, jax.lax.rsqrt(deg), 0.0)
            norm = dinv[src] * dinv[dst]
            msg = h[src] * norm[:, None]
            out = jax.ops.segment_sum(msg, dst, num_segments=n) + b
            return out
        key = jax.random.key(seed)
        k1, k2, k3, k4 = jax.random.split(key, 4)
        x = jax.random.normal(k1, (N_NODES, DIM), dtype=jnp.float32)
        W = jax.random.normal(k2, (DIM, DIM), dtype=jnp.float32) * (1.0 / np.sqrt(DIM))
        b = jax.random.normal(k3, (DIM,), dtype=jnp.float32) * 0.01
        edge_index = jax.random.randint(k4, (2, N_EDGES), 0, N_NODES, dtype=jnp.int64)
        return {'x': x, 'W': W, 'b': b, 'edge_index': edge_index}
    _L1_gnn_all = _L1_gnn_setup()
    _L1_gnn_in = {k: v for k, v in _L1_gnn_all.items() if k in ('W', 'b')}
    del _L1_gnn_all

    def _L1_ffn_setup():
        import jax, jax.numpy as jnp
        import numpy as np
        DIM = 256
        H = 8
        D = 64
        G = 64
        INNER = H * D
        SCALE = D ** (-0.5)
        key = jax.random.key(seed)
        ks = jax.random.split(key, 12)
        B, N = (4, 512)
        x = jax.random.normal(ks[0], (B, N, DIM), dtype=jnp.float32)
        s = lambda fan_in: 1.0 / np.sqrt(fan_in)
        W_fx = jax.random.normal(ks[1], (DIM, INNER), dtype=jnp.float32) * s(DIM)
        b_fx = jnp.zeros((INNER,), dtype=jnp.float32)
        W_x = jax.random.normal(ks[2], (DIM, INNER), dtype=jnp.float32) * s(DIM)
        b_x = jnp.zeros((INNER,), dtype=jnp.float32)
        A = jax.random.normal(ks[3], (G, D), dtype=jnp.float32)
        Q, _ = jnp.linalg.qr(A.T)
        W_slice = Q[:, :G].astype(jnp.float32)
        b_slice = jnp.zeros((G,), dtype=jnp.float32)
        W_q = jax.random.normal(ks[4], (D, D), dtype=jnp.float32) * s(D)
        W_k = jax.random.normal(ks[5], (D, D), dtype=jnp.float32) * s(D)
        W_v = jax.random.normal(ks[6], (D, D), dtype=jnp.float32) * s(D)
        W_out = jax.random.normal(ks[7], (INNER, DIM), dtype=jnp.float32) * s(INNER)
        b_out = jnp.zeros((DIM,), dtype=jnp.float32)
        temperature = jnp.ones((1, H, 1, 1), dtype=jnp.float32) * 0.5
        return {'x': x, 'W_fx': W_fx, 'b_fx': b_fx, 'W_x': W_x, 'b_x': b_x, 'W_slice': W_slice, 'b_slice': b_slice, 'W_q': W_q, 'W_k': W_k, 'W_v': W_v, 'W_out': W_out, 'b_out': b_out, 'temperature': temperature}
    _L1_ffn_all = _L1_ffn_setup()
    _L1_ffn_in = {k: v for k, v in _L1_ffn_all.items() if k in ('W_fx', 'b_fx', 'W_x', 'b_x', 'W_slice', 'b_slice', 'W_q', 'W_k', 'W_v', 'W_out', 'b_out', 'temperature')}
    del _L1_ffn_all

    def _L2_gnn_setup():
        import jax, jax.numpy as jnp
        import numpy as np
        N_NODES = 50000
        N_EDGES = 25000
        D_IN = 256
        D_OUT = 256
        key = jax.random.key(seed)
        k1, k2, k3 = jax.random.split(key, 3)
        x = jax.random.normal(k1, (N_NODES, D_IN), dtype=jnp.float32)
        edge_index = jax.random.randint(k2, (2, N_EDGES), 0, N_NODES, dtype=jnp.int64)
        W = jax.random.normal(k3, (D_IN, D_OUT), dtype=jnp.float32) * (1.0 / np.sqrt(D_IN))
        b = jnp.zeros((D_OUT,), dtype=jnp.float32)
        return {'x': x, 'edge_index': edge_index, 'W': W, 'b': b}
    _L2_gnn_all = _L2_gnn_setup()
    _L2_gnn_in = {k: v for k, v in _L2_gnn_all.items() if k in ('W', 'b')}
    del _L2_gnn_all

    def _L2_ffn_setup():
        import jax, jax.numpy as jnp
        import numpy as np
        NUM_EXPERTS = 8
        TOP_K = 2
        B, S, D = (8, 256, 256)

        def _moe(tokens, router_w, w1, b1, w2, b2):
            N = tokens.shape[0]
            E = router_w.shape[0]
            logits = tokens.astype(jnp.float32) @ router_w.astype(jnp.float32).T
            probs = jax.nn.softmax(logits, axis=-1)
            rw, re = jax.lax.top_k(probs, TOP_K)
            if TOP_K > 1:
                rw = rw / jnp.maximum(rw.sum(-1, keepdims=True), 1e-12)
            rw = rw.astype(tokens.dtype)
            combine = jnp.zeros((N, E), tokens.dtype).at[jnp.arange(N)[:, None], re].set(rw)
            out = tokens
            for e in range(E):
                h = jax.nn.gelu(tokens @ w1[e] + b1[e], approximate=False)
                y = h @ w2[e] + b2[e]
                out = out + combine[:, e:e + 1] * y
            return out
        key = jax.random.key(seed)
        ks = jax.random.split(key, 4)
        scale = 1.0 / np.sqrt(D).astype(np.float32)
        return {'input_embeddings': jax.random.normal(ks[0], (B, S, D), jnp.float32), 'router_w': jax.random.normal(ks[1], (NUM_EXPERTS, D), jnp.float32) * scale, 'w1': jax.random.normal(ks[2], (NUM_EXPERTS, D, D), jnp.float32) * scale, 'b1': jnp.zeros((NUM_EXPERTS, D), jnp.float32), 'w2': jax.random.normal(ks[3], (NUM_EXPERTS, D, D), jnp.float32) * scale, 'b2': jnp.zeros((NUM_EXPERTS, D), jnp.float32)}
    _L2_ffn_all = _L2_ffn_setup()
    _L2_ffn_in = {k: v for k, v in _L2_ffn_all.items() if k in ('router_w', 'w1', 'b1', 'w2', 'b2')}
    del _L2_ffn_all

    def _L3_gnn_setup():
        import jax, jax.numpy as jnp
        import numpy as np
        N_NODES = 50000
        N_EDGES = 50000
        H_SIZE = 256
        HEADS = 8
        HEAD_DIM = H_SIZE // HEADS
        NEG_SLOPE = 0.2
        key = jax.random.key(seed)
        k_x, k_e, k_w, k_as, k_ad, k_b = jax.random.split(key, 6)
        x = jax.random.normal(k_x, (N_NODES, H_SIZE), dtype=jnp.float32)
        edge_index = jax.random.randint(k_e, (2, N_EDGES), 0, N_NODES, dtype=jnp.int64)
        scale = 1.0 / np.sqrt(H_SIZE)
        W = jax.random.normal(k_w, (H_SIZE, HEADS, HEAD_DIM), dtype=jnp.float32) * scale
        att_src = jax.random.normal(k_as, (HEADS, HEAD_DIM), dtype=jnp.float32) * scale
        att_dst = jax.random.normal(k_ad, (HEADS, HEAD_DIM), dtype=jnp.float32) * scale
        bias = jnp.zeros((H_SIZE,), dtype=jnp.float32)
        return {'x': x, 'edge_index': edge_index, 'W': W, 'att_src': att_src, 'att_dst': att_dst, 'bias': bias}
    _L3_gnn_all = _L3_gnn_setup()
    _L3_gnn_in = {k: v for k, v in _L3_gnn_all.items() if k in ('W', 'att_src', 'att_dst', 'bias')}
    del _L3_gnn_all

    def _L3_ffn_setup():
        import math
        import jax, jax.numpy as jnp
        import numpy as np
        CAPACITY_FACTOR = 1.25
        TOP_K = 2
        LN_EPS = 1e-05

        def _layer_norm(x, gamma, beta):
            mu = jnp.mean(x, axis=-1, keepdims=True)
            var = jnp.var(x, axis=-1, keepdims=True)
            return (x - mu) * jax.lax.rsqrt(var + LN_EPS) * gamma + beta
        key = jax.random.key(seed)
        ks = jax.random.split(key, 4)
        B, S, D, F, E = (8, 128, 256, 512, 8)
        x = jax.random.normal(ks[0], (B, S, D), dtype=jnp.float32)
        Wr = jax.random.normal(ks[1], (D, E), dtype=jnp.float32) / np.sqrt(D)
        br = jnp.zeros((E,), jnp.float32)
        W1 = jax.random.normal(ks[2], (E, D, F), dtype=jnp.float32) / np.sqrt(D)
        b1 = jnp.zeros((E, F), jnp.float32)
        W2 = jax.random.normal(ks[3], (E, F, D), dtype=jnp.float32) / np.sqrt(F)
        b2 = jnp.zeros((E, D), jnp.float32)
        gamma = jnp.ones((D,), jnp.float32)
        beta = jnp.zeros((D,), jnp.float32)
        return {'x': x, 'Wr': Wr, 'br': br, 'W1': W1, 'b1': b1, 'W2': W2, 'b2': b2, 'gamma': gamma, 'beta': beta}
    _L3_ffn_all = _L3_ffn_setup()
    _L3_ffn_in = {k: v for k, v in _L3_ffn_all.items() if k in ('Wr', 'br', 'W1', 'b1', 'W2', 'b2', 'gamma', 'beta')}
    del _L3_ffn_all
    return {'x': x, 'src': src, 'dst': dst, 'L0_gnn_weight': _L0_gnn_in['weight'], 'L0_gnn_attn_l': _L0_gnn_in['attn_l'], 'L0_gnn_attn_r': _L0_gnn_in['attn_r'], 'L0_ffn_attention_mask': _L0_ffn_in['attention_mask'], 'L0_ffn_wr': _L0_ffn_in['wr'], 'L0_ffn_br': _L0_ffn_in['br'], 'L0_ffn_w1': _L0_ffn_in['w1'], 'L0_ffn_b1': _L0_ffn_in['b1'], 'L0_ffn_w2': _L0_ffn_in['w2'], 'L0_ffn_b2': _L0_ffn_in['b2'], 'L1_gnn_W': _L1_gnn_in['W'], 'L1_gnn_b': _L1_gnn_in['b'], 'L1_ffn_W_fx': _L1_ffn_in['W_fx'], 'L1_ffn_b_fx': _L1_ffn_in['b_fx'], 'L1_ffn_W_x': _L1_ffn_in['W_x'], 'L1_ffn_b_x': _L1_ffn_in['b_x'], 'L1_ffn_W_slice': _L1_ffn_in['W_slice'], 'L1_ffn_b_slice': _L1_ffn_in['b_slice'], 'L1_ffn_W_q': _L1_ffn_in['W_q'], 'L1_ffn_W_k': _L1_ffn_in['W_k'], 'L1_ffn_W_v': _L1_ffn_in['W_v'], 'L1_ffn_W_out': _L1_ffn_in['W_out'], 'L1_ffn_b_out': _L1_ffn_in['b_out'], 'L1_ffn_temperature': _L1_ffn_in['temperature'], 'L2_gnn_W': _L2_gnn_in['W'], 'L2_gnn_b': _L2_gnn_in['b'], 'L2_ffn_router_w': _L2_ffn_in['router_w'], 'L2_ffn_w1': _L2_ffn_in['w1'], 'L2_ffn_b1': _L2_ffn_in['b1'], 'L2_ffn_w2': _L2_ffn_in['w2'], 'L2_ffn_b2': _L2_ffn_in['b2'], 'L3_gnn_W': _L3_gnn_in['W'], 'L3_gnn_att_src': _L3_gnn_in['att_src'], 'L3_gnn_att_dst': _L3_gnn_in['att_dst'], 'L3_gnn_bias': _L3_gnn_in['bias'], 'L3_ffn_Wr': _L3_ffn_in['Wr'], 'L3_ffn_br': _L3_ffn_in['br'], 'L3_ffn_W1': _L3_ffn_in['W1'], 'L3_ffn_b1': _L3_ffn_in['b1'], 'L3_ffn_W2': _L3_ffn_in['W2'], 'L3_ffn_b2': _L3_ffn_in['b2'], 'L3_ffn_gamma': _L3_ffn_in['gamma'], 'L3_ffn_beta': _L3_ffn_in['beta']}

def reference(x, src, dst, L0_gnn_weight, L0_gnn_attn_l, L0_gnn_attn_r, L0_ffn_attention_mask, L0_ffn_wr, L0_ffn_br, L0_ffn_w1, L0_ffn_b1, L0_ffn_w2, L0_ffn_b2, L1_gnn_W, L1_gnn_b, L1_ffn_W_fx, L1_ffn_b_fx, L1_ffn_W_x, L1_ffn_b_x, L1_ffn_W_slice, L1_ffn_b_slice, L1_ffn_W_q, L1_ffn_W_k, L1_ffn_W_v, L1_ffn_W_out, L1_ffn_b_out, L1_ffn_temperature, L2_gnn_W, L2_gnn_b, L2_ffn_router_w, L2_ffn_w1, L2_ffn_b1, L2_ffn_w2, L2_ffn_b2, L3_gnn_W, L3_gnn_att_src, L3_gnn_att_dst, L3_gnn_bias, L3_ffn_Wr, L3_ffn_br, L3_ffn_W1, L3_ffn_b1, L3_ffn_W2, L3_ffn_b2, L3_ffn_gamma, L3_ffn_beta):
    import jax
    import jax.numpy as jnp

    def _L0_gnn_ref(x, edge_index, weight, attn_l, attn_r):
        import jax, jax.numpy as jnp
        import numpy as np
        N, IN_CH, HEADS, OUT_CH, E = (50000, 256, 4, 64, 25000)
        heads, out_ch = attn_l.shape
        n = x.shape[0]
        xt = jnp.matmul(x, weight).reshape(-1, heads, out_ch)
        row, col = (edge_index[0], edge_index[1])
        alpha_l = jnp.einsum('ehd,hd->eh', xt[row], attn_l)
        alpha_r = jnp.einsum('ehd,hd->eh', xt[col], attn_r)
        alpha = jax.nn.softmax(jax.nn.leaky_relu(alpha_l + alpha_r, 0.01), axis=1)
        tmp = jnp.einsum('nh,nhd->nd', alpha[:n], xt[col[:n]])
        out = jnp.broadcast_to(tmp[:, None, :], (n, heads, out_ch))
        return out.reshape(n, heads * out_ch)

    def _L0_ffn_ref(x, attention_mask, wr, br, w1, b1, w2, b2):
        import jax, jax.numpy as jnp
        import numpy as np
        B, S, D = (8, 128, 256)
        H = 4 * D
        CAPACITY = 0.5
        b, s, d = x.shape
        weights = (jnp.einsum('bsd,do->bso', x, wr) + br)[..., 0]
        k = max(1, int(CAPACITY * s))
        kk = k - 1 if k > 1 else 1
        _, idx = jax.lax.top_k(weights, k)
        sel_idx = idx[:, :kk]
        sel = jnp.take_along_axis(x, sel_idx[:, :, None], axis=1)
        h = jax.nn.gelu(jnp.einsum('bkd,dh->bkh', sel, w1) + b1)
        y = jnp.einsum('bkh,hd->bkd', h, w2) + b2
        w_sel = jnp.take_along_axis(weights, sel_idx, axis=1)
        y = y * w_sel[..., None]
        batch_idx = jnp.arange(b)[:, None]
        processed = jnp.zeros_like(x).at[batch_idx, sel_idx].set(y)
        return processed + x

    def _L1_gnn_ref(x, W, b, edge_index):
        import jax, jax.numpy as jnp
        import numpy as np
        N_NODES = 50000
        N_EDGES = 25000
        DIM = 256

        def _gcn_forward(x, W, b, edge_index):
            n = x.shape[0]
            loop = jnp.arange(n, dtype=edge_index.dtype)
            src = jnp.concatenate([edge_index[0], loop])
            dst = jnp.concatenate([edge_index[1], loop])
            h = x @ W
            deg = jax.ops.segment_sum(jnp.ones_like(dst, dtype=h.dtype), dst, num_segments=n)
            dinv = jnp.where(deg > 0, jax.lax.rsqrt(deg), 0.0)
            norm = dinv[src] * dinv[dst]
            msg = h[src] * norm[:, None]
            out = jax.ops.segment_sum(msg, dst, num_segments=n) + b
            return out
        return jax.nn.relu(_gcn_forward(x, W, b, edge_index))

    def _L1_ffn_ref(x, W_fx, b_fx, W_x, b_x, W_slice, b_slice, W_q, W_k, W_v, W_out, b_out, temperature):
        import jax, jax.numpy as jnp
        import numpy as np
        DIM = 256
        H = 8
        D = 64
        G = 64
        INNER = H * D
        SCALE = D ** (-0.5)
        B, N, _ = x.shape
        fx_mid = (x @ W_fx + b_fx).reshape(B, N, H, D).transpose(0, 2, 1, 3)
        x_mid = (x @ W_x + b_x).reshape(B, N, H, D).transpose(0, 2, 1, 3)
        temp = jnp.clip(temperature, 0.1, 5.0)
        slice_weights = jax.nn.softmax((x_mid @ W_slice + b_slice) / temp, axis=-1)
        slice_norm = slice_weights.sum(axis=2)
        slice_token = jnp.einsum('bhnc,bhng->bhgc', fx_mid, slice_weights)
        slice_token = slice_token / (slice_norm[..., None] + 1e-05)
        q = slice_token @ W_q
        k = slice_token @ W_k
        v = slice_token @ W_v
        attn = jax.nn.softmax(jnp.einsum('bhgc,bhkc->bhgk', q, k) * SCALE, axis=-1)
        out_slice = jnp.einsum('bhgk,bhkc->bhgc', attn, v)
        out_x = jnp.einsum('bhgc,bhng->bhnc', out_slice, slice_weights)
        out_x = out_x.transpose(0, 2, 1, 3).reshape(B, N, INNER)
        return out_x @ W_out + b_out

    def _L2_gnn_ref(x, edge_index, W, b):
        import jax, jax.numpy as jnp
        import numpy as np
        N_NODES = 50000
        N_EDGES = 25000
        D_IN = 256
        D_OUT = 256
        N = x.shape[0]
        loops = jnp.arange(N, dtype=edge_index.dtype)
        src = jnp.concatenate([edge_index[0], loops])
        dst = jnp.concatenate([edge_index[1], loops])
        deg = jax.ops.segment_sum(jnp.ones_like(dst, dtype=x.dtype), dst, num_segments=N)
        dinv = jax.lax.rsqrt(deg)
        norm = dinv[src] * dinv[dst]
        xw = jnp.matmul(x, W)
        msg = xw[src] * norm[:, None]
        agg = jax.ops.segment_sum(msg, dst, num_segments=N)
        return jax.nn.relu(agg + b)

    def _L2_ffn_ref(input_embeddings, router_w, w1, b1, w2, b2):
        import jax, jax.numpy as jnp
        import numpy as np
        NUM_EXPERTS = 8
        TOP_K = 2
        B, S, D = (8, 256, 256)

        def _moe(tokens, router_w, w1, b1, w2, b2):
            N = tokens.shape[0]
            E = router_w.shape[0]
            logits = tokens.astype(jnp.float32) @ router_w.astype(jnp.float32).T
            probs = jax.nn.softmax(logits, axis=-1)
            rw, re = jax.lax.top_k(probs, TOP_K)
            if TOP_K > 1:
                rw = rw / jnp.maximum(rw.sum(-1, keepdims=True), 1e-12)
            rw = rw.astype(tokens.dtype)
            combine = jnp.zeros((N, E), tokens.dtype).at[jnp.arange(N)[:, None], re].set(rw)
            out = tokens
            for e in range(E):
                h = jax.nn.gelu(tokens @ w1[e] + b1[e], approximate=False)
                y = h @ w2[e] + b2[e]
                out = out + combine[:, e:e + 1] * y
            return out
        b, s, d = input_embeddings.shape
        tokens = input_embeddings.reshape(b * s, d)
        return _moe(tokens, router_w, w1, b1, w2, b2).reshape(b, s, d)

    def _L3_gnn_ref(x, edge_index, W, att_src, att_dst, bias):
        import jax, jax.numpy as jnp
        import numpy as np
        N_NODES = 50000
        N_EDGES = 50000
        H_SIZE = 256
        HEADS = 8
        HEAD_DIM = H_SIZE // HEADS
        NEG_SLOPE = 0.2
        'GATConv (concat heads) -> relu -> dropout(eval=identity).\n\n            x: [N, F]; edge_index: [2, E] with (src=row0, dst=row1) meaning message j->i.\n            '
        N = x.shape[0]
        h = jnp.einsum('nf,fhd->nhd', x, W)
        a_src = jnp.sum(h * att_src, axis=-1)
        a_dst = jnp.sum(h * att_dst, axis=-1)
        src = edge_index[0]
        dst = edge_index[1]
        e = jax.nn.leaky_relu(a_src[src] + a_dst[dst], NEG_SLOPE)
        e_max = jax.ops.segment_max(e, dst, num_segments=N)
        e_exp = jnp.exp(e - e_max[dst])
        denom = jax.ops.segment_sum(e_exp, dst, num_segments=N)
        alpha = e_exp / (denom[dst] + 1e-16)
        msg = h[src] * alpha[:, :, None]
        out = jax.ops.segment_sum(msg, dst, num_segments=N)
        out = out.reshape(N, -1) + bias
        return jax.nn.relu(out)

    def _L3_ffn_ref(x, Wr, br, W1, b1, W2, b2, gamma, beta):
        import math
        import jax, jax.numpy as jnp
        import numpy as np
        CAPACITY_FACTOR = 1.25
        TOP_K = 2
        LN_EPS = 1e-05

        def _layer_norm(x, gamma, beta):
            mu = jnp.mean(x, axis=-1, keepdims=True)
            var = jnp.var(x, axis=-1, keepdims=True)
            return (x - mu) * jax.lax.rsqrt(var + LN_EPS) * gamma + beta
        B, S, D = x.shape
        E = Wr.shape[1]
        N = B * S
        K = TOP_K
        logits = jnp.mean(x, axis=1) @ Wr + br
        routing_weights = jax.nn.softmax(logits, axis=-1)
        capacity = float(math.ceil(N * CAPACITY_FACTOR / E))
        expected_loads = routing_weights.sum(axis=0) * (N / B)
        scale = jnp.where(expected_loads > capacity, capacity / expected_loads, 1.0)
        routing_weights = jax.nn.softmax(routing_weights * scale, axis=-1)
        rw_tok = jnp.broadcast_to(routing_weights[:, None, :], (B, S, E)).reshape(N, E)
        top_w, top_i = jax.lax.top_k(rw_tok, K)
        top_w = jax.nn.softmax(top_w, axis=-1)
        xf = x.reshape(N, D)
        h = jax.nn.gelu(jnp.einsum('nd,edf->enf', xf, W1) + b1[:, None, :], approximate=False)
        y = jnp.einsum('enf,efd->end', h, W2) + b2[:, None, :]
        w_dense = jnp.zeros((N, E), x.dtype).at[jnp.arange(N)[:, None], top_i].add(top_w)
        out = jnp.einsum('ne,end->nd', w_dense, y).reshape(B, S, D)
        out = _layer_norm(out + x, gamma, beta)
        return out
    edge_index = jnp.stack([src, dst])
    x = x + _L0_gnn_ref(_layernorm(x, axis=-1), edge_index, L0_gnn_weight, L0_gnn_attn_l, L0_gnn_attn_r)
    x = x + _L0_ffn_ref(_layernorm(x, axis=-1)[None], L0_ffn_attention_mask, L0_ffn_wr, L0_ffn_br, L0_ffn_w1, L0_ffn_b1, L0_ffn_w2, L0_ffn_b2)[0]
    x = x + _L1_gnn_ref(_layernorm(x, axis=-1), L1_gnn_W, L1_gnn_b, edge_index)
    x = x + _L1_ffn_ref(_layernorm(x, axis=-1)[None], L1_ffn_W_fx, L1_ffn_b_fx, L1_ffn_W_x, L1_ffn_b_x, L1_ffn_W_slice, L1_ffn_b_slice, L1_ffn_W_q, L1_ffn_W_k, L1_ffn_W_v, L1_ffn_W_out, L1_ffn_b_out, L1_ffn_temperature)[0]
    x = x + _L2_gnn_ref(_layernorm(x, axis=-1), edge_index, L2_gnn_W, L2_gnn_b)
    x = x + _L2_ffn_ref(_layernorm(x, axis=-1)[None], L2_ffn_router_w, L2_ffn_w1, L2_ffn_b1, L2_ffn_w2, L2_ffn_b2)[0]
    x = x + _L3_gnn_ref(_layernorm(x, axis=-1), edge_index, L3_gnn_W, L3_gnn_att_src, L3_gnn_att_dst, L3_gnn_bias)
    x = x + _L3_ffn_ref(_layernorm(x, axis=-1)[None], L3_ffn_Wr, L3_ffn_br, L3_ffn_W1, L3_ffn_b1, L3_ffn_W2, L3_ffn_b2, L3_ffn_gamma, L3_ffn_beta)[0]
    return x

_drawn_inputs = setup_inputs


def setup_inputs(seed=0):
    import zlib

    import numpy as np

    out = dict(_drawn_inputs(seed))
    spreads = {'L0_ffn_b1': (0.0, 0.8),
     'L0_ffn_b2': (0.0, 0.553),
     'L1_ffn_b_fx': (0.0, 0.1),
     'L1_ffn_b_x': (0.0, 0.8),
     'L1_ffn_b_slice': (0.0, 2.0),
     'L1_ffn_b_out': (0.0, 0.1),
     'L1_ffn_temperature': (0.5, 0.6),
     'L2_gnn_b': (0.0, 0.1),
     'L2_ffn_b1': (0.0, 0.526),
     'L2_ffn_b2': (0.0, 0.338),
     'L3_gnn_bias': (0.0, 0.422),
     'L3_ffn_br': (0.0, 0.8),
     'L3_ffn_b1': (0.0, 0.719),
     'L3_ffn_b2': (0.0, 0.48),
     'L3_ffn_gamma': (1.0, 0.2),
     'L3_ffn_beta': (0.0, 0.349)}
    factors = {'L0_ffn_wr': 3.428,
     'L0_ffn_w1': 4.143,
     'L0_ffn_w2': 3.635,
     'L1_gnn_b': 8.0,
     'L1_ffn_W_x': 8.0,
     'L1_ffn_W_slice': 8.0,
     'L1_ffn_W_q': 8.0,
     'L1_ffn_W_k': 8.0,
     'L3_gnn_att_src': 4.09,
     'L3_gnn_att_dst': 21.518}
    for name, (base, spread) in spreads.items():
        noise = np.random.default_rng([zlib.crc32(name.encode()), seed]).standard_normal(out[name].shape)
        drawn = base * np.exp(spread * noise) if base else spread * noise
        out[name] = jnp.asarray(drawn.astype(out[name].dtype))
    for name, factor in factors.items():
        out[name] = (out[name] * factor).astype(out[name].dtype)
    return out
```

```python
import concourse.bass as bass
from concourse import mybir
from contextlib import ExitStack

F32 = mybir.dt.float32
I32 = mybir.dt.int32
BF16 = mybir.dt.bfloat16
ALU = mybir.AluOpType
ACT = mybir.ActivationFunctionType
AX = mybir.AxisListType
ds = bass.ds

P = 128
D = 256
KB = D // P
N_NODES = 3125
N_EDGES = 50000
NT = (N_NODES + P - 1) // P
REST = N_NODES - (NT - 1) * P
CH = 5
NC = NT // CH
CW = CH * P
HALF = CW // 2
ROW = 264
ET = 392
SLOTS = 416
GRP = 8
NG = 4
BODY = GRP * NG
TURNS = SLOTS // BODY
LN_EPS = 1e-5
KSEL = 1561
CAP3 = float(-(-N_NODES * 5 // 4 // 8))
ORDER = ("g0", "f0", "g1", "t1", "g2", "m2", "g3", "f3", "n3")
GNNS = ("g0", "g1", "g2", "g3")
BIG_NUM = 3.0e38
AHEAD = 5


def tiles_before(st):
    return NT * ORDER.index(st)


def rows_before(st):
    return NT * GNNS.index(st)


class Chain:

    def __init__(self, sem):
        self.sem, self.done, self.turn = sem, 0, 0

    def mark(self, ins):
        ins.then_inc(self.sem, 1)
        self.done += 1

    def sync(self, eng):
        eng.wait_ge(self.sem, self.turn + self.done)

    def step(self, eng, ins):
        self.mark(ins)
        self.sync(eng)

    def enter(self, i, per):
        self.turn, self.first = i * per, self.done

    def leave(self, n, per):
        assert self.done - self.first == per, (self.done - self.first, per)
        self.done, self.turn = self.first + n * per, 0


def build(nc, a, out):
    ctx = ExitStack()
    with ctx:
        def sb(name, shape, dt=F32):
            return ctx.enter_context(nc.sbuf_tensor(name, shape, dt))

        sems = {}

        def sem(name):
            if name not in sems:
                sems[name] = ctx.enter_context(nc.semaphore(name))
            return sems[name]

        X = sb("X", [P, NT * D])
        ACC = sb("ACC", [P, NT * ROW])
        BIG = sb("BIG", [P, 12800])
        XS = sb("XS", [P, CH * D])
        XT = sb("XT", [P, KB * CW])
        WA = sb("WA", [P, 4096])
        WB = sb("WB", [P, 4096])
        WG = sb("WG", [P, KB * 272])
        SW = sb("SW", [P, CH * 512])
        OH = sb("OH", [P, 2 * GRP * P])
        SRCI = sb("SRCI", [P, SLOTS + GRP * NG], I32)
        DREL = sb("DREL", [P, SLOTS + GRP * NG])
        IDX = sb("IDX", [P, NG * GRP], I32)
        WROW = sb("WROW", [1, 512], I32)
        IDENT = sb("IDENT", [P, P])
        ONES = sb("ONES", [P, P])
        IOTA = sb("IOTA", [P, P])
        IOTAB = sb("IOTAB", [P, P], BF16)
        ZEROB = sb("ZEROB", [P, NT], BF16)
        IOTAP = sb("IOTAP", [P, 4])
        LOWER = sb("LOWER", [P, P])
        MASK = sb("MASK", [P, NT])
        ST6 = sb("ST6", [P, NT * 6])
        MEAN = sb("MEAN", [P, NT])
        VAR = sb("VAR", [P, NT])
        RSTD = sb("RSTD", [P, NT])
        NMR = sb("NMR", [P, NT])
        ONEP = sb("ONEP", [P, NT])
        T1 = sb("T1", [P, NT])
        T2 = sb("T2", [P, NT])
        DINV = sb("DINV", [P, NT])
        SMALL = sb("SMALL", [P, 6 * 200])
        IDN = sb("IDN", [P, 2 * NT], I32)
        SLI = sb("SLI", [P, 4], I32)
        SLF = sb("SLF", [P, 16])
        TMP = sb("TMP", [P, 2 * ROW])
        COEF = sb("COEF", [P, NT])
        CSTB = sb("CSTB", [P, 13 * D])
        B1 = sb("B1", [P, 16])
        PB = [ctx.enter_context(nc.psum_tensor(f"PB{i}", [P, 512], F32)) for i in range(8)]

        table = nc.dram_tensor("table", (NT * P, ROW), F32, kind="Internal").ap()
        wtab = nc.dram_tensor("wtab", (1, NT * P), F32, kind="Internal").ap()

        G = BIG[:, 0:BODY * ROW]
        RANKROW = BIG[:, 5120:5120 + NT * P]
        JUNK = BIG[:, 5120 + NT * P:5120 + 2 * NT * P]
        HT = BIG[:, 0:8 * CW]
        dst2 = SW[:, 0:ET].bitcast(I32)
        dlo = SW[:, ET:2 * ET].bitcast(I32)
        dhi = SW[:, 2 * ET:3 * ET].bitcast(I32)
        dlob = SW[:, 3 * ET:3 * ET + ET // 2].bitcast(BF16)
        dhib = SW[:, 4 * ET:4 * ET + ET // 2].bitcast(BF16)
        HB = 7
        ob = OH[:, 0:HB * P].bitcast(BF16)
        oa = TMP[:, 0:HB * NT].bitcast(BF16)
        slot_src = SW[:, 0:512].bitcast(I32)
        slot_dst = SW[:, 512:1024].bitcast(I32)
        slot_srcf = SW[:, 1024:1536]
        slot_dstf = SW[:, 1536:2048]
        ADS = SMALL[:, 0:200]

        def tile(buf, t, w=D, stride=D):
            return buf[:, ds(t * stride, w)]

        GW = 272
        WXS, WFX = WA[:, 0:1024], WA[:, 1024:2048]
        WXT = WA[0:64, 2048:4096]
        WSL, WQ, WK, WV = (WB[0:64, 64 * n:64 * n + 64] for n in range(4))
        WOUT = WB[0:64, 256:2304]
        BX, BXR = WB[0:64, 2304:2312], WB[0:64, 2312:3336]
        BFX, BOUT, TEMPC = WB[0:1, 3336:3848], WB[:, 3848:3850], WB[:, 3850:3858]
        BSL, RTEMP = WB[:, 3858:3922], WB[:, 3922:3930]
        LBIAS = CSTB[:, 9 * D:11 * D]
        SWT = BIG[:, :]
        VW, MO, MM = ACC[0:64, 0:2048], ACC[0:64, 2048:3072], ACC[:, 4096:5120]
        TOKT = XS[:, 0:1024]
        NORM, RN, RNB, KT, VT = SW[0:1, 0:512], SW[0:1, 512:1024], SW[0:64, 512:1024], SW[0:64, 1024:1536], SW[0:64, 1536:2048]
        TOK, QT, ATT, ATTT = XT[0:64, 0:512], XT[0:64, 512:1024], SW[0:64, 0:512], SW[0:64, 2048:2560]
        ROUTER = CSTB[:, 12 * D:12 * D + 16]
        B2D = ACC[0:8 * CH, 0:CH * D]
        COMBW = SMALL[:, 960:960 + P]
        COMB = COMBW[:, 0:8 * CH]
        COMBT = SMALL[0:8 * CH, 800:800 + P]
        AD = SMALL[:, 0:16 * NT]
        OH4, OHT = WA, WB
        WHEAD = sb("WHEAD", [1, 512], I32)
        WR, BR = CSTB[:, 12 * D + 16:12 * D + 32], CSTB[:, 12 * D + 32:12 * D + 40]
        CHOSEN = sb("CHOSEN", [1, 2], I32)
        dvec = Chain(sem("dve_line"))

        block = ctx.enter_context(nc.Block())

        @block.sync
        def _(sp):
            sp.dma_start(dst2, a["dst"].rearrange("(p c) -> p c", p=P)).then_inc(sem("ld_dst"), 16)
            sp.wait_ge(sem("x_padded"), 1)
            sp.dma_start(X[:, 0:(NT - 1) * D].rearrange("p (t c) -> p t c", c=D),
                         a["x"][0:(NT - 1) * P, :].rearrange("(t p) c -> p t c", p=P)).then_inc(sem("ld_x"), 16)
            sp.dma_start(X[0:REST, (NT - 1) * D:NT * D], a["x"][(NT - 1) * P:N_NODES, :]).then_inc(sem("ld_x"), 16)
            with nc.allow_non_contiguous_dma(reason="edge index columns"):
                sp.dma_start(IDN[:, 0:NT], a["dst"][0:NT * P].rearrange("(t p) -> p t", p=P)).then_inc(sem("ld_idn"), 16)
                sp.dma_start(IDN[:, NT:2 * NT], a["src"][0:NT * P].rearrange("(t p) -> p t", p=P)).then_inc(sem("ld_idn"), 16)
            wg = WG[:, :].rearrange("p (b c) -> p b c", b=KB)
            sp.dma_start(wg[:, :, 0:D], a["L0_gnn_weight"].rearrange("(b p) c -> p b c", p=P)).then_inc(sem("ld_w0"), 16)
            sp.dma_start(CSTB[:, 0:D], a["L0_gnn_attn_l"].rearrange("h d -> (h d)").partition_broadcast(P)).then_inc(sem("ld_w0"), 16)
            sp.dma_start(CSTB[:, D:2 * D], a["L0_gnn_attn_r"].rearrange("h d -> (h d)").partition_broadcast(P)).then_inc(sem("ld_w0"), 16)

            def store_table(st):
                for c in range(NC):
                    sp.wait_ge(sem("rows"), rows_before(st) + AHEAD + (c + 1) * CH)
                    sp.dma_start(table[c * CW:(c + 1) * CW, :].rearrange("(t p) c -> p t c", p=P),
                                 ACC[:, c * CH * ROW:(c + 1) * CH * ROW].rearrange("p (t c) -> p t c", c=ROW)).then_inc(sem("table_stored"), 16)
                    sp.wait_ge(sem("table_stored"), (GNNS.index(st) * NC + c + 1) * 16)
            store_table("g0")

            sp.dma_start(WA[:, 0:KB * 1024].rearrange("p (b c) -> p b c", b=KB), a["L0_ffn_w1"].rearrange("(b p) c -> p b c", p=P)).then_inc(sem("ld_f0"), 16)
            sp.dma_start(WB[:, 0:8 * D].rearrange("p (b c) -> p b c", b=8), a["L0_ffn_w2"].rearrange("(b p) c -> p b c", p=P)).then_inc(sem("ld_f0"), 16)
            with nc.allow_non_contiguous_dma(reason="bias columns"):
                sp.dma_start(B1[:, 0:8], a["L0_ffn_b1"].rearrange("(b p) -> p b", p=P)).then_inc(sem("ld_f0"), 16)
            sp.dma_start(CSTB[:, 2 * D:3 * D], a["L0_ffn_b2"].partition_broadcast(P)).then_inc(sem("ld_f0"), 16)
            sp.dma_start(CSTB[:, 3 * D:4 * D], a["L0_ffn_wr"].rearrange("a b -> (a b)").partition_broadcast(P)).then_inc(sem("ld_f0"), 16)
            sp.dma_start(SLF[:, 15:16], a["L0_ffn_br"].partition_broadcast(P)).then_inc(sem("ld_f0"), 16)
            sp.wait_ge(sem("f0_scoreT"), 1)
            sp.dma_start(wtab.rearrange("a (t p) -> (a t) p", p=P), TMP[0:NT, 0:P]).then_inc(sem("f0_wtab"), 16)
            sp.wait_ge(sem("f0_wtab"), 16)
            sp.dma_start(RANKROW, wtab.rearrange("a b -> (a b)").partition_broadcast(P)).then_inc(sem("f0_rankrow"), 16)

            for n, name in ((4, "L1_gnn_b"), (5, "L2_gnn_b"), (6, "L3_gnn_bias"), (7, "L3_ffn_gamma"), (8, "L3_ffn_beta")):
                sp.dma_start(CSTB[:, n * D:(n + 1) * D], a[name].partition_broadcast(P)).then_inc(sem("ld_bias"), 16)
            sp.wait_ge(sem("g0_mm"), AHEAD + NT)
            sp.dma_start(wg[:, :, 0:D], a["L1_gnn_W"].rearrange("(b p) c -> p b c", p=P)).then_inc(sem("ld_w1"), 16)
            store_table("g1")

            sp.wait_ge(sem("f0_y"), NT)
            sp.dma_start(WA[:, 1024:2048].rearrange("p (b c) -> p b c", b=KB), a["L1_ffn_W_fx"].rearrange("(b p) c -> p b c", p=P)).then_inc(sem("ld_t1"), 16)
            sp.dma_start(WA[0:64, 2048:4096].rearrange("p (h c) -> p h c", h=8), a["L1_ffn_W_xT"].rearrange("(h p) c -> p h c", p=64)).then_inc(sem("ld_t1"), 16)
            for n, name in enumerate(("W_slice", "W_q", "W_k", "W_v")):
                sp.dma_start(WB[0:64, 64 * n:64 * n + 64], a["L1_ffn_" + name]).then_inc(sem("ld_t1"), 16)
            sp.dma_start(WB[0:64, 256:2304].rearrange("p (h c) -> p h c", h=8), a["L1_ffn_W_out"].rearrange("(h p) c -> p h c", p=64)).then_inc(sem("ld_t1"), 16)
            with nc.allow_non_contiguous_dma(reason="bias columns"):
                sp.dma_start(BX, a["L1_ffn_b_x"].rearrange("(h p) -> p h", p=64)).then_inc(sem("ld_t1"), 16)
                sp.dma_start(BOUT, a["L1_ffn_b_out"].rearrange("(b p) -> p b", p=P)).then_inc(sem("ld_t1"), 16)
            sp.dma_start(BFX, a["L1_ffn_b_fx"].rearrange("(a n) -> a n", a=1)).then_inc(sem("ld_t1"), 16)
            sp.dma_start(TEMPC, a["L1_ffn_temperature"].rearrange("a h b c -> (a h b c)").partition_broadcast(P)).then_inc(sem("ld_t1"), 16)
            sp.dma_start(BSL, a["L1_ffn_b_slice"].partition_broadcast(P)).then_inc(sem("ld_t1"), 16)
            sp.wait_ge(sem("t1_mout"), 1)
            sp.dma_start(MM[64:P, :], MO).then_inc(sem("t1_moved"), 16)

            sp.wait_ge(sem("g1_mm"), AHEAD + NT)
            sp.dma_start(wg[:, :, 0:D], a["L2_gnn_W"].rearrange("(b p) c -> p b c", p=P)).then_inc(sem("ld_w2"), 16)
            store_table("g2")

            sp.wait_ge(sem("t1_out"), AHEAD + NT)
            sp.dma_start(WA[:, :].rearrange("p (e b c) -> p e b c", e=8, b=KB), a["L2_ffn_w1"].rearrange("e (b p) c -> p e b c", p=P)).then_inc(sem("ld_m2"), 16)
            sp.dma_start(WB[:, :].rearrange("p (e b c) -> p e b c", e=8, b=KB), a["L2_ffn_w2"].rearrange("e (b p) c -> p e b c", p=P)).then_inc(sem("ld_m2"), 16)
            with nc.allow_non_contiguous_dma(reason="bias columns"):
                sp.dma_start(B1[:, :].rearrange("p (e b) -> p e b", e=8), a["L2_ffn_b1"].rearrange("e (b p) -> p e b", p=P)).then_inc(sem("ld_m2"), 16)
            sp.dma_start(ROUTER.rearrange("p (b e) -> p b e", b=KB), a["L2_ffn_router_wT"].rearrange("(b p) e -> p b e", p=P)).then_inc(sem("ld_m2"), 16)
            sp.wait_ge(sem("m2_b2zero"), 1)
            for j in range(CH):
                sp.dma_start(B2D[j * 8:(j + 1) * 8, j * D:(j + 1) * D], a["L2_ffn_b2"]).then_inc(sem("ld_m2"), 16)

            sp.wait_ge(sem("g2_mm"), AHEAD + NT)
            sp.dma_start(wg[:, :, 0:D], a["L3_gnn_W"].rearrange("(b p) h d -> p b (h d)", p=P)).then_inc(sem("ld_w3"), 16)
            sp.dma_start(CSTB[:, 0:D], a["L3_gnn_att_src"].rearrange("h d -> (h d)").partition_broadcast(P)).then_inc(sem("ld_w3"), 16)
            sp.dma_start(CSTB[:, D:2 * D], a["L3_gnn_att_dst"].rearrange("h d -> (h d)").partition_broadcast(P)).then_inc(sem("ld_w3"), 16)
            store_table("g3")

            sp.dma_start(WR.rearrange("p (b e) -> p b e", b=KB), a["L3_ffn_Wr"].rearrange("(b p) e -> p b e", p=P)).then_inc(sem("ld_wr"), 16)
            sp.dma_start(BR, a["L3_ffn_br"].partition_broadcast(P)).then_inc(sem("ld_wr"), 16)
            sp.wait_ge(sem("f3_chosen"), 1)
            for k in range(2):
                e = sp.value_load(CHOSEN[0:1, k:k + 1], min_val=0, max_val=7)
                one = lambda name: a[name][ds(e, 1)]
                sp.dma_start(WA[:, :].rearrange("p (b k f) -> p b k f", b=4, k=2)[:, 0:KB, k, :],
                             one("L3_ffn_W1").rearrange("e (b p) f -> p (e b) f", p=P)).then_inc(sem("ld_f3"), 16)
                sp.dma_start(WB[:, k * 1024:(k + 1) * 1024].rearrange("p (b c) -> p b c", b=4),
                             one("L3_ffn_W2").rearrange("e (b p) c -> p (e b) c", p=P)).then_inc(sem("ld_f3"), 16)
                with nc.allow_non_contiguous_dma(reason="bias columns"):
                    sp.dma_start(B1[:, k * 4:(k + 1) * 4], one("L3_ffn_b1").rearrange("e (b p) -> p (e b)", p=P)).then_inc(sem("ld_f3"), 16)
                sp.dma_start(CSTB[:, k * D:(k + 1) * D], one("L3_ffn_b2").rearrange("e c -> (e c)").partition_broadcast(P)).then_inc(sem("ld_f3"), 16)

            sp.wait_ge(sem("finished"), 1)
            sp.dma_start(out[0:(NT - 1) * P, :].rearrange("(t p) c -> p t c", p=P),
                         X[:, 0:(NT - 1) * D].rearrange("p (t c) -> p t c", c=D)).then_inc(sem("stored"), 16)
            sp.dma_start(out[(NT - 1) * P:N_NODES, :], X[0:REST, (NT - 1) * D:NT * D]).then_inc(sem("stored"), 16)
            sp.wait_ge(sem("stored"), 32)

        @block.gpsimd
        def _(g):
            g.iota(IOTA[:, :], pattern=[[1, P]], base=0, channel_multiplier=0, allow_small_or_imprecise_dtypes=True).then_inc(sem("cst"), 1)
            g.iota(IOTAP[:, :], pattern=[[P, 4]], base=0, channel_multiplier=1, allow_small_or_imprecise_dtypes=True).then_inc(sem("cst"), 1)
            g.memset(ONES[:, :], 1.0).then_inc(sem("cst"), 1)
            g.wait_ge(sem("cst"), 3)
            g.affine_select(out=IDENT[:, :], in_=ONES[:, :], compare_op=ALU.is_equal, fill=0.0, base=0,
                            pattern=[[-1, P]], channel_multiplier=1).then_inc(sem("cst"), 1)
            g.affine_select(out=LOWER[:, :], in_=ONES[:, :], compare_op=ALU.is_gt, fill=0.0, base=0,
                            pattern=[[-1, P]], channel_multiplier=1).then_inc(sem("cst"), 1)
            g.affine_select(out=MASK[:, :], in_=ONES[:, 0:NT], compare_op=ALU.is_gt, fill=0.0, base=N_NODES,
                            pattern=[[-P, NT]], channel_multiplier=-1).then_inc(sem("cst"), 1)
            g.wait_ge(sem("slot_tile"), 1)
            for k in range(4):
                g.indirect_dma_start(out=slot_src[:, k * P:(k + 1) * P], out_offset=None, in_=a["src"].rearrange("(t e) -> t e", e=P),
                                     in_offset=bass.IndirectOffsetOnAxis(ap=SLI[:, k:k + 1], axis=0)).then_inc(sem("ld_slots"), 16)
                g.indirect_dma_start(out=slot_dst[:, k * P:(k + 1) * P], out_offset=None, in_=a["dst"].rearrange("(t e) -> t e", e=P),
                                     in_offset=bass.IndirectOffsetOnAxis(ap=SLI[:, k:k + 1], axis=0)).then_inc(sem("ld_slots"), 16)
            g.wait_ge(sem("table_stored"), 16 * NC)
            g.wait_ge(sem("ld_idn"), 32)
            for t in range(NT):
                g.indirect_dma_start(out=BIG[:, t * ROW:(t + 1) * ROW], out_offset=None, in_=table,
                                     in_offset=bass.IndirectOffsetOnAxis(ap=IDN[:, t:t + 1], axis=0)).then_inc(sem("g0_gathered"), 16)
                g.indirect_dma_start(out=ACC[:, t * ROW:(t + 1) * ROW], out_offset=None, in_=table,
                                     in_offset=bass.IndirectOffsetOnAxis(ap=IDN[:, NT + t:NT + t + 1], axis=0)).then_inc(sem("g0_gathered"), 16)

            def gather_slots(tb, st):
                g.wait_ge(sem("table_stored"), (GNNS.index(tb) + 1) * NC * 16)
                g.wait_ge(sem("slots_ready"), 1)
                for q in range(2):
                    g.tensor_copy(IDX[:, q * GRP:(q + 1) * GRP], SRCI[:, q * GRP:(q + 1) * GRP]).then_inc(sem(f"{st}_ix"), 1)
                with g.Fori(0, TURNS) as i:
                    for q in range(NG):
                        n = i * BODY + q * GRP
                        r = (q + 2) % NG
                        g.wait_ge(sem(f"{st}_mm"), BODY + n - GRP)
                        g.wait_ge(sem(f"{st}_ix"), i * NG + q + 1)
                        g.tensor_copy(IDX[:, r * GRP:(r + 1) * GRP], SRCI[:, ds(n + 2 * GRP, GRP)]).then_inc(sem(f"{st}_ix"), 1)
                        for k in range(q * GRP, (q + 1) * GRP):
                            g.indirect_dma_start(out=G[:, k * ROW:(k + 1) * ROW], out_offset=None, in_=table,
                                                 in_offset=bass.IndirectOffsetOnAxis(ap=IDX[:, k:k + 1], axis=0)).then_inc(sem(f"{st}_in{q}"), 16)
                g.wait_ge(sem(f"{st}_ix"), TURNS * NG + 2)

            gather_slots("g1", "a1")
            gather_slots("g2", "a2")
            gather_slots("g3", "a3")
            for k in range(GRP):
                g.indirect_dma_start(out=G[:, k * ROW:(k + 1) * ROW], out_offset=None, in_=table,
                                     in_offset=bass.IndirectOffsetOnAxis(ap=IDX[:, k:k + 1], axis=0)).then_inc(sem("a3_in0"), 16)

        @block.tensor
        def _(pe):
            pe.sem_inc(sem("tp"), AHEAD)
            pe.wait_ge(sem("cst"), 6)
            hist = PB[7][:, 0:NT]
            pe.wait_ge(sem("iotab"), 1)
            pe.sem_inc(sem("h_used"), 2)
            pe.matmul(hist, IOTAB[:, :], ZEROB[:, :], start=True, stop=False, skip_group_check=True)
            with pe.Fori(0, ET // (2 * HB)) as i:
                for r in range(2):
                    pe.wait_ge(sem("h_onehot"), i * 2 + r + 1)
                    for k in range(HB):
                        mm = pe.matmul(hist, ob[:, (r * HB + k) * P:(r * HB + k + 1) * P], oa[:, (r * HB + k) * NT:(r * HB + k + 1) * NT],
                                       start=False, stop=False, skip_group_check=True)
                    mm.then_inc(sem("h_used"), 1)
            pe.matmul(hist, IOTAB[:, :], ZEROB[:, :], start=False, stop=True, skip_group_check=True).then_inc(sem("hist"), 1)
            pe.wait_ge(sem("hist_sb"), 1)
            pe.matmul(PB[6][:, 0:NT], ONES[:, :], T1[:, :], start=True, stop=True).then_inc(sem("totals"), 1)
            pe.wait_ge(sem("slot_rows"), 1)
            for k in range(4):
                pe.transpose(PB[4][:, k * P:(k + 1) * P], slot_srcf[:, k * P:(k + 1) * P], IDENT[:, :])
                pe.transpose(PB[5][:, k * P:(k + 1) * P], slot_dstf[:, k * P:(k + 1) * P], IDENT[:, :])
                mm = pe.matmul(PB[6][0:1, k * P:(k + 1) * P], SLF[:, 4 + k:5 + k], IDENT[:, :], start=True, stop=True)
            mm.then_inc(sem("slotsT"), 1)

            def turn(st, c, j):
                n = c * CH + j
                pe.wait_ge(sem("xs"), tiles_before(st) + n + 1)
                pe.wait_ge(sem("xt"), tiles_before(st) + AHEAD + n + 1 - (1 if j == 0 else 2))
                for b in range(KB):
                    mm = pe.transpose(PB[j % 2][:, b * P:(b + 1) * P], XS[:, j * D + b * P:j * D + (b + 1) * P], IDENT[:, :])
                mm.then_inc(sem("tp"), 1)

            def project(st, width):
                pe.sem_inc(sem(f"{st}_mm"), AHEAD)
                with pe.Fori(0, NC) as c:
                    for j in range(CH):
                        turn(st, c, j)
                    for j in range(CH):
                        n = c * CH + j
                        pe.wait_ge(sem("xt"), tiles_before(st) + AHEAD + n + 1)
                        pe.wait_ge(sem("rows"), rows_before(st) + AHEAD + n + 1 - CH)
                        for b in range(KB):
                            mm = pe.matmul(PB[2 + j][:, 0:width], XT[:, b * CW + j * P:b * CW + (j + 1) * P],
                                           WG[:, b * GW:b * GW + width], start=(b == 0), stop=(b == KB - 1))
                        mm.then_inc(sem(f"{st}_mm"), 1)

            pe.wait_ge(sem("g0_weights"), 1)
            project("g0", ROW)

            def ffn(st, w1, w2):
                pe.sem_inc(sem(f"{st}_hid"), AHEAD)
                with pe.Fori(0, NC) as c:
                    for j in range(CH):
                        turn(st, c, j)
                    pe.wait_ge(sem("xt"), tiles_before(st) + AHEAD + c * CH + CH)
                    for h in range(8):
                        n = c * 8 + h
                        pe.wait_ge(sem(f"{st}_act"), AHEAD + n + 1 - 2)
                        for s in range(2):
                            for b in range(KB):
                                mm = pe.matmul(PB[2 + 2 * (h % 2) + s][:, 0:HALF], w1[:, b * 1024 + h * P:b * 1024 + (h + 1) * P],
                                               XT[:, b * CW + s * HALF:b * CW + (s + 1) * HALF], start=(b == 0), stop=(b == KB - 1))
                        mm.then_inc(sem(f"{st}_hid"), 1)
                    pe.wait_ge(sem(f"{st}_act"), AHEAD + c * 8 + 8)
                    for j in range(CH):
                        n = c * CH + j
                        pe.wait_ge(sem(f"{st}_out"), AHEAD + n + 1 - (1 if j == 0 else 2))
                        for h in range(8):
                            mm = pe.matmul(PB[6 + j % 2][:, 0:D], HT[:, h * CW + j * P:h * CW + (j + 1) * P], w2[:, h * D:(h + 1) * D],
                                           start=(h == 0), stop=(h == 7))
                        mm.then_inc(sem(f"{st}_y"), 1)

            pe.wait_ge(sem("f0_score"), 1)
            pe.transpose(PB[2][0:NT, 0:P], COEF[:, :], IDENT[:, :]).then_inc(sem("f0_scoreP"), 1)
            pe.wait_ge(sem("ld_f0"), 16 * 6)
            pe.wait_ge(sem("f0_scoreT"), 1)
            ffn("f0", WA, WB)

            def sum_slots(st, width):
                pe.sem_inc(sem(f"{st}_mm"), BODY)
                with pe.Fori(0, TURNS) as i:
                    for q in range(NG):
                        pe.wait_ge(sem(f"{st}_in{q}"), 16 * GRP * (i + 1))
                        pe.wait_ge(sem(f"{st}_oh"), i * NG + q + 1)
                        for k in range(GRP):
                            n = i * BODY + q * GRP + k
                            pe.wait_ge(sem(f"{st}_acc"), BODY + n + 1 - GRP)
                            pe.matmul(PB[k][:, 0:width], OH[:, ((q % 2) * GRP + k) * P:((q % 2) * GRP + k + 1) * P],
                                      G[:, (q * GRP + k) * ROW:(q * GRP + k) * ROW + width], start=True, stop=True).then_inc(sem(f"{st}_mm"), 1)

            pe.wait_ge(sem("ld_w1"), 16)
            project("g1", D)
            sum_slots("a1", D)

            def slices(st):
                pe.wait_ge(sem("ld_t1"), 16 * 12)
                pe.wait_ge(sem("a1_acc"), BODY + SLOTS)
                for b in range(KB):
                    for h in range(8):
                        pe.matmul(PB[b][:, h * 64:h * 64 + 64], WXT[:, h * D + b * P:h * D + (b + 1) * P], WSL, start=True, stop=True)
                pe.wait_ge(sem(f"{st}_bxr"), 1)
                for h in range(8):
                    mm = pe.matmul(PB[2][:, h * 64:h * 64 + 64], BXR[:, h * P:(h + 1) * P], WSL, start=True, stop=True)
                mm.then_inc(sem(f"{st}_wxs"), 1)
                pe.sem_inc(sem(f"{st}_lg"), AHEAD)
                pe.sem_inc(sem(f"{st}_tok"), AHEAD)
                pe.wait_ge(sem(f"{st}_fold"), 1)
                for k in (4, 5):
                    pe.matmul(PB[k][:, :], ONES[:, :], TMP[:, 0:512], start=True, stop=False, skip_group_check=True)
                pe.matmul(PB[6][0:1, :], ONES[:, 0:1], TMP[:, 0:512], start=True, stop=False, skip_group_check=True)
                with pe.Fori(0, NC) as c:
                    for j in range(CH):
                        turn(st, c, j)
                    for j in range(CH):
                        n = c * CH + j
                        pe.wait_ge(sem("xt"), tiles_before(st) + AHEAD + n + 1)
                        pe.wait_ge(sem(f"{st}_lgc"), AHEAD + n + 1 - (1 if j == 0 else 2))
                        for b in range(KB):
                            mm = pe.matmul(PB[2 + j % 2][:, :], XT[:, b * CW + j * P:b * CW + (j + 1) * P], WXS[:, b * 512:(b + 1) * 512],
                                           start=(b == 0), stop=(b == KB - 1))
                        mm.then_inc(sem(f"{st}_lg"), 1)
                    for j in range(CH):
                        n = c * CH + j
                        w = SW[:, j * 512:(j + 1) * 512]
                        pe.wait_ge(sem(f"{st}_sw"), n + 1)
                        for b in range(KB):
                            pe.matmul(PB[4 + b][:, :], XS[:, j * D + b * P:j * D + (b + 1) * P], w, start=False, stop=False, skip_group_check=True)
                        pe.matmul(PB[6][0:1, :], ONES[:, 0:1], w, start=False, stop=False, skip_group_check=True)
                        pe.wait_ge(sem(f"{st}_swt"), AHEAD + n + 1 - 1)
                        for b in range(4):
                            mm = pe.transpose(PB[7][:, b * P:(b + 1) * P], w[:, b * P:(b + 1) * P], IDENT[:, :])
                        mm.then_inc(sem(f"{st}_tok"), 1)
                for k in (4, 5):
                    pe.matmul(PB[k][:, :], ONES[:, :], TMP[:, 0:512], start=False, stop=True, skip_group_check=True)
                pe.matmul(PB[6][0:1, :], ONES[:, 0:1], TMP[:, 0:512], start=False, stop=True, skip_group_check=True).then_inc(sem(f"{st}_sums"), 1)
                pe.wait_ge(sem(f"{st}_norm"), 1)
                for h in range(8):
                    o = slice(h * 64, h * 64 + 64)
                    for b in range(KB):
                        pe.matmul(PB[0][0:64, o], WFX[:, b * 512 + h * 64:b * 512 + h * 64 + 64], TOKT[:, b * 512 + h * 64:b * 512 + h * 64 + 64], start=(b == 0), stop=False)
                    pe.matmul(PB[0][0:64, o], BFX[:, o], NORM[:, o], start=False, stop=True)
                pe.matmul(PB[1][0:64, :], ONES[0:1, 0:64], RN, start=True, stop=True).then_inc(sem(f"{st}_tokens"), 1)
                pe.wait_ge(sem(f"{st}_token"), 1)
                for k, w in ((2, WQ), (3, WK), (4, WV)):
                    mm = pe.matmul(PB[k][0:64, :], w, TOK, start=True, stop=True)
                mm.then_inc(sem(f"{st}_qkv"), 1)
                pe.wait_ge(sem(f"{st}_qkvc"), 1)
                for h in range(8):
                    o = slice(h * 64, h * 64 + 64)
                    mm = pe.matmul(PB[5][0:64, o], QT[:, o], KT[:, o], start=True, stop=True)
                mm.then_inc(sem(f"{st}_att"), 1)
                for h in range(8):
                    mm = pe.matmul(PB[h // 2][0:64, (h % 2) * D:(h % 2 + 1) * D], VT[:, h * 64:h * 64 + 64], WOUT[:, h * D:(h + 1) * D], start=True, stop=True)
                mm.then_inc(sem(f"{st}_vw"), 1)
                pe.wait_ge(sem(f"{st}_soft"), 1)
                for h in range(8):
                    o = slice(h * 64, h * 64 + 64)
                    mm = pe.transpose(PB[6][0:64, o], ATT[:, o], IDENT[0:64, 0:64])
                mm.then_inc(sem(f"{st}_attT"), 1)
                pe.wait_ge(sem(f"{st}_attc"), 1)
                for h in range(8):
                    mm = pe.matmul(PB[h // 2][0:64, (h % 2) * D:(h % 2 + 1) * D], ATTT[:, h * 64:h * 64 + 64], VW[:, h * D:(h + 1) * D], start=True, stop=True)
                mm.then_inc(sem(f"{st}_m"), 1)
                pe.wait_ge(sem(f"{st}_moved"), 16)
                pe.wait_ge(sem(f"{st}_mout"), 1)
                pe.sem_inc(sem(f"{st}_o"), AHEAD)
                pe.sem_inc(sem(f"{st}_y"), AHEAD)
                with pe.Fori(0, NC) as c:
                    for i in range(4):
                        n = c * 4 + i
                        f, half = i // 2, i % 2
                        pe.wait_ge(sem(f"{st}_ob"), AHEAD + n + 1 - 4)
                        for b in range(4):
                            mm = pe.matmul(PB[i][:, 0:HALF], MM[:, b * D + f * P:b * D + (f + 1) * P], SWT[:, ds(c * CW + b * NT * P + half * HALF, HALF)],
                                           start=(b == 0), stop=(b == 3))
                        mm.then_inc(sem(f"{st}_o"), 1)
                    pe.wait_ge(sem(f"{st}_ob"), AHEAD + c * 4 + 4)
                    for j in range(CH):
                        n = c * CH + j
                        pe.wait_ge(sem(f"{st}_out"), AHEAD + n + 1 - (1 if j == 0 else 2))
                        for f in range(KB):
                            mm = pe.transpose(PB[4 + j % 2][:, f * P:(f + 1) * P], XT[:, f * CW + j * P:f * CW + (j + 1) * P], IDENT[:, :])
                        mm.then_inc(sem(f"{st}_y"), 1)

            slices("t1")
            pe.wait_ge(sem("ld_w2"), 16)
            project("g2", D)
            sum_slots("a2", D)

            def experts(st):
                pe.sem_inc(sem(f"{st}_hid"), AHEAD)
                with pe.Fori(0, NC) as c:
                    pe.wait_ge(sem(f"{st}_b2"), AHEAD + c)
                    for j in range(CH):
                        turn(st, c, j)
                    pe.wait_ge(sem("xt"), tiles_before(st) + AHEAD + c * CH + CH)
                    for j in range(CH):
                        for b in range(KB):
                            mm = pe.matmul(PB[1][:, j * 8:j * 8 + 8], XT[:, b * CW + j * P:b * CW + (j + 1) * P], ROUTER[:, b * 8:b * 8 + 8],
                                           start=(b == 0), stop=(b == KB - 1))
                    mm.then_inc(sem(f"{st}_logits"), 1)

                    def hidden(e):
                        for h in range(KB):
                            pe.wait_ge(sem(f"{st}_act"), AHEAD + (c * 8 + e) * 2 + h + 1 - 2)
                            for s in range(2):
                                for b in range(KB):
                                    mm = pe.matmul(PB[2 + 2 * h + s][:, 0:HALF], WA[:, (e * KB + b) * D + h * P:(e * KB + b) * D + (h + 1) * P],
                                                   XT[:, b * CW + s * HALF:b * CW + (s + 1) * HALF], start=(b == 0), stop=(b == KB - 1))
                            mm.then_inc(sem(f"{st}_hid"), 1)

                    def outputs(e):
                        pe.wait_ge(sem(f"{st}_act"), AHEAD + (c * 8 + e) * 2 + 2)
                        for j in range(CH):
                            pe.wait_ge(sem(f"{st}_out"), AHEAD + (c * 8 + e) * CH + j + 1 - 2)
                            for h in range(KB):
                                mm = pe.matmul(PB[6 + (e * CH + j) % 2][:, 0:D], HT[:, ((e % 2) * KB + h) * CW + j * P:((e % 2) * KB + h) * CW + (j + 1) * P],
                                               WB[:, (e * KB + h) * D:(e * KB + h + 1) * D], start=(h == 0), stop=(h == KB - 1))
                            mm.then_inc(sem(f"{st}_y"), 1)
                    hidden(0)
                    for e in range(1, 8):
                        hidden(e)
                        outputs(e - 1)
                    outputs(7)
                    pe.wait_ge(sem(f"{st}_comb"), c + 1)
                    pe.transpose(PB[0][:, 0:P], COMBW, IDENT[:, :]).then_inc(sem(f"{st}_combT"), 1)
                    pe.wait_ge(sem(f"{st}_combTc"), c + 1)
                    for k in range(3):
                        w = min(512, CH * D - k * 512)
                        mm = pe.matmul(PB[k][:, 0:w], COMBT, B2D[:, k * 512:k * 512 + w], start=True, stop=True)
                    mm.then_inc(sem(f"{st}_b2y"), 1)

            pe.wait_ge(sem("ld_m2"), 16 * 9)
            experts("m2")

            def sum_attended(st):
                regs = [pe.alloc_register(f"{st}_win{k}") for k in range(GRP)]

                def turned(g, r, first):
                    pe.wait_ge(sem(f"{st}_oh"), g + 1)
                    for s in range(2):
                        if not first:
                            pe.wait_ge(sem(f"{st}_tpc"), 2 * g + s - 1)
                        for k in range(4):
                            o = (r * GRP + s * 4 + k) * P
                            mm = pe.transpose(PB[4 + s][:, k * P:(k + 1) * P], OH4[:, o:o + P], IDENT[:, :])
                        mm.then_inc(sem(f"{st}_turned"), 1)

                def terms(g, r, n0):
                    pe.wait_ge(sem(f"{st}_tpc"), 2 * g + 2)
                    pe.wait_ge(sem(f"{st}_z"), g)
                    pe.load(regs, WHEAD[0:1, ds(n0, GRP)] if not isinstance(n0, int) else WHEAD[0:1, n0:n0 + GRP])
                    for k in range(GRP):
                        w = pe.snap(regs[k], min_val=0, max_val=(NT - 1) * 8)
                        mm = pe.matmul(PB[6 + r % 2][:, k * 16:k * 16 + 16].rearrange("p (a h) -> p a h", a=2), OHT[:, ((r % 2) * GRP + k) * P:((r % 2) * GRP + k + 1) * P],
                                       AD.rearrange("p (a n) -> p a n", a=2)[:, :, ds(w, 8)], start=True, stop=True)
                    mm.then_inc(sem(f"{st}_ad"), 1)

                pe.sem_inc(sem(f"{st}_mm"), BODY)
                turned(0, 0, True)
                pe.wait_ge(sem("g3_ad"), 1)
                turned(1, 1, False)
                terms(0, 0, 0)
                with pe.Fori(0, TURNS) as i:
                    for q in range(NG):
                        g = i * NG + q
                        turned(g + 2, (q + 2) % NG, False)
                        terms(g + 1, q + 1, (g + 1) * GRP)
                        pe.wait_ge(sem(f"{st}_scaled"), g + 1)
                        for k in range(GRP):
                            n = i * BODY + q * GRP + k
                            pe.wait_ge(sem(f"{st}_acc"), BODY + n + 1 - 4)
                            pe.matmul(PB[k % 4][:, 0:ROW], OH4[:, (q * GRP + k) * P:(q * GRP + k + 1) * P],
                                      G[:, (q * GRP + k) * ROW:(q * GRP + k + 1) * ROW], start=True, stop=True).then_inc(sem(f"{st}_mm"), 1)

            pe.wait_ge(sem("g3_weights"), 1)
            project("g3", 272)
            pe.wait_ge(sem("g3_umax"), 1)
            pe.transpose(PB[0][0:8, 0:P], SMALL[:, 800:808], IDENT[:, :]).then_inc(sem("g3_uT"), 1)
            pe.wait_ge(sem("g3_udiag"), 1)
            pe.matmul(PB[0][:, 0:8], ONES[0:8, :], SMALL[0:8, 816:824], start=True, stop=True).then_inc(sem("g3_u"), 1)
            sum_attended("a3")

            pe.wait_ge(sem("f3_stats"), 1)
            for b in range(KB):
                for t in range(NT):
                    pe.matmul(PB[b][:, 0:1], X[:, t * D + b * P:t * D + (b + 1) * P], RSTD[:, t:t + 1], start=(t == 0), stop=False)
                mm = pe.matmul(PB[b][:, 0:1], ONES[:, :], SMALL[:, 0:1], start=False, stop=True)
            mm.then_inc(sem("f3_mean"), 1)
            pe.wait_ge(sem("f3_meanb"), 1)
            pe.wait_ge(sem("ld_wr"), 32)
            for b in range(KB):
                mm = pe.matmul(PB[2][:, 0:8], OH[:, b * P:(b + 1) * P], WR[:, b * 8:b * 8 + 8], start=(b == 0), stop=(b == KB - 1))
            mm.then_inc(sem("f3_logits"), 1)
            pe.wait_ge(sem("f3_weights"), 1)
            ffn("f3", WA, WB)

        @block.scalar
        def _(act):
            act.sem_inc(sem("xt"), AHEAD)
            act.wait_ge(sem("deg"), 1)
            act.activation(DINV[:, :], VAR[:, :], ACT.Sqrt).then_inc(sem("dinv"), 1)

            def ln_root(st):
                act.wait_ge(sem("var"), ORDER.index(st) + 1)
                act.activation(T1[:, :], VAR[:, :], ACT.Sqrt).then_inc(sem("std"), 1)

            def to_xt(st, c, j):
                act.wait_ge(sem("tp"), tiles_before(st) + AHEAD + c * CH + j + 1)
                act.activation(XT[:, :].rearrange("p (b n) -> p b n", b=KB)[:, :, j * P:(j + 1) * P],
                               PB[j % 2][:, 0:D].rearrange("p (b n) -> p b n", b=KB), ACT.Copy).then_inc(sem("xt"), 1)

            def project(st):
                with act.Fori(0, NC) as c:
                    for j in range(CH):
                        act.wait_ge(sem(f"{st}_mm"), AHEAD + c * CH + j + 1 - CH)
                        to_xt(st, c, j)

            def ffn(st, func):
                act.sem_inc(sem(f"{st}_act"), AHEAD)
                with act.Fori(0, NC) as c:
                    act.wait_ge(sem(f"{st}_hid"), AHEAD + c * 8)
                    for j in range(CH):
                        to_xt(st, c, j)
                    for h in range(8):
                        act.wait_ge(sem(f"{st}_hid"), AHEAD + c * 8 + h + 1)
                        k = 2 + 2 * (h % 2)
                        for s in range(2):
                            ins = act.activation(HT[:, h * CW + s * HALF:h * CW + (s + 1) * HALF], PB[k + s][:, 0:HALF], func, bias=B1[:, h:h + 1])
                        ins.then_inc(sem(f"{st}_act"), 1)

            ln_root("g0")
            project("g0")
            act.wait_ge(sem("g0_logit"), 1)
            act.activation(ADS[:, 0:4 * NT], ADS[:, 0:4 * NT], ACT.Exp).then_inc(sem("g0_exp"), 1)
            ln_root("f0")
            act.wait_ge(sem("f0_scoreP"), 1)
            act.activation(TMP[0:NT, 0:P], PB[2][0:NT, 0:P], ACT.Copy).then_inc(sem("f0_scoreT"), 1)
            ffn("f0", ACT.Gelu_apprx_tanh)
            ln_root("g1")
            project("g1")
            def slices(st):
                act.sem_inc(sem(f"{st}_swt"), AHEAD)
                with act.Fori(0, NC) as c:
                    for j in range(CH):
                        act.wait_ge(sem(f"{st}_lg"), AHEAD + c * CH + j + 1 - CH)
                        to_xt(st, c, j)
                    for j in range(CH):
                        n = c * CH + j
                        w = SW[:, j * 512:(j + 1) * 512]
                        act.wait_ge(sem(f"{st}_sub"), n + 1)
                        act.activation(w, w, ACT.Exp).then_inc(sem(f"{st}_exp"), 1)
                        if j:
                            to_swt(st, n - 1)
                    to_swt(st, c * CH + CH - 1)
                act.wait_ge(sem(f"{st}_sub2"), 1)
                act.activation(ATT, ATT, ACT.Exp, scale=0.125).then_inc(sem(f"{st}_exp2"), 1)
                act.sem_inc(sem(f"{st}_ob"), AHEAD)
                with act.Fori(0, NC) as c:
                    act.wait_ge(sem(f"{st}_y"), AHEAD + c * CH)
                    for i in range(4):
                        f, half = i // 2, i % 2
                        act.wait_ge(sem(f"{st}_o"), AHEAD + c * 4 + i + 1)
                        act.activation(XT[:, f * CW + half * HALF:f * CW + (half + 1) * HALF], PB[i][:, 0:HALF], ACT.Identity,
                                       bias=BOUT[:, f:f + 1]).then_inc(sem(f"{st}_ob"), 1)

            def to_swt(st, n):
                act.wait_ge(sem(f"{st}_tok"), AHEAD + n + 1)
                act.activation(SWT.rearrange("p (b n) -> p b n", b=4)[:, :, ds(n * P, P)], PB[7][:, :].rearrange("p (b n) -> p b n", b=4),
                               ACT.Copy).then_inc(sem(f"{st}_swt"), 1)

            ln_root("t1")
            slices("t1")
            ln_root("g2")
            project("g2")

            st = "m2"
            ln_root(st)
            act.sem_inc(sem(f"{st}_act"), AHEAD)
            with act.Fori(0, NC) as c:
                act.wait_ge(sem(f"{st}_hid"), AHEAD + c * 16)
                for j in range(CH):
                    to_xt(st, c, j)
                act.wait_ge(sem(f"{st}_sub"), c + 1)
                act.activation(COMB, COMB, ACT.Exp).then_inc(sem(f"{st}_exp"), 1)
                for h in range(16):
                    act.wait_ge(sem(f"{st}_hid"), AHEAD + c * 16 + h + 1)
                    for s in range(2):
                        ins = act.activation(HT[:, (h % 4) * CW + s * HALF:(h % 4) * CW + (s + 1) * HALF], PB[2 + 2 * (h % 2) + s][:, 0:HALF],
                                             ACT.Gelu, bias=B1[:, h:h + 1])
                    ins.then_inc(sem(f"{st}_act"), 1)

            ln_root("g3")
            project("g3")
            st = "a3"
            act.sem_inc(sem(f"{st}_z"), 1)

            def copy_turned(g, r):
                for s in range(2):
                    act.wait_ge(sem(f"{st}_turned"), 2 * g + s + 1)
                    act.activation(OHT[:, (r * 2 + s) * 512:(r * 2 + s + 1) * 512], PB[4 + s][:, :], ACT.Copy).then_inc(sem(f"{st}_tpc"), 1)

            def exps(g, r):
                act.wait_ge(sem(f"{st}_z"), g + 2)
                act.activation(G[:, r * GRP * ROW:(r + 1) * GRP * ROW].rearrange("p (k c) -> p k c", c=ROW)[:, :, D:D + 8],
                               TMP[:, (r % 2) * 64:(r % 2 + 1) * 64].rearrange("p (k h) -> p k h", k=GRP), ACT.Exp).then_inc(sem(f"{st}_exp"), 1)
            copy_turned(0, 0)
            copy_turned(1, 1)
            exps(0, 0)
            with act.Fori(0, TURNS) as i:
                for q in range(NG):
                    g = i * NG + q
                    copy_turned(g + 2, q % 2)
                    exps(g + 1, (q + 1) % NG)

            ln_root("f3")
            act.wait_ge(sem("f3_sub"), 1)
            act.activation(SMALL[:, 16:24], SMALL[:, 16:24], ACT.Exp).then_inc(sem("f3_exp"), 1)
            act.wait_ge(sem("f3_sub"), 2)
            act.activation(SMALL[:, 16:24], SMALL[:, 16:24], ACT.Exp).then_inc(sem("f3_exp"), 1)
            act.wait_ge(sem("f3_sub"), 3)
            act.activation(SMALL[:, 48:49], SMALL[:, 48:49], ACT.Exp).then_inc(sem("f3_exp"), 1)
            ffn("f3", ACT.Gelu)
            act.wait_ge(sem("var"), ORDER.index("n3") + 1)
            act.activation(T1[:, :], VAR[:, :], ACT.Sqrt).then_inc(sem("std"), 1)

        @block.vector
        def _(v):
            line = dvec
            v.sem_inc(sem("rows"), AHEAD)
            v.memset(X[:, (NT - 1) * D:NT * D], 0.0).then_inc(sem("x_padded"), 1)
            line.mark(v.memset(ZEROB[:, :], 0.0))
            v.wait_ge(sem("cst"), 6)
            line.sync(v)
            v.tensor_copy(IOTAB[:, :], IOTA[:, :]).then_inc(sem("iotab"), 1)
            v.wait_ge(sem("ld_dst"), 16)
            line.mark(v.tensor_scalar(dlo, dst2, P - 1, None, ALU.bitwise_and))
            line.step(v, v.tensor_scalar(dhi, dst2, 7, None, ALU.arith_shift_right))
            line.mark(v.tensor_copy(dlob, dlo))
            line.step(v, v.tensor_copy(dhib, dhi))
            v.wait_ge(sem("iotab"), 1)
            with v.Fori(0, ET // (2 * HB)) as i:
                for r in range(2):
                    v.wait_ge(sem("h_used"), i * 2 + r + 1)
                    v.tensor_tensor(ob[:, r * HB * P:(r + 1) * HB * P].rearrange("p (k n) -> p k n", k=HB),
                                    IOTAB[:, :].unsqueeze(1).to_broadcast([P, HB, P]),
                                    dlob[:, ds(i * 2 * HB + r * HB, HB)].unsqueeze(2).to_broadcast([P, HB, P]), ALU.is_equal)
                    v.tensor_tensor(oa[:, r * HB * NT:(r + 1) * HB * NT].rearrange("p (k n) -> p k n", k=HB),
                                    IOTAB[:, 0:NT].unsqueeze(1).to_broadcast([P, HB, NT]),
                                    dhib[:, ds(i * 2 * HB + r * HB, HB)].unsqueeze(2).to_broadcast([P, HB, NT]),
                                    ALU.is_equal).then_inc(sem("h_onehot"), 1)
            v.wait_ge(sem("hist"), 1)
            v.tensor_copy(T1[:, :], PB[7][:, 0:NT]).then_inc(sem("hist_sb"), 1)
            v.wait_ge(sem("hist_sb"), 1)
            line.step(v, v.tensor_scalar(T2[:, :], T1[:, :], 1.0, None, ALU.add))
            v.reciprocal(VAR[:, :], T2[:, :]).then_inc(sem("deg"), 1)
            v.wait_ge(sem("totals"), 1)
            line.step(v, v.tensor_copy(SMALL[:, 0:NT], PB[6][:, 0:NT]))
            line.step(v, v.tensor_tensor_scan(SMALL[:, 32:32 + NT], SMALL[:, 0:NT], SMALL[:, 0:NT], 0.0, ALU.add, ALU.bypass))
            line.step(v, v.tensor_copy(SMALL[:, 64:64 + NT].bitcast(I32), SMALL[:, 32:32 + NT]))
            line.step(v, v.tensor_scalar(SMALL[:, 96:96 + NT].bitcast(I32), SMALL[:, 64:64 + NT].bitcast(I32), 7, None, ALU.arith_shift_right))
            line.step(v, v.tensor_copy(SMALL[:, 128:128 + NT], SMALL[:, 96:96 + NT].bitcast(I32)))
            line.step(v, v.scalar_tensor_tensor(SMALL[:, 160:160 + NT - 1], IOTA[:, 0:NT - 1], 1.0, SMALL[:, 128:128 + NT - 1], ALU.add, ALU.add))
            rank = SMALL[:, 160:160 + NT - 1].unsqueeze(1).to_broadcast([P, 4, NT - 1])
            le = SMALL[:, 200:200 + 4 * (NT - 1)].rearrange("p (k w) -> p k w", k=4)
            line.step(v, v.tensor_tensor(le, rank, IOTAP[:, :].unsqueeze(2).to_broadcast([P, 4, NT - 1]), ALU.is_le))
            line.step(v, v.tensor_reduce(SLF[:, 0:4], le, AX.X, ALU.add))
            line.step(v, v.tensor_tensor(SLF[:, 8:12], IOTAP[:, :], SLF[:, 0:4], ALU.subtract))
            line.step(v, v.tensor_scalar(SLF[:, 8:12], SLF[:, 8:12], float(ET - 1), None, ALU.min))
            v.tensor_copy(SLI[:, :], SLF[:, 8:12]).then_inc(sem("slot_tile"), 1)
            line.mark(v.tensor_scalar(SLF[:, 4:8], SLF[:, 0:4], float(ROW), None, ALU.mult))
            line.step(v, v.tensor_scalar(SLF[:, 0:4], SLF[:, 0:4], float(P), None, ALU.mult))
            v.wait_ge(sem("ld_slots"), 8 * 16)
            line.mark(v.tensor_copy(slot_srcf, slot_src))
            line.step(v, v.tensor_copy(slot_dstf, slot_dst))
            for k in range(4):
                ins = v.tensor_scalar(slot_dstf[:, k * P:(k + 1) * P], slot_dstf[:, k * P:(k + 1) * P], SLF[:, k:k + 1], None, ALU.subtract)
            ins.then_inc(sem("slot_rows"), 1)
            v.wait_ge(sem("slotsT"), 1)
            v.tensor_copy(SRCI[:, 0:SLOTS], PB[4][:, 0:SLOTS])
            v.tensor_copy(DREL[:, 0:SLOTS], PB[5][:, 0:SLOTS])
            v.memset(SRCI[:, SLOTS:], 0)
            v.memset(DREL[:, SLOTS:], -1.0)
            v.tensor_copy(WROW[:, :], PB[6][0:1, 0:512]).then_inc(sem("slots_ready"), 1)
            v.wait_ge(sem("slots_ready"), 1)

            def ln_stats(st):
                with v.Fori(0, NT) as t:
                    v.bn_stats(tile(ST6, t, 6, 6), tile(X, t)).then_inc(sem("bn"), 1)
                moments(st)

            def moments(st):
                v.wait_ge(sem("bn"), tiles_before(st) + NT)
                s6 = ST6[:, :].rearrange("p (t k) -> p k t", k=6)
                line.mark(v.tensor_tensor(T1[:, :], s6[:, 1, :], s6[:, 4, :], ALU.subtract))
                line.mark(v.tensor_tensor(MEAN[:, :], s6[:, 1, :], s6[:, 4, :], ALU.add))
                line.step(v, v.tensor_tensor(T2[:, :], s6[:, 2, :], s6[:, 5, :], ALU.add))
                line.step(v, v.tensor_tensor(T1[:, :], T1[:, :], T1[:, :], ALU.mult))
                line.mark(v.tensor_scalar(MEAN[:, :], MEAN[:, :], 0.5, None, ALU.mult))
                line.mark(v.tensor_scalar(T1[:, :], T1[:, :], 0.25, LN_EPS, ALU.mult, ALU.add))
                line.sync(v)
                v.scalar_tensor_tensor(VAR[:, :], T2[:, :], 1.0 / D, T1[:, :], ALU.mult, ALU.add).then_inc(sem("var"), 1)
                v.wait_ge(sem("std"), ORDER.index(st) + 1)
                line.step(v, v.reciprocal(RSTD[:, :], T1[:, :]))
                line.step(v, v.tensor_tensor(RSTD[:, :], RSTD[:, :], MASK[:, :], ALU.mult))
                line.step(v, v.scalar_tensor_tensor(NMR[:, :], MEAN[:, :], -1.0, RSTD[:, :], ALU.mult, ALU.mult))
                line.step(v, v.tensor_scalar(ONEP[:, :], RSTD[:, :], 1.0, None, ALU.add))

            def ln_apply(st, c, j, keep):
                t = c * CH + j
                v.wait_ge(sem("tp"), tiles_before(st) + AHEAD + t + 1 - CH)
                v.tensor_scalar(XS[:, j * D:(j + 1) * D], tile(X, t), MEAN[:, ds(t, 1)], RSTD[:, ds(t, 1)],
                                ALU.subtract, ALU.mult).then_inc(sem("xs"), 1)
                if keep:
                    line.mark(v.tensor_scalar(tile(X, t), tile(X, t), ONEP[:, ds(t, 1)], NMR[:, ds(t, 1)], ALU.mult, ALU.add))

            def attention_columns(dst, left, right, w, done):
                for b in range(KB):
                    for k, vec in ((0, left), (1, right)):
                        line.step(v, v.tensor_tensor(TMP[:, 0:D], WG[:, b * GW:b * GW + D], vec, ALU.mult))
                        line.step(v, v.tensor_reduce(dst(b, k), TMP[:, 0:D].rearrange("p (h d) -> p h d", h=w), AX.X, ALU.add))
                v.sem_inc(sem(done), 1)

            v.wait_ge(sem("ld_x"), 32)
            v.wait_ge(sem("dinv"), 1)
            v.wait_ge(sem("x_padded"), 1)
            ln_stats("g0")
            v.wait_ge(sem("ld_w0"), 16 * 3)
            attention_columns(lambda b, k: WG[:, b * GW + D + 4 * k:b * GW + D + 4 * k + 4], CSTB[:, 0:D], CSTB[:, D:2 * D], 4, "g0_weights")

            def project(st, width, scaled):
                with v.Fori(0, NC) as c:
                    for j in range(CH):
                        ln_apply(st, c, j, False)
                    for j in range(CH):
                        t = c * CH + j
                        v.wait_ge(sem(f"{st}_mm"), AHEAD + t + 1)
                        if scaled:
                            ins = v.tensor_scalar(tile(ACC, t, width, ROW), PB[2 + j][:, 0:width], DINV[:, ds(t, 1)], None, ALU.mult)
                        else:
                            ins = v.tensor_copy(tile(ACC, t, min(width, ROW), ROW), PB[2 + j][:, 0:min(width, ROW)])
                            if width > ROW:
                                ins = v.tensor_copy(AD[:, ds(t * 8, 8)], PB[2 + j][:, ROW:width])
                        ins.then_inc(sem("rows"), 1)

            project("g0", ROW, False)
            v.wait_ge(sem("g0_gathered"), 16 * 2 * NT)
            heads = lambda buf: buf.rearrange("p (t c) -> p t c", c=ROW)
            al = ADS[:, 0:4 * NT].rearrange("p (t h) -> p t h", h=4)
            z2 = SMALL[:, 200:200 + 4 * NT].rearrange("p (t h) -> p t h", h=4)
            line.step(v, v.tensor_tensor(al, heads(ACC[:, :])[:, :, D:D + 4], heads(BIG[:, 0:NT * ROW])[:, :, D + 4:D + 8], ALU.add))
            line.step(v, v.tensor_scalar(z2, al, 0.01, None, ALU.mult))
            line.step(v, v.tensor_tensor(al, al, z2, ALU.max))
            line.step(v, v.tensor_reduce(T1[:, :], al, AX.X, ALU.max))
            v.tensor_tensor(al, al, T1[:, :].unsqueeze(2).to_broadcast([P, NT, 4]), ALU.subtract).then_inc(sem("g0_logit"), 1)
            v.wait_ge(sem("g0_exp"), 1)
            line.step(v, v.tensor_reduce(T1[:, :], al, AX.X, ALU.add))
            line.step(v, v.reciprocal(T2[:, :], T1[:, :]))
            line.step(v, v.tensor_tensor(T2[:, :], T2[:, :], MASK[:, :], ALU.mult))
            line.step(v, v.tensor_tensor(al, al, T2[:, :].unsqueeze(2).to_broadcast([P, NT, 4]), ALU.mult))
            per = 3
            with v.Fori(0, NT) as t:
                line.enter(t, per)
                line.step(v, v.tensor_tensor(TMP[:, 0:D].rearrange("p (h d) -> p h d", h=4), tile(BIG, t, D, ROW).rearrange("p (h d) -> p h d", h=4),
                                             ADS[:, ds(t * 4, 4)].unsqueeze(2).to_broadcast([P, 4, 64]), ALU.mult))
                line.step(v, v.tensor_reduce(TMP[:, D:D + 64], TMP[:, 0:D].rearrange("p (h d) -> p d h", h=4), AX.X, ALU.add))
                line.mark(v.tensor_tensor(tile(X, t).rearrange("p (h d) -> p h d", h=4), tile(X, t).rearrange("p (h d) -> p h d", h=4),
                                          TMP[:, D:D + 64].unsqueeze(1).to_broadcast([P, 4, 64]), ALU.add))
            line.leave(NT, per)
            line.sync(v)

            ln_stats("f0")
            v.wait_ge(sem("ld_f0"), 16 * 6)
            per = 2
            with v.Fori(0, NT) as t:
                line.enter(t, per)
                line.step(v, v.tensor_scalar(TMP[:, 0:D], tile(X, t), MEAN[:, ds(t, 1)], RSTD[:, ds(t, 1)], ALU.subtract, ALU.mult))
                line.step(v, v.scalar_tensor_tensor(TMP[:, D:2 * D], TMP[:, 0:D], 1.0, CSTB[:, 3 * D:4 * D], ALU.mult, ALU.mult, accum_out=T1[:, ds(t, 1)]))
            line.leave(NT, per)
            line.sync(v)
            line.mark(v.tensor_scalar(T2[:, :], MASK[:, :], BIG_NUM, -BIG_NUM, ALU.mult, ALU.add))
            line.step(v, v.tensor_scalar(T1[:, :], T1[:, :], SLF[:, 15:16], None, ALU.add))
            v.tensor_tensor(COEF[:, :], T1[:, :], T2[:, :], ALU.add).then_inc(sem("f0_score"), 1)
            v.wait_ge(sem("f0_rankrow"), 16)
            SC = SMALL[:, 400:400 + 3 * NT]
            line.step(v, v.memset(SC, 0.0))
            for t in range(NT):
                line.step(v, v.tensor_scalar(JUNK[:, t * P:NT * P], RANKROW[:, t * P:NT * P], COEF[:, t:t + 1], 0.0, ALU.is_gt, ALU.add, accum_out=SC[:, t:t + 1]))
                if t:
                    line.step(v, v.tensor_scalar(JUNK[:, 0:t * P], RANKROW[:, 0:t * P], COEF[:, t:t + 1], 0.0, ALU.is_ge, ALU.add, accum_out=SC[:, NT + t:NT + t + 1]))
                line.step(v, v.scalar_tensor_tensor(OH[:, 0:P], RANKROW[:, t * P:(t + 1) * P], COEF[:, t:t + 1], LOWER[:, :], ALU.is_equal, ALU.mult,
                                                 accum_out=SC[:, 2 * NT + t:2 * NT + t + 1]))
            line.sync(v)
            line.step(v, v.tensor_tensor(T1[:, :], SC[:, 0:NT], SC[:, NT:2 * NT], ALU.add))
            line.step(v, v.tensor_tensor(T1[:, :], T1[:, :], SC[:, 2 * NT:3 * NT], ALU.add))
            line.step(v, v.tensor_scalar(T1[:, :], T1[:, :], float(KSEL), None, ALU.is_lt))
            line.step(v, v.tensor_tensor(COEF[:, :], T1[:, :], COEF[:, :], ALU.mult))
            v.sem_inc(sem("f0_out"), AHEAD)
            per = 2 * CH
            with v.Fori(0, NC) as c:
                line.enter(c, per)
                for j in range(CH):
                    ln_apply("f0", c, j, True)
                for j in range(CH):
                    t = c * CH + j
                    v.wait_ge(sem("f0_y"), t + 1)
                    v.tensor_tensor(TMP[:, (j % 2) * D:(j % 2 + 1) * D], PB[6 + j % 2][:, 0:D], CSTB[:, 2 * D:3 * D], ALU.add).then_inc(sem("f0_out"), 1)
                    v.wait_ge(sem("f0_out"), AHEAD + t + 1)
                    line.mark(v.scalar_tensor_tensor(tile(X, t), TMP[:, (j % 2) * D:(j % 2 + 1) * D], COEF[:, ds(t, 1)], tile(X, t), ALU.mult, ALU.add))
            line.leave(NC, per)
            line.sync(v)

            def sum_slots(st, width):
                v.sem_inc(sem(f"{st}_acc"), BODY)

                def onehot(half, first):
                    v.tensor_tensor(OH[:, half * GRP * P:(half + 1) * GRP * P].rearrange("p (k n) -> p k n", k=GRP),
                                    IOTA[:, :].unsqueeze(1).to_broadcast([P, GRP, P]),
                                    DREL[:, ds(first, GRP)].unsqueeze(2).to_broadcast([P, GRP, P]), ALU.is_equal).then_inc(sem(f"{st}_oh"), 1)
                onehot(0, 0)
                regs = [v.alloc_register(f"{st}_row{k}") for k in range(GRP)]
                with v.Fori(0, TURNS) as i:
                    for q in range(NG):
                        n0 = i * BODY + q * GRP
                        v.wait_ge(sem(f"{st}_mm"), BODY + n0)
                        onehot((q + 1) % 2, n0 + GRP)
                        v.load(regs, WROW[0:1, ds(n0, GRP)])
                        for k in range(GRP):
                            row = v.snap(regs[k], min_val=0, max_val=(NT - 1) * ROW)
                            v.wait_ge(sem(f"{st}_mm"), BODY + n0 + k + 1)
                            v.wait_ge(sem(f"{st}_acc"), BODY + n0 + k)
                            dst = ACC[:, ds(row, width)]
                            v.tensor_tensor(dst, dst, PB[k][:, 0:width], ALU.add).then_inc(sem(f"{st}_acc"), 1)
                v.wait_ge(sem(f"{st}_acc"), BODY + SLOTS)
                for r in regs:
                    v.free_register(r)

            def gcn(st, sums, bias):
                ln_stats(st)
                project(st, D, True)
                v.wait_ge(sem("table_stored"), (GNNS.index(st) + 1) * NC * 16)
                v.wait_ge(sem("rows"), rows_before(st) + AHEAD + NT)
                sum_slots(sums, D)
                per = 2
                v.wait_ge(sem("ld_bias"), 16 * 5)
                with v.Fori(0, NT) as t:
                    line.enter(t, per)
                    line.step(v, v.scalar_tensor_tensor(TMP[:, 0:D], tile(ACC, t, D, ROW), DINV[:, ds(t, 1)], bias, ALU.mult, ALU.add))
                    line.step(v, v.scalar_tensor_tensor(tile(X, t), TMP[:, 0:D], 0.0, tile(X, t), ALU.max, ALU.add))
                line.leave(NT, per)
                line.sync(v)

            gcn("g1", "a1", CSTB[:, 4 * D:5 * D])

            st = "t1"
            ln_stats(st)
            v.wait_ge(sem("ld_t1"), 16 * 12)
            line.mark(v.tensor_copy(BXR.rearrange("p (h n) -> p h n", h=8), BX.unsqueeze(2).to_broadcast([64, 8, P])))
            line.mark(v.memset(TMP[:, 0:512], 0.0))
            line.step(v, v.tensor_scalar(TEMPC, TEMPC, 0.1, 5.0, ALU.max, ALU.min))
            v.reciprocal(RTEMP, TEMPC).then_inc(sem(f"{st}_bxr"), 1)
            v.wait_ge(sem(f"{st}_bxr"), 1)
            v.wait_ge(sem(f"{st}_wxs"), 1)
            g8 = lambda buf: buf.rearrange("p (h g) -> p h g", h=8)
            rt = RTEMP.unsqueeze(2).to_broadcast([P, 8, 64])
            line.mark(v.tensor_tensor(g8(WXS[:, 0:512]), g8(PB[0][:, :]), rt, ALU.mult))
            line.mark(v.tensor_tensor(g8(WXS[:, 512:1024]), g8(PB[1][:, :]), rt, ALU.mult))
            line.step(v, v.tensor_tensor(g8(LBIAS), g8(PB[2][:, :]), BSL.unsqueeze(1).to_broadcast([P, 8, 64]), ALU.add))
            v.tensor_tensor(g8(LBIAS), g8(LBIAS), rt, ALU.mult).then_inc(sem(f"{st}_fold"), 1)
            v.wait_ge(sem(f"{st}_fold"), 1)
            v.sem_inc(sem(f"{st}_lgc"), AHEAD)
            per = 3 * CH
            with v.Fori(0, NC) as c:
                line.enter(c, per)
                for j in range(CH):
                    v.wait_ge(sem(f"{st}_tok"), AHEAD + c * CH + j + 1 - CH)
                    ln_apply(st, c, j, False)

                def shift(j):
                    n = c * CH + j
                    w = SW[:, j * 512:(j + 1) * 512]
                    v.wait_ge(sem(f"{st}_lg"), AHEAD + n + 1)
                    v.tensor_tensor(w, PB[2 + j % 2][:, :], LBIAS, ALU.add).then_inc(sem(f"{st}_lgc"), 1)
                    v.wait_ge(sem(f"{st}_lgc"), AHEAD + n + 1)
                    line.step(v, v.tensor_reduce(SMALL[:, j * 8:j * 8 + 8], g8(w), AX.X, ALU.max))
                    v.tensor_tensor(g8(w), g8(w), SMALL[:, j * 8:j * 8 + 8].unsqueeze(2).to_broadcast([P, 8, 64]), ALU.subtract).then_inc(sem(f"{st}_sub"), 1)

                def normalise(j):
                    n = c * CH + j
                    w = SW[:, j * 512:(j + 1) * 512]
                    sm = SMALL[:, 64 + j * 8:64 + j * 8 + 8]
                    v.wait_ge(sem(f"{st}_exp"), n + 1)
                    line.step(v, v.tensor_reduce(sm, g8(w), AX.X, ALU.add))
                    line.step(v, v.reciprocal(sm, sm))
                    v.tensor_scalar(sm, sm, MASK[:, ds(n, 1)], None, ALU.mult).then_inc(sem(f"{st}_rs"), 1)
                    v.wait_ge(sem(f"{st}_rs"), n + 1)
                    v.tensor_tensor(g8(w), g8(w), sm.unsqueeze(2).to_broadcast([P, 8, 64]), ALU.mult).then_inc(sem(f"{st}_sw"), 1)
                shift(0)
                for j in range(1, CH):
                    shift(j)
                    normalise(j - 1)
                normalise(CH - 1)
            line.leave(NC, per)
            v.wait_ge(sem(f"{st}_sums"), 1)
            line.mark(v.tensor_copy(TOKT[:, 0:512], PB[4][:, :]))
            line.mark(v.tensor_copy(TOKT[:, 512:1024], PB[5][:, :]))
            line.step(v, v.tensor_copy(NORM, PB[6][0:1, :]))
            line.step(v, v.tensor_scalar(RN, NORM, 1e-5, None, ALU.add))
            v.reciprocal(RN, RN).then_inc(sem(f"{st}_norm"), 1)
            v.wait_ge(sem(f"{st}_tokens"), 1)
            line.step(v, v.tensor_copy(RNB, PB[1][0:64, :]))
            v.tensor_tensor(TOK, PB[0][0:64, :], RNB, ALU.mult).then_inc(sem(f"{st}_token"), 1)
            v.wait_ge(sem(f"{st}_qkv"), 1)
            line.mark(v.tensor_copy(QT, PB[2][0:64, :]))
            line.step(v, v.tensor_copy(KT, PB[3][0:64, :]))
            v.tensor_copy(VT, PB[4][0:64, :]).then_inc(sem(f"{st}_qkvc"), 1)
            v.wait_ge(sem(f"{st}_att"), 1)
            sm = SMALL[0:64, 0:8]
            smb = sm.unsqueeze(2).to_broadcast([64, 8, 64])
            line.step(v, v.tensor_reduce(sm, g8(PB[5][0:64, :]), AX.X, ALU.max))
            v.tensor_tensor(g8(ATT), g8(PB[5][0:64, :]), smb, ALU.subtract).then_inc(sem(f"{st}_sub2"), 1)
            v.wait_ge(sem(f"{st}_vw"), 1)
            for k in range(4):
                line.mark(v.tensor_copy(VW[:, k * 512:(k + 1) * 512], PB[k][0:64, :]))
            v.wait_ge(sem(f"{st}_exp2"), 1)
            line.step(v, v.tensor_reduce(sm, g8(ATT), AX.X, ALU.add))
            line.step(v, v.reciprocal(sm, sm))
            v.tensor_tensor(g8(ATT), g8(ATT), smb, ALU.mult).then_inc(sem(f"{st}_soft"), 1)
            v.wait_ge(sem(f"{st}_attT"), 1)
            v.tensor_copy(ATTT, PB[6][0:64, :]).then_inc(sem(f"{st}_attc"), 1)
            v.wait_ge(sem(f"{st}_m"), 1)
            for k in range(4):
                line.mark(v.tensor_copy(MM[0:64, k * D:(k + 1) * D], PB[k][0:64, 0:D]))
                ins = v.tensor_copy(MO[:, k * D:(k + 1) * D], PB[k][0:64, D:2 * D])
            ins.then_inc(sem(f"{st}_mout"), 1)
            v.sem_inc(sem(f"{st}_out"), AHEAD)
            with v.Fori(0, NC) as c:
                for j in range(CH):
                    n = c * CH + j
                    v.wait_ge(sem(f"{st}_y"), AHEAD + n + 1)
                    v.tensor_tensor(tile(X, n), tile(X, n), PB[4 + j % 2][:, 0:D], ALU.add).then_inc(sem(f"{st}_out"), 1)
            v.wait_ge(sem(f"{st}_out"), AHEAD + NT)

            gcn("g2", "a2", CSTB[:, 5 * D:6 * D])

            def first_of(row, best, onehot, tmp, n):
                r8 = lambda buf: buf.rearrange("p (n e) -> p n e", e=8)
                wide = lambda buf: buf.unsqueeze(2).to_broadcast([P, n, 8])
                iota8 = IOTA[:, 0:8].unsqueeze(1).to_broadcast([P, n, 8])
                line.step(v, v.tensor_reduce(best, r8(row), AX.X, ALU.max))
                line.step(v, v.tensor_tensor(r8(tmp), r8(row), wide(best), ALU.is_lt))
                line.step(v, v.scalar_tensor_tensor(r8(tmp), r8(tmp), 8.0, iota8, ALU.mult, ALU.add))
                line.step(v, v.tensor_reduce(onehot[:, 0:n], r8(tmp), AX.X, ALU.min))
                line.step(v, v.tensor_tensor(r8(tmp), iota8, wide(onehot[:, 0:n]), ALU.is_equal))
                line.step(v, v.tensor_copy(onehot, tmp))

            st = "m2"
            line.step(v, v.memset(COMBW, 0.0))
            v.memset(ACC[:, 0:CH * D], 0.0).then_inc(sem(f"{st}_b2zero"), 1)
            ln_stats(st)
            v.wait_ge(sem("ld_m2"), 16 * 9)
            v.sem_inc(sem(f"{st}_out"), AHEAD)
            v.sem_inc(sem(f"{st}_b2"), AHEAD)
            r8 = lambda buf: buf.rearrange("p (n e) -> p n e", e=8)
            wide = lambda buf: buf.unsqueeze(2).to_broadcast([P, CH, 8])
            BEST, TOT, BEST2 = SMALL[:, 64:64 + CH], SMALL[:, 72:72 + CH], SMALL[:, 80:80 + CH]
            F1, F2, W8 = SMALL[:, 120:160], SMALL[:, 160:200], SMALL[:, 200:240]
            PROB = SMALL[:, 240:280]
            per = CH + 22
            with v.Fori(0, NC) as c:
                line.enter(c, per)
                for j in range(CH):
                    ln_apply(st, c, j, True)
                v.wait_ge(sem(f"{st}_logits"), c + 1)
                line.step(v, v.tensor_reduce(BEST, r8(PB[1][:, 0:8 * CH]), AX.X, ALU.max))
                v.tensor_tensor(r8(COMB), r8(PB[1][:, 0:8 * CH]), wide(BEST), ALU.subtract).then_inc(sem(f"{st}_sub"), 1)
                v.wait_ge(sem(f"{st}_exp"), c + 1)
                line.step(v, v.tensor_reduce(TOT, r8(COMB), AX.X, ALU.add))
                line.step(v, v.reciprocal(TOT, TOT))
                line.step(v, v.tensor_tensor(r8(PROB), r8(COMB), wide(TOT), ALU.mult))
                first_of(PROB, BEST, F1, W8, CH)
                line.step(v, v.scalar_tensor_tensor(COMB, F1, -2.0, PROB, ALU.mult, ALU.add))
                first_of(COMB, BEST2, F2, W8, CH)
                line.step(v, v.tensor_tensor(TOT, BEST, BEST2, ALU.add))
                line.step(v, v.tensor_scalar(TOT, TOT, 1e-12, None, ALU.max))
                line.step(v, v.reciprocal(TOT, TOT))
                line.step(v, v.tensor_tensor(F1, F1, F2, ALU.add))
                line.step(v, v.tensor_tensor(F1, F1, PROB, ALU.mult))
                v.tensor_tensor(r8(COMB), r8(F1), wide(TOT), ALU.mult).then_inc(sem(f"{st}_comb"), 1)
                v.wait_ge(sem(f"{st}_comb"), c + 1)
                for e in range(8):
                    for j in range(CH):
                        n = (c * 8 + e) * CH + j
                        v.wait_ge(sem(f"{st}_y"), n + 1)
                        v.wait_ge(sem(f"{st}_out"), AHEAD + n + 1 - CH)
                        v.scalar_tensor_tensor(tile(X, c * CH + j), PB[6 + (e * CH + j) % 2][:, 0:D], COMB[:, j * 8 + e:j * 8 + e + 1], tile(X, c * CH + j),
                                               ALU.mult, ALU.add).then_inc(sem(f"{st}_out"), 1)
                v.wait_ge(sem(f"{st}_combT"), c + 1)
                v.tensor_copy(COMBT, PB[0][0:8 * CH, 0:P]).then_inc(sem(f"{st}_combTc"), 1)
                v.wait_ge(sem(f"{st}_b2y"), c + 1)
                v.wait_ge(sem(f"{st}_out"), AHEAD + (c + 1) * 8 * CH)
                for k in range(3):
                    w = min(512, CH * D - k * 512)
                    xx = X[:, ds(c * CH * D + k * 512, w)]
                    ins = v.tensor_tensor(xx, xx, PB[k][:, 0:w], ALU.add)
                ins.then_inc(sem(f"{st}_b2"), 1)
                v.wait_ge(sem(f"{st}_b2"), AHEAD + c + 1)
            line.leave(NC, per)
            line.sync(v)

            st = "g3"
            v.tensor_scalar(WHEAD[:, :], WROW[:, :], 255, None, ALU.bitwise_and).then_inc(sem(f"{st}_whead"), 1)
            ln_stats(st)
            v.wait_ge(sem("ld_w3"), 16 * 3)
            attention_columns(lambda b, k: WG[:, b * GW + D + 8 * k:b * GW + D + 8 * k + 8], CSTB[:, 0:D], CSTB[:, D:2 * D], 8, "g3_weights")
            project(st, 272, False)
            v.wait_ge(sem("rows"), rows_before(st) + AHEAD + NT)
            UM = SMALL[:, 800:808]
            line.step(v, v.tensor_reduce(UM, ACC[:, :].rearrange("p (t c) -> p c t", c=ROW)[:, D:D + 8, :], AX.X, ALU.max))
            v.sem_inc(sem(f"{st}_umax"), 1)
            v.wait_ge(sem(f"{st}_uT"), 1)
            line.step(v, v.tensor_reduce(SMALL[0:8, 808:809], PB[0][0:8, 0:P], AX.X, ALU.max))
            v.tensor_scalar(SMALL[0:8, 816:824], IDENT[0:8, 0:8], SMALL[0:8, 808:809], None, ALU.mult).then_inc(sem(f"{st}_udiag"), 1)
            v.wait_ge(sem(f"{st}_u"), 1)
            line.step(v, v.tensor_copy(UM, PB[0][:, 0:8]))
            h8 = lambda buf: buf.rearrange("p (t h) -> p t h", h=8)
            a_dst, bound, slope = AD[:, 0:8 * NT], AD[:, 8 * NT:16 * NT], SMALL[:, 850:850 + 8 * NT]
            line.step(v, v.tensor_tensor(h8(bound), h8(a_dst), UM.unsqueeze(1).to_broadcast([P, NT, 8]), ALU.add))
            line.step(v, v.tensor_scalar(slope, bound, 0.2, None, ALU.mult))
            v.tensor_tensor(bound, bound, slope, ALU.max).then_inc(sem(f"{st}_ad"), 1)
            v.wait_ge(sem("table_stored"), (GNNS.index(st) + 1) * NC * 16)
            line.step(v, v.memset(ACC[:, :], 0.0))

            st = "a3"
            v.sem_inc(sem(f"{st}_acc"), BODY)
            r8 = lambda buf: buf.rearrange("p (k h) -> p k h", h=8)

            def onehot(r, first):
                v.tensor_tensor(OH4[:, r * GRP * P:(r + 1) * GRP * P].rearrange("p (k n) -> p k n", k=GRP),
                                IOTA[:, :].unsqueeze(1).to_broadcast([P, GRP, P]),
                                DREL[:, ds(first, GRP)].unsqueeze(2).to_broadcast([P, GRP, P]), ALU.is_equal).then_inc(sem(f"{st}_oh"), 1)

            def logits(g, r, gathered):
                v.wait_ge(sem(f"{st}_in{r}"), gathered)
                v.wait_ge(sem(f"{st}_ad"), g + 1)
                rows = G[:, r * GRP * ROW:(r + 1) * GRP * ROW].rearrange("p (k c) -> p k c", c=ROW)
                terms = PB[6 + r % 2][:, 0:16 * GRP].rearrange("p (k c) -> p k c", c=16)
                z, low = r8(TMP[:, (r % 2) * 64:(r % 2 + 1) * 64]), r8(TMP[:, 128:192])
                line.step(v, v.tensor_tensor(z, rows[:, :, D:D + 8], terms[:, :, 0:8], ALU.add))
                line.step(v, v.tensor_scalar(low, z, 0.2, None, ALU.mult))
                line.step(v, v.tensor_tensor(z, z, low, ALU.max))
                v.tensor_tensor(z, z, terms[:, :, 8:16], ALU.subtract).then_inc(sem(f"{st}_z"), 1)

            def scale(g, r):
                v.wait_ge(sem(f"{st}_exp"), g + 1)
                for k in range(GRP):
                    row = G[:, (r * GRP + k) * ROW:(r * GRP + k + 1) * ROW]
                    chans = row[:, 0:D].rearrange("p (h d) -> p h d", h=8)
                    ins = v.tensor_tensor(chans, chans, row[:, D:D + 8].unsqueeze(2).to_broadcast([P, 8, 32]), ALU.mult)
                ins.then_inc(sem(f"{st}_scaled"), 1)

            for r in range(3):
                onehot(r, r * GRP)
            logits(0, 0, 16 * GRP)
            scale(0, 0)
            regs = [v.alloc_register(f"{st}_row{k}") for k in range(GRP)]
            per = 3
            with v.Fori(0, TURNS) as i:
                line.enter(i, per * NG)
                for q in range(NG):
                    g = i * NG + q
                    n0 = i * BODY + q * GRP
                    v.wait_ge(sem(f"{st}_mm"), BODY + n0)
                    onehot((q + 3) % NG, n0 + 3 * GRP)
                    logits(g + 1, (q + 1) % NG, 16 * GRP * (i + 1 + (q + 1) // NG))
                    v.load(regs, WROW[0:1, ds(n0, GRP)])
                    for k in range(GRP):
                        if k == 4:
                            scale(g + 1, (q + 1) % NG)
                        row = v.snap(regs[k], min_val=0, max_val=(NT - 1) * ROW)
                        v.wait_ge(sem(f"{st}_mm"), BODY + n0 + k + 1)
                        v.wait_ge(sem(f"{st}_acc"), BODY + n0 + k)
                        dst = ACC[:, ds(row, ROW)]
                        v.tensor_tensor(dst, dst, PB[k % 4][:, 0:ROW], ALU.add).then_inc(sem(f"{st}_acc"), 1)
            line.leave(TURNS, per * NG)
            v.wait_ge(sem(f"{st}_acc"), BODY + SLOTS)
            for r in regs:
                v.free_register(r)
            DEN = SMALL[:, 400:400 + 8 * NT]
            line.step(v, v.tensor_scalar(h8(DEN), ACC[:, :].rearrange("p (t c) -> p t c", c=ROW)[:, :, D:D + 8], 1e-16, None, ALU.add))
            line.step(v, v.reciprocal(DEN, DEN))
            per = 3
            with v.Fori(0, NT) as t:
                line.enter(t, per)
                line.step(v, v.tensor_tensor(TMP[:, 0:D].rearrange("p (h d) -> p h d", h=8), tile(ACC, t, D, ROW).rearrange("p (h d) -> p h d", h=8),
                                             DEN[:, ds(t * 8, 8)].unsqueeze(2).to_broadcast([P, 8, 32]), ALU.mult))
                line.step(v, v.tensor_tensor(TMP[:, 0:D], TMP[:, 0:D], CSTB[:, 6 * D:7 * D], ALU.add))
                line.step(v, v.scalar_tensor_tensor(tile(X, t), TMP[:, 0:D], 0.0, tile(X, t), ALU.max, ALU.add))
            line.leave(NT, per)

            st = "f3"
            ln_stats(st)
            line.sync(v)
            v.tensor_reduce(SMALL[:, 0:1], NMR[:, :], AX.X, ALU.add).then_inc(sem(f"{st}_stats"), 1)
            v.wait_ge(sem(f"{st}_mean"), 1)
            for b in range(KB):
                ins = v.tensor_scalar(OH[:, b * P:(b + 1) * P], ONES[:, :], PB[b][:, 0:1], 1.0 / N_NODES, ALU.mult, ALU.mult)
            ins.then_inc(sem(f"{st}_meanb"), 1)
            R, S1, P2 = SMALL[:, 16:24], SMALL[:, 24:25], SMALL[:, 32:40]
            v.wait_ge(sem(f"{st}_logits"), 1)
            v.wait_ge(sem("ld_wr"), 32)

            def softmax8(n):
                line.step(v, v.tensor_reduce(S1, R, AX.X, ALU.max))
                v.tensor_scalar(R, R, S1, None, ALU.subtract).then_inc(sem(f"{st}_sub"), 1)
                v.wait_ge(sem(f"{st}_exp"), n)
                line.step(v, v.tensor_reduce(S1, R, AX.X, ALU.add))
                line.step(v, v.reciprocal(S1, S1))
                line.step(v, v.tensor_scalar(R, R, S1, None, ALU.mult))
            line.step(v, v.tensor_tensor(R, PB[2][:, 0:8], BR, ALU.add))
            softmax8(1)
            line.step(v, v.tensor_scalar(P2, R, float(N_NODES), None, ALU.mult))
            line.step(v, v.reciprocal(P2, P2))
            line.step(v, v.tensor_scalar(P2, P2, CAP3, 1.0, ALU.mult, ALU.min))
            line.step(v, v.tensor_tensor(R, R, P2, ALU.mult))
            softmax8(2)
            B1_, B2_, F1, F2, W8 = SMALL[:, 40:41], SMALL[:, 41:42], SMALL[:, 64:72], SMALL[:, 72:80], SMALL[:, 80:88]
            first_of(R, B1_, F1, W8, 1)
            line.step(v, v.scalar_tensor_tensor(R, F1, -2.0, R, ALU.mult, ALU.add))
            first_of(R, B2_, F2, W8, 1)
            for k, F in ((0, F1), (1, F2)):
                line.step(v, v.tensor_tensor(W8, F, IOTA[:, 0:8], ALU.mult))
                line.step(v, v.tensor_reduce(SMALL[:, 42 + k:43 + k], W8, AX.X, ALU.add))
            v.tensor_copy(CHOSEN[:, :], SMALL[0:1, 42:44]).then_inc(sem(f"{st}_chosen"), 1)
            v.tensor_scalar(SMALL[:, 48:49], B2_, B1_, None, ALU.subtract).then_inc(sem(f"{st}_sub"), 1)
            v.wait_ge(sem(f"{st}_exp"), 3)
            line.step(v, v.tensor_scalar(SMALL[:, 49:50], SMALL[:, 48:49], 1.0, None, ALU.add))
            line.step(v, v.reciprocal(SMALL[:, 50:51], SMALL[:, 49:50]))
            line.step(v, v.tensor_tensor(SMALL[:, 51:52], SMALL[:, 48:49], SMALL[:, 50:51], ALU.mult))
            v.wait_ge(sem("ld_f3"), 16 * 8)
            for k in range(2):
                w = WB[:, k * 1024:(k + 1) * 1024]
                line.mark(v.tensor_scalar(w, w, SMALL[:, 50 + k:51 + k], None, ALU.mult))
            line.step(v, v.tensor_scalar(CSTB[:, 0:D], CSTB[:, 0:D], SMALL[:, 50:51], None, ALU.mult))
            v.scalar_tensor_tensor(CSTB[:, 0:D], CSTB[:, D:2 * D], SMALL[:, 51:52], CSTB[:, 0:D], ALU.mult, ALU.add).then_inc(sem(f"{st}_weights"), 1)
            v.wait_ge(sem(f"{st}_weights"), 1)
            v.sem_inc(sem(f"{st}_out"), AHEAD)
            per = CH
            with v.Fori(0, NC) as c:
                line.enter(c, per)
                for j in range(CH):
                    ln_apply(st, c, j, False)
                for j in range(CH):
                    t = c * CH + j
                    o = tile(ACC, t, D, ROW)
                    v.wait_ge(sem(f"{st}_y"), t + 1)
                    v.wait_ge(sem("xs"), tiles_before(st) + t + 1)
                    v.tensor_tensor(TMP[:, 0:D], PB[6 + j % 2][:, 0:D], XS[:, j * D:(j + 1) * D], ALU.add).then_inc(sem(f"{st}_out"), 1)
                    v.wait_ge(sem(f"{st}_out"), AHEAD + t + 1)
                    line.step(v, v.tensor_tensor(o, TMP[:, 0:D], CSTB[:, 0:D], ALU.add))
                    v.bn_stats(tile(ST6, t, 6, 6), o).then_inc(sem("bn"), 1)
            line.leave(NC, per)
            line.sync(v)
            moments("n3")
            per = 4
            with v.Fori(0, NT) as t:
                line.enter(t, per)
                o = tile(ACC, t, D, ROW)
                line.step(v, v.tensor_scalar(TMP[:, 0:D], o, MEAN[:, ds(t, 1)], RSTD[:, ds(t, 1)], ALU.subtract, ALU.mult))
                line.step(v, v.tensor_tensor(TMP[:, 0:D], TMP[:, 0:D], CSTB[:, 7 * D:8 * D], ALU.mult))
                line.step(v, v.tensor_tensor(TMP[:, 0:D], TMP[:, 0:D], CSTB[:, 8 * D:9 * D], ALU.add))
                line.step(v, v.tensor_tensor(tile(X, t), tile(X, t), TMP[:, 0:D], ALU.add))
            line.leave(NT, per)
            line.sync(v)

            v.memset(ONEP[:, :], 0.0).then_inc(sem("finished"), 1)



def kernel(**inputs):
    import numpy as _np
    import concourse.bacc as _bacc
    from concourse import mybir as _mybir
    from concourse.bass_utils import run_bass_kernel_spmd as _run

    nc = _bacc.Bacc("TRN2", target_bir_lowering=False, num_devices=1)
    pad = ET * P - N_EDGES
    laid = dict(inputs)
    laid["src"] = _np.concatenate([inputs["src"], _np.zeros(pad, _np.int32)])
    laid["dst"] = _np.concatenate([inputs["dst"], _np.full(pad, 4095, _np.int32)])
    laid["L1_ffn_W_xT"] = _np.transpose(inputs["L1_ffn_W_x"])
    laid["L2_ffn_router_wT"] = _np.transpose(inputs["L2_ffn_router_w"])
    arrays, args = {}, {}
    for name in laid:
        x = _np.ascontiguousarray(laid[name])
        arrays[f"in_{name}"] = x
        args[name] = nc.dram_tensor(f"in_{name}", x.shape, _mybir.dt.from_np(x.dtype), kind="ExternalInput").ap()
    out = nc.dram_tensor("out_0", (N_NODES, D), F32, kind="ExternalOutput").ap()
    build(nc, args, out)
    r = _run(nc, [arrays], core_ids=[0])
    return r.results[0]["out_0"]
```

```python
import concourse.bass as bass
from concourse import mybir
from contextlib import ExitStack

F32 = mybir.dt.float32
I32 = mybir.dt.int32
BF16 = mybir.dt.bfloat16
ALU = mybir.AluOpType
ACT = mybir.ActivationFunctionType
AX = mybir.AxisListType
ds = bass.ds

P = 128
D = 256
KB = D // P
N_NODES = 3125
N_EDGES = 50000
NT = (N_NODES + P - 1) // P
REST = N_NODES - (NT - 1) * P
CH = 5
NC = NT // CH
CW = CH * P
HALF = CW // 2
ROW = 264
ET = 392
SLOTS = 416
GRP = 8
NG = 4
BODY = GRP * NG
TURNS = SLOTS // BODY
LN_EPS = 1e-5
KSEL = 1561
CAP3 = float(-(-N_NODES * 5 // 4 // 8))
ORDER = ("g0", "f0", "g1", "t1", "g2", "m2", "g3", "f3", "n3")
GNNS = ("g0", "g1", "g2", "g3")
BIG_NUM = 3.0e38
AHEAD = 5


def tiles_before(st):
    return NT * ORDER.index(st)


def rows_before(st):
    return NT * GNNS.index(st)


class Chain:

    def __init__(self, sem):
        self.sem, self.done, self.turn = sem, 0, 0

    def mark(self, ins):
        ins.then_inc(self.sem, 1)
        self.done += 1

    def sync(self, eng):
        eng.wait_ge(self.sem, self.turn + self.done)

    def step(self, eng, ins):
        self.mark(ins)
        self.sync(eng)

    def enter(self, i, per):
        self.turn, self.first = i * per, self.done

    def leave(self, n, per):
        assert self.done - self.first == per, (self.done - self.first, per)
        self.done, self.turn = self.first + n * per, 0


def build(nc, a, out):
    ctx = ExitStack()
    with ctx:
        def sb(name, shape, dt=F32):
            return ctx.enter_context(nc.sbuf_tensor(name, shape, dt))

        sems = {}

        def sem(name):
            if name not in sems:
                sems[name] = ctx.enter_context(nc.semaphore(name))
            return sems[name]

        X = sb("X", [P, NT * D])
        ACC = sb("ACC", [P, NT * ROW])
        BIG = sb("BIG", [P, 12800])
        XS = sb("XS", [P, CH * D])
        XT = sb("XT", [P, KB * CW])
        WA = sb("WA", [P, 4096])
        WB = sb("WB", [P, 4096])
        WG = sb("WG", [P, KB * 272])
        SW = sb("SW", [P, CH * 512])
        OH = sb("OH", [P, 2 * GRP * P])
        SRCI = sb("SRCI", [P, SLOTS + GRP * NG], I32)
        DREL = sb("DREL", [P, SLOTS + GRP * NG])
        IDX = sb("IDX", [P, NG * GRP], I32)
        WROW = sb("WROW", [1, 512], I32)
        IDENT = sb("IDENT", [P, P])
        ONES = sb("ONES", [P, P])
        IOTA = sb("IOTA", [P, P])
        IOTAB = sb("IOTAB", [P, P], BF16)
        ZEROB = sb("ZEROB", [P, NT], BF16)
        IOTAP = sb("IOTAP", [P, 4])
        LOWER = sb("LOWER", [P, P])
        MASK = sb("MASK", [P, NT])
        ST6 = sb("ST6", [P, NT * 6])
        MEAN = sb("MEAN", [P, NT])
        VAR = sb("VAR", [P, NT])
        RSTD = sb("RSTD", [P, NT])
        NMR = sb("NMR", [P, NT])
        ONEP = sb("ONEP", [P, NT])
        T1 = sb("T1", [P, NT])
        T2 = sb("T2", [P, NT])
        DINV = sb("DINV", [P, NT])
        SMALL = sb("SMALL", [P, 6 * 200])
        IDN = sb("IDN", [P, 2 * NT], I32)
        SLI = sb("SLI", [P, 4], I32)
        SLF = sb("SLF", [P, 16])
        TMP = sb("TMP", [P, 2 * ROW])
        COEF = sb("COEF", [P, NT])
        CSTB = sb("CSTB", [P, 13 * D])
        B1 = sb("B1", [P, 16])
        PB = [ctx.enter_context(nc.psum_tensor(f"PB{i}", [P, 512], F32)) for i in range(8)]

        table = nc.dram_tensor("table", (NT * P, ROW), F32, kind="Internal").ap()
        wtab = nc.dram_tensor("wtab", (1, NT * P), F32, kind="Internal").ap()

        G = BIG[:, 0:BODY * ROW]
        RANKROW = BIG[:, 5120:5120 + NT * P]
        JUNK = BIG[:, 5120 + NT * P:5120 + 2 * NT * P]
        HT = BIG[:, 0:8 * CW]
        dst2 = SW[:, 0:ET].bitcast(I32)
        dlo = SW[:, ET:2 * ET].bitcast(I32)
        dhi = SW[:, 2 * ET:3 * ET].bitcast(I32)
        dlob = SW[:, 3 * ET:3 * ET + ET // 2].bitcast(BF16)
        dhib = SW[:, 4 * ET:4 * ET + ET // 2].bitcast(BF16)
        HB = 7
        ob = OH[:, 0:HB * P].bitcast(BF16)
        oa = TMP[:, 0:HB * NT].bitcast(BF16)
        slot_src = SW[:, 0:512].bitcast(I32)
        slot_dst = SW[:, 512:1024].bitcast(I32)
        slot_srcf = SW[:, 1024:1536]
        slot_dstf = SW[:, 1536:2048]
        ADS = SMALL[:, 0:200]

        def tile(buf, t, w=D, stride=D):
            return buf[:, ds(t * stride, w)]

        GW = 272
        WXS, WFX = WA[:, 0:1024], WA[:, 1024:2048]
        WXT = WA[0:64, 2048:4096]
        WSL, WQ, WK, WV = (WB[0:64, 64 * n:64 * n + 64] for n in range(4))
        WOUT = WB[0:64, 256:2304]
        BX, BXR = WB[0:64, 2304:2312], WB[0:64, 2312:3336]
        BFX, BOUT, TEMPC = WB[0:1, 3336:3848], WB[:, 3848:3850], WB[:, 3850:3858]
        BSL, RTEMP = WB[:, 3858:3922], WB[:, 3922:3930]
        LBIAS = CSTB[:, 9 * D:11 * D]
        SWT = BIG[:, :]
        VW, MO, MM = ACC[0:64, 0:2048], ACC[0:64, 2048:3072], ACC[:, 4096:5120]
        TOKT = XS[:, 0:1024]
        WSUM = SMALL[:, 200:712]
        NORM, RN, RNB, KT, VT = SW[0:1, 0:512], SW[0:1, 512:1024], SW[0:64, 512:1024], SW[0:64, 1024:1536], SW[0:64, 1536:2048]
        TOK, QT, ATT, ATTT = XT[0:64, 0:512], XT[0:64, 512:1024], SW[0:64, 0:512], SW[0:64, 2048:2560]
        ROUTER = CSTB[:, 12 * D:12 * D + 16]
        B2D = ACC[0:8 * CH, 0:CH * D]
        COMBW = SMALL[:, 960:960 + P]
        COMB = COMBW[:, 0:8 * CH]
        COMBT = SMALL[0:8 * CH, 800:800 + P]
        AD = SMALL[:, 0:16 * NT]
        OH4, OHT = WA, WB
        WHEAD = sb("WHEAD", [1, 512], I32)
        WR, BR = CSTB[:, 12 * D + 16:12 * D + 32], CSTB[:, 12 * D + 32:12 * D + 40]
        CHOSEN = sb("CHOSEN", [1, 2], I32)
        dvec = Chain(sem("dve_line"))

        def chunks(eng, body):
            with eng.Fori(0, NC - 1) as c:
                body(c, True)
            body(NC - 1, False)

        block = ctx.enter_context(nc.Block())

        @block.sync
        def _(sp):
            sp.wait_ge(sem("x_padded"), 1)
            sp.dma_start(X[:, 0:(NT - 1) * D].rearrange("p (t c) -> p t c", c=D),
                         a["x"][0:(NT - 1) * P, :].rearrange("(t p) c -> p t c", p=P)).then_inc(sem("ld_x"), 16)
            sp.dma_start(X[0:REST, (NT - 1) * D:NT * D], a["x"][(NT - 1) * P:N_NODES, :]).then_inc(sem("ld_x"), 16)
            with nc.allow_non_contiguous_dma(reason="edge index columns"):
                sp.dma_start(IDN[:, 0:NT], a["dst"][0:NT * P].rearrange("(t p) -> p t", p=P)).then_inc(sem("ld_idn"), 16)
                sp.dma_start(IDN[:, NT:2 * NT], a["src"][0:NT * P].rearrange("(t p) -> p t", p=P)).then_inc(sem("ld_idn"), 16)
            sp.dma_start(dst2, a["dst"].rearrange("(p c) -> p c", p=P)).then_inc(sem("ld_dst"), 16)
            wg = WG[:, :].rearrange("p (b c) -> p b c", b=KB)
            sp.dma_start(wg[:, :, 0:D], a["L0_gnn_weight"].rearrange("(b p) c -> p b c", p=P)).then_inc(sem("ld_w0"), 16)
            sp.dma_start(CSTB[:, 0:D], a["L0_gnn_attn_l"].rearrange("h d -> (h d)").partition_broadcast(P)).then_inc(sem("ld_w0"), 16)
            sp.dma_start(CSTB[:, D:2 * D], a["L0_gnn_attn_r"].rearrange("h d -> (h d)").partition_broadcast(P)).then_inc(sem("ld_w0"), 16)

            def store_table(st):
                for c in range(NC):
                    sp.wait_ge(sem("rows"), rows_before(st) + AHEAD + (c + 1) * CH)
                    sp.dma_start(table[c * CW:(c + 1) * CW, :].rearrange("(t p) c -> p t c", p=P),
                                 ACC[:, c * CH * ROW:(c + 1) * CH * ROW].rearrange("p (t c) -> p t c", c=ROW)).then_inc(sem("table_stored"), 16)
                    sp.wait_ge(sem("table_stored"), (GNNS.index(st) * NC + c + 1) * 16)
            store_table("g0")

            sp.dma_start(WA[:, 0:KB * 1024].rearrange("p (b c) -> p b c", b=KB), a["L0_ffn_w1"].rearrange("(b p) c -> p b c", p=P)).then_inc(sem("ld_f0"), 16)
            sp.dma_start(WB[:, 0:8 * D].rearrange("p (b c) -> p b c", b=8), a["L0_ffn_w2"].rearrange("(b p) c -> p b c", p=P)).then_inc(sem("ld_f0"), 16)
            with nc.allow_non_contiguous_dma(reason="bias columns"):
                sp.dma_start(B1[:, 0:8], a["L0_ffn_b1"].rearrange("(b p) -> p b", p=P)).then_inc(sem("ld_f0"), 16)
            sp.dma_start(CSTB[:, 2 * D:3 * D], a["L0_ffn_b2"].partition_broadcast(P)).then_inc(sem("ld_f0"), 16)
            sp.dma_start(CSTB[:, 3 * D:4 * D], a["L0_ffn_wr"].rearrange("a b -> (a b)").partition_broadcast(P)).then_inc(sem("ld_f0"), 16)
            sp.dma_start(SLF[:, 15:16], a["L0_ffn_br"].partition_broadcast(P)).then_inc(sem("ld_f0"), 16)
            sp.wait_ge(sem("f0_scoreT"), 1)
            sp.dma_start(wtab.rearrange("a (t p) -> (a t) p", p=P), TMP[0:NT, 0:P]).then_inc(sem("f0_wtab"), 16)
            sp.wait_ge(sem("f0_wtab"), 16)
            sp.dma_start(RANKROW, wtab.rearrange("a b -> (a b)").partition_broadcast(P)).then_inc(sem("f0_rankrow"), 16)

            for n, name in ((4, "L1_gnn_b"), (5, "L2_gnn_b"), (6, "L3_gnn_bias"), (7, "L3_ffn_gamma"), (8, "L3_ffn_beta")):
                sp.dma_start(CSTB[:, n * D:(n + 1) * D], a[name].partition_broadcast(P)).then_inc(sem("ld_bias"), 16)
            sp.wait_ge(sem("g0_mm"), AHEAD + NT)
            sp.dma_start(wg[:, :, 0:D], a["L1_gnn_W"].rearrange("(b p) c -> p b c", p=P)).then_inc(sem("ld_w1"), 16)
            store_table("g1")

            sp.wait_ge(sem("f0_y"), NT)
            sp.dma_start(WA[:, 1024:2048].rearrange("p (b c) -> p b c", b=KB), a["L1_ffn_W_fx"].rearrange("(b p) c -> p b c", p=P)).then_inc(sem("ld_t1"), 16)
            sp.dma_start(WA[0:64, 2048:4096].rearrange("p (h c) -> p h c", h=8), a["L1_ffn_W_xT"].rearrange("(h p) c -> p h c", p=64)).then_inc(sem("ld_t1"), 16)
            for n, name in enumerate(("W_slice", "W_q", "W_k", "W_v")):
                sp.dma_start(WB[0:64, 64 * n:64 * n + 64], a["L1_ffn_" + name]).then_inc(sem("ld_t1"), 16)
            sp.dma_start(WB[0:64, 256:2304].rearrange("p (h c) -> p h c", h=8), a["L1_ffn_W_out"].rearrange("(h p) c -> p h c", p=64)).then_inc(sem("ld_t1"), 16)
            with nc.allow_non_contiguous_dma(reason="bias columns"):
                sp.dma_start(BX, a["L1_ffn_b_x"].rearrange("(h p) -> p h", p=64)).then_inc(sem("ld_t1"), 16)
                sp.dma_start(BOUT, a["L1_ffn_b_out"].rearrange("(b p) -> p b", p=P)).then_inc(sem("ld_t1"), 16)
            sp.dma_start(BFX, a["L1_ffn_b_fx"].rearrange("(a n) -> a n", a=1)).then_inc(sem("ld_t1"), 16)
            sp.dma_start(TEMPC, a["L1_ffn_temperature"].rearrange("a h b c -> (a h b c)").partition_broadcast(P)).then_inc(sem("ld_t1"), 16)
            sp.dma_start(BSL, a["L1_ffn_b_slice"].partition_broadcast(P)).then_inc(sem("ld_t1"), 16)
            sp.wait_ge(sem("t1_mout"), 1)
            sp.dma_start(MM[64:P, :], MO).then_inc(sem("t1_moved"), 16)

            sp.wait_ge(sem("g1_mm"), AHEAD + NT)
            sp.dma_start(wg[:, :, 0:D], a["L2_gnn_W"].rearrange("(b p) c -> p b c", p=P)).then_inc(sem("ld_w2"), 16)
            store_table("g2")

            sp.wait_ge(sem("t1_out"), AHEAD + NT)
            sp.dma_start(WA[:, :].rearrange("p (e b c) -> p e b c", e=8, b=KB), a["L2_ffn_w1"].rearrange("e (b p) c -> p e b c", p=P)).then_inc(sem("ld_m2"), 16)
            sp.dma_start(WB[:, :].rearrange("p (e b c) -> p e b c", e=8, b=KB), a["L2_ffn_w2"].rearrange("e (b p) c -> p e b c", p=P)).then_inc(sem("ld_m2"), 16)
            with nc.allow_non_contiguous_dma(reason="bias columns"):
                sp.dma_start(B1[:, :].rearrange("p (e b) -> p e b", e=8), a["L2_ffn_b1"].rearrange("e (b p) -> p e b", p=P)).then_inc(sem("ld_m2"), 16)
            sp.dma_start(ROUTER.rearrange("p (b e) -> p b e", b=KB), a["L2_ffn_router_wT"].rearrange("(b p) e -> p b e", p=P)).then_inc(sem("ld_m2"), 16)
            sp.wait_ge(sem("m2_b2zero"), 1)
            for j in range(CH):
                sp.dma_start(B2D[j * 8:(j + 1) * 8, j * D:(j + 1) * D], a["L2_ffn_b2"]).then_inc(sem("ld_m2"), 16)

            sp.wait_ge(sem("g2_mm"), AHEAD + NT)
            sp.dma_start(wg[:, :, 0:D], a["L3_gnn_W"].rearrange("(b p) h d -> p b (h d)", p=P)).then_inc(sem("ld_w3"), 16)
            sp.dma_start(CSTB[:, 0:D], a["L3_gnn_att_src"].rearrange("h d -> (h d)").partition_broadcast(P)).then_inc(sem("ld_w3"), 16)
            sp.dma_start(CSTB[:, D:2 * D], a["L3_gnn_att_dst"].rearrange("h d -> (h d)").partition_broadcast(P)).then_inc(sem("ld_w3"), 16)
            store_table("g3")

            sp.dma_start(WR.rearrange("p (b e) -> p b e", b=KB), a["L3_ffn_Wr"].rearrange("(b p) e -> p b e", p=P)).then_inc(sem("ld_wr"), 16)
            sp.dma_start(BR, a["L3_ffn_br"].partition_broadcast(P)).then_inc(sem("ld_wr"), 16)
            sp.wait_ge(sem("f3_chosen"), 1)
            for k in range(2):
                e = sp.value_load(CHOSEN[0:1, k:k + 1], min_val=0, max_val=7)
                one = lambda name: a[name][ds(e, 1)]
                sp.dma_start(WA[:, :].rearrange("p (b k f) -> p b k f", b=4, k=2)[:, 0:KB, k, :],
                             one("L3_ffn_W1").rearrange("e (b p) f -> p (e b) f", p=P)).then_inc(sem("ld_f3"), 16)
                sp.dma_start(WB[:, k * 1024:(k + 1) * 1024].rearrange("p (b c) -> p b c", b=4),
                             one("L3_ffn_W2").rearrange("e (b p) c -> p (e b) c", p=P)).then_inc(sem("ld_f3"), 16)
                with nc.allow_non_contiguous_dma(reason="bias columns"):
                    sp.dma_start(B1[:, k * 4:(k + 1) * 4], one("L3_ffn_b1").rearrange("e (b p) -> p (e b)", p=P)).then_inc(sem("ld_f3"), 16)
                sp.dma_start(CSTB[:, k * D:(k + 1) * D], one("L3_ffn_b2").rearrange("e c -> (e c)").partition_broadcast(P)).then_inc(sem("ld_f3"), 16)

            for c in range(NC):
                sp.wait_ge(sem("finished"), c + 1)
                full = min(CH, NT - 1 - c * CH)
                sp.dma_start(out[c * CW:c * CW + full * P, :].rearrange("(t p) c -> p t c", p=P),
                             X[:, c * CH * D:(c * CH + full) * D].rearrange("p (t c) -> p t c", c=D)).then_inc(sem("stored"), 16)
            sp.dma_start(out[(NT - 1) * P:N_NODES, :], X[0:REST, (NT - 1) * D:NT * D]).then_inc(sem("stored"), 16)
            sp.wait_ge(sem("stored"), (NC + 1) * 16)

        @block.gpsimd
        def _(g):
            g.iota(IOTA[:, :], pattern=[[1, P]], base=0, channel_multiplier=0, allow_small_or_imprecise_dtypes=True).then_inc(sem("cst"), 1)
            g.iota(IOTAP[:, :], pattern=[[P, 4]], base=0, channel_multiplier=1, allow_small_or_imprecise_dtypes=True).then_inc(sem("cst"), 1)
            g.memset(ONES[:, :], 1.0).then_inc(sem("cst"), 1)
            g.wait_ge(sem("cst"), 3)
            g.affine_select(out=IDENT[:, :], in_=ONES[:, :], compare_op=ALU.is_equal, fill=0.0, base=0,
                            pattern=[[-1, P]], channel_multiplier=1).then_inc(sem("cst"), 1)
            g.affine_select(out=LOWER[:, :], in_=ONES[:, :], compare_op=ALU.is_gt, fill=0.0, base=0,
                            pattern=[[-1, P]], channel_multiplier=1).then_inc(sem("cst"), 1)
            g.affine_select(out=MASK[:, :], in_=ONES[:, 0:NT], compare_op=ALU.is_gt, fill=0.0, base=N_NODES,
                            pattern=[[-P, NT]], channel_multiplier=-1).then_inc(sem("cst"), 1)
            g.wait_ge(sem("table_stored"), 16 * NC)
            g.wait_ge(sem("ld_idn"), 32)
            for t in range(NT):
                g.indirect_dma_start(out=BIG[:, t * ROW:(t + 1) * ROW], out_offset=None, in_=table,
                                     in_offset=bass.IndirectOffsetOnAxis(ap=IDN[:, t:t + 1], axis=0)).then_inc(sem("g0_gathered"), 16)
                g.indirect_dma_start(out=ACC[:, t * ROW:(t + 1) * ROW], out_offset=None, in_=table,
                                     in_offset=bass.IndirectOffsetOnAxis(ap=IDN[:, NT + t:NT + t + 1], axis=0)).then_inc(sem("g0_gathered"), 16)

            g.wait_ge(sem("slot_tile"), 1)
            for k in range(4):
                g.indirect_dma_start(out=slot_src[:, k * P:(k + 1) * P], out_offset=None, in_=a["src"].rearrange("(t e) -> t e", e=P),
                                     in_offset=bass.IndirectOffsetOnAxis(ap=SLI[:, k:k + 1], axis=0)).then_inc(sem("ld_slots"), 16)
                g.indirect_dma_start(out=slot_dst[:, k * P:(k + 1) * P], out_offset=None, in_=a["dst"].rearrange("(t e) -> t e", e=P),
                                     in_offset=bass.IndirectOffsetOnAxis(ap=SLI[:, k:k + 1], axis=0)).then_inc(sem("ld_slots"), 16)
            def gather_slots(tb, st):
                g.wait_ge(sem("table_stored"), (GNNS.index(tb) + 1) * NC * 16)
                g.wait_ge(sem("slots_ready"), 1)
                g.tensor_copy(IDX[:, 0:GRP], SRCI[:, 0:GRP]).then_inc(sem(f"{st}_ix"), 1)
                with g.Fori(0, TURNS) as i:
                    for q in range(NG):
                        n = i * BODY + q * GRP
                        r = (q + 1) % NG
                        g.wait_ge(sem(f"{st}_mm"), BODY + n - 2 * GRP)
                        g.wait_ge(sem(f"{st}_ix"), i * NG + q + 1)
                        g.tensor_copy(IDX[:, r * GRP:(r + 1) * GRP], SRCI[:, ds(n + GRP, GRP)]).then_inc(sem(f"{st}_ix"), 1)
                        for k in range(q * GRP, (q + 1) * GRP):
                            g.indirect_dma_start(out=G[:, k * ROW:(k + 1) * ROW], out_offset=None, in_=table,
                                                 in_offset=bass.IndirectOffsetOnAxis(ap=IDX[:, k:k + 1], axis=0)).then_inc(sem(f"{st}_in{q}"), 16)
                g.wait_ge(sem(f"{st}_ix"), TURNS * NG + 1)

            gather_slots("g1", "a1")
            gather_slots("g2", "a2")
            gather_slots("g3", "a3")
            for k in range(GRP):
                g.indirect_dma_start(out=G[:, k * ROW:(k + 1) * ROW], out_offset=None, in_=table,
                                     in_offset=bass.IndirectOffsetOnAxis(ap=IDX[:, k:k + 1], axis=0)).then_inc(sem("a3_in0"), 16)

        @block.tensor
        def _(pe):
            pe.sem_inc(sem("tp"), AHEAD)
            pe.wait_ge(sem("cst"), 6)
            def turn(st, c, j):
                n = c * CH + j
                pe.wait_ge(sem("xs"), tiles_before(st) + n + 1)
                pe.wait_ge(sem("xt"), tiles_before(st) + AHEAD + n + 1 - (1 if j == 0 else 2))
                for b in range(KB):
                    mm = pe.transpose(PB[j % 2][:, b * P:(b + 1) * P], XS[:, j * D + b * P:j * D + (b + 1) * P], IDENT[:, :])
                mm.then_inc(sem("tp"), 1)

            def project(st, width):
                pe.sem_inc(sem(f"{st}_mm"), AHEAD)
                with pe.Fori(0, NC) as c:
                    for j in range(CH):
                        turn(st, c, j)
                    for j in range(CH):
                        n = c * CH + j
                        pe.wait_ge(sem("xt"), tiles_before(st) + AHEAD + n + 1)
                        pe.wait_ge(sem("rows"), rows_before(st) + AHEAD + n + 1 - CH)
                        for b in range(KB):
                            mm = pe.matmul(PB[2 + j][:, 0:width], XT[:, b * CW + j * P:b * CW + (j + 1) * P],
                                           WG[:, b * GW:b * GW + width], start=(b == 0), stop=(b == KB - 1))
                        mm.then_inc(sem(f"{st}_mm"), 1)

            pe.wait_ge(sem("g0_weights"), 1)
            project("g0", ROW)

            hist = PB[7][:, 0:NT]
            pe.wait_ge(sem("iotab"), 1)
            pe.sem_inc(sem("h_used"), 2)
            pe.matmul(hist, IOTAB[:, :], ZEROB[:, :], start=True, stop=False, skip_group_check=True)
            with pe.Fori(0, ET // (2 * HB)) as i:
                for r in range(2):
                    pe.wait_ge(sem("h_onehot"), i * 2 + r + 1)
                    for k in range(HB):
                        mm = pe.matmul(hist, ob[:, (r * HB + k) * P:(r * HB + k + 1) * P], oa[:, (r * HB + k) * NT:(r * HB + k + 1) * NT],
                                       start=False, stop=False, skip_group_check=True)
                    mm.then_inc(sem("h_used"), 1)
            pe.matmul(hist, IOTAB[:, :], ZEROB[:, :], start=False, stop=True, skip_group_check=True).then_inc(sem("hist"), 1)
            pe.wait_ge(sem("hist_sb"), 1)
            pe.matmul(PB[6][:, 0:NT], ONES[:, :], T1[:, :], start=True, stop=True).then_inc(sem("totals"), 1)
            pe.wait_ge(sem("slot_rows"), 1)
            for k in range(4):
                pe.transpose(PB[4][:, k * P:(k + 1) * P], slot_srcf[:, k * P:(k + 1) * P], IDENT[:, :])
                pe.transpose(PB[5][:, k * P:(k + 1) * P], slot_dstf[:, k * P:(k + 1) * P], IDENT[:, :])
                mm = pe.matmul(PB[6][0:1, k * P:(k + 1) * P], SLF[:, 4 + k:5 + k], IDENT[:, :], start=True, stop=True)
            mm.then_inc(sem("slotsT"), 1)

            def ffn(st, w1, w2):
                pe.sem_inc(sem(f"{st}_hid"), AHEAD)

                def body(c, more):
                    pe.wait_ge(sem("xt"), tiles_before(st) + AHEAD + c * CH + CH)
                    for h in range(8):
                        n = c * 8 + h
                        pe.wait_ge(sem(f"{st}_act"), AHEAD + n + 1 - 2)
                        for s in range(2):
                            for b in range(KB):
                                mm = pe.matmul(PB[2 + 2 * (h % 2) + s][:, 0:HALF], w1[:, b * 1024 + h * P:b * 1024 + (h + 1) * P],
                                               XT[:, b * CW + s * HALF:b * CW + (s + 1) * HALF], start=(b == 0), stop=(b == KB - 1))
                        mm.then_inc(sem(f"{st}_hid"), 1)
                    if more:
                        for j in range(CH):
                            turn(st, c + 1, j)
                    pe.wait_ge(sem(f"{st}_act"), AHEAD + c * 8 + 8)
                    for j in range(CH):
                        n = c * CH + j
                        pe.wait_ge(sem(f"{st}_out"), AHEAD + n + 1 - (1 if j == 0 else 2))
                        for h in range(8):
                            mm = pe.matmul(PB[6 + j % 2][:, 0:D], HT[:, h * CW + j * P:h * CW + (j + 1) * P], w2[:, h * D:(h + 1) * D],
                                           start=(h == 0), stop=(h == 7))
                        mm.then_inc(sem(f"{st}_y"), 1)
                for j in range(CH):
                    turn(st, 0, j)
                chunks(pe, body)

            pe.wait_ge(sem("f0_score"), 1)
            pe.transpose(PB[2][0:NT, 0:P], COEF[:, :], IDENT[:, :]).then_inc(sem("f0_scoreP"), 1)
            pe.wait_ge(sem("ld_f0"), 16 * 6)
            pe.wait_ge(sem("f0_scoreT"), 1)
            ffn("f0", WA, WB)

            def sum_slots(st, width):
                pe.sem_inc(sem(f"{st}_mm"), BODY)
                with pe.Fori(0, TURNS) as i:
                    for q in range(NG):
                        pe.wait_ge(sem(f"{st}_in{q}"), 16 * GRP * (i + 1))
                        pe.wait_ge(sem(f"{st}_oh"), i * NG + q + 1)
                        for k in range(GRP):
                            n = i * BODY + q * GRP + k
                            pe.wait_ge(sem(f"{st}_acc"), BODY + n + 1 - GRP)
                            pe.matmul(PB[k][:, 0:width], OH[:, ((q % 2) * GRP + k) * P:((q % 2) * GRP + k + 1) * P],
                                      G[:, (q * GRP + k) * ROW:(q * GRP + k) * ROW + width], start=True, stop=True).then_inc(sem(f"{st}_mm"), 1)

            pe.wait_ge(sem("ld_w1"), 16)
            project("g1", D)
            sum_slots("a1", D)

            def slices(st):
                pe.wait_ge(sem("ld_t1"), 16 * 12)
                pe.wait_ge(sem("a1_acc"), BODY + SLOTS)
                for b in range(KB):
                    for h in range(8):
                        pe.matmul(PB[b][:, h * 64:h * 64 + 64], WXT[:, h * D + b * P:h * D + (b + 1) * P], WSL, start=True, stop=True)
                pe.wait_ge(sem(f"{st}_bxr"), 1)
                for h in range(8):
                    mm = pe.matmul(PB[2][:, h * 64:h * 64 + 64], BXR[:, h * P:(h + 1) * P], WSL, start=True, stop=True)
                mm.then_inc(sem(f"{st}_wxs"), 1)
                pe.sem_inc(sem(f"{st}_lg"), AHEAD)
                pe.sem_inc(sem(f"{st}_tok"), AHEAD)
                pe.wait_ge(sem(f"{st}_fold"), 1)
                for k in (4, 5):
                    pe.matmul(PB[k][:, :], ONES[:, :], TMP[:, 0:512], start=True, stop=False, skip_group_check=True)
                with pe.Fori(0, NC) as c:
                    for j in range(CH):
                        turn(st, c, j)
                    for j in range(CH):
                        n = c * CH + j
                        pe.wait_ge(sem("xt"), tiles_before(st) + AHEAD + n + 1)
                        pe.wait_ge(sem(f"{st}_lgc"), AHEAD + n + 1 - (1 if j == 0 else 2))
                        for b in range(KB):
                            mm = pe.matmul(PB[2 + j % 2][:, :], XT[:, b * CW + j * P:b * CW + (j + 1) * P], WXS[:, b * 512:(b + 1) * 512],
                                           start=(b == 0), stop=(b == KB - 1))
                        mm.then_inc(sem(f"{st}_lg"), 1)
                    for j in range(CH):
                        n = c * CH + j
                        w = SW[:, j * 512:(j + 1) * 512]
                        pe.wait_ge(sem(f"{st}_sw"), n + 1)
                        for b in range(KB):
                            pe.matmul(PB[4 + b][:, :], XS[:, j * D + b * P:j * D + (b + 1) * P], w, start=False, stop=False, skip_group_check=True)
                        pe.wait_ge(sem(f"{st}_swt"), AHEAD + n + 1 - 1)
                        for b in range(4):
                            mm = pe.transpose(PB[7][:, b * P:(b + 1) * P], w[:, b * P:(b + 1) * P], IDENT[:, :])
                        mm.then_inc(sem(f"{st}_tok"), 1)
                for k in (4, 5):
                    pe.matmul(PB[k][:, :], ONES[:, :], TMP[:, 0:512], start=False, stop=True, skip_group_check=True)
                pe.wait_ge(sem(f"{st}_wsum"), 1)
                pe.matmul(PB[6][0:1, :], ONES[:, 0:1], WSUM, start=True, stop=True).then_inc(sem(f"{st}_sums"), 1)
                pe.wait_ge(sem(f"{st}_norm"), 1)
                for h in range(8):
                    o = slice(h * 64, h * 64 + 64)
                    for b in range(KB):
                        pe.matmul(PB[0][0:64, o], WFX[:, b * 512 + h * 64:b * 512 + h * 64 + 64], TOKT[:, b * 512 + h * 64:b * 512 + h * 64 + 64], start=(b == 0), stop=False)
                    pe.matmul(PB[0][0:64, o], BFX[:, o], NORM[:, o], start=False, stop=True)
                pe.matmul(PB[1][0:64, :], ONES[0:1, 0:64], RN, start=True, stop=True).then_inc(sem(f"{st}_tokens"), 1)
                pe.wait_ge(sem(f"{st}_token"), 1)
                for k, w in ((2, WQ), (3, WK), (4, WV)):
                    mm = pe.matmul(PB[k][0:64, :], w, TOK, start=True, stop=True)
                mm.then_inc(sem(f"{st}_qkv"), 1)
                pe.wait_ge(sem(f"{st}_qkvc"), 1)
                for h in range(8):
                    o = slice(h * 64, h * 64 + 64)
                    mm = pe.matmul(PB[5][0:64, o], QT[:, o], KT[:, o], start=True, stop=True)
                mm.then_inc(sem(f"{st}_att"), 1)
                for h in range(8):
                    mm = pe.matmul(PB[h // 2][0:64, (h % 2) * D:(h % 2 + 1) * D], VT[:, h * 64:h * 64 + 64], WOUT[:, h * D:(h + 1) * D], start=True, stop=True)
                mm.then_inc(sem(f"{st}_vw"), 1)
                pe.wait_ge(sem(f"{st}_soft"), 1)
                for h in range(8):
                    o = slice(h * 64, h * 64 + 64)
                    mm = pe.transpose(PB[6][0:64, o], ATT[:, o], IDENT[0:64, 0:64])
                mm.then_inc(sem(f"{st}_attT"), 1)
                pe.wait_ge(sem(f"{st}_attc"), 1)
                for h in range(8):
                    mm = pe.matmul(PB[h // 2][0:64, (h % 2) * D:(h % 2 + 1) * D], ATTT[:, h * 64:h * 64 + 64], VW[:, h * D:(h + 1) * D], start=True, stop=True)
                mm.then_inc(sem(f"{st}_m"), 1)
                pe.wait_ge(sem(f"{st}_moved"), 16)
                pe.wait_ge(sem(f"{st}_mout"), 1)
                pe.sem_inc(sem(f"{st}_o"), AHEAD)
                pe.sem_inc(sem(f"{st}_y"), AHEAD)
                with pe.Fori(0, NC) as c:
                    for i in range(4):
                        n = c * 4 + i
                        f, half = i // 2, i % 2
                        pe.wait_ge(sem(f"{st}_ob"), AHEAD + n + 1 - 4)
                        for b in range(4):
                            mm = pe.matmul(PB[i][:, 0:HALF], MM[:, b * D + f * P:b * D + (f + 1) * P], SWT[:, ds(c * CW + b * NT * P + half * HALF, HALF)],
                                           start=(b == 0), stop=(b == 3))
                        mm.then_inc(sem(f"{st}_o"), 1)
                    pe.wait_ge(sem(f"{st}_ob"), AHEAD + c * 4 + 4)
                    for j in range(CH):
                        n = c * CH + j
                        pe.wait_ge(sem(f"{st}_out"), AHEAD + n + 1 - (1 if j == 0 else 2))
                        for f in range(KB):
                            mm = pe.transpose(PB[4 + j % 2][:, f * P:(f + 1) * P], XT[:, f * CW + j * P:f * CW + (j + 1) * P], IDENT[:, :])
                        mm.then_inc(sem(f"{st}_y"), 1)

            slices("t1")
            pe.wait_ge(sem("ld_w2"), 16)
            project("g2", D)
            sum_slots("a2", D)

            def experts(st):
                pe.sem_inc(sem(f"{st}_hid"), AHEAD)

                def turned(c):
                    for j in range(CH):
                        turn(st, c, j)
                    pe.wait_ge(sem("xt"), tiles_before(st) + AHEAD + c * CH + CH)
                    for j in range(CH):
                        for b in range(KB):
                            mm = pe.matmul(PB[1][:, j * 8:j * 8 + 8], XT[:, b * CW + j * P:b * CW + (j + 1) * P], ROUTER[:, b * 8:b * 8 + 8],
                                           start=(b == 0), stop=(b == KB - 1))
                    mm.then_inc(sem(f"{st}_logits"), 1)

                def body(c, more):
                    pe.wait_ge(sem(f"{st}_b2"), AHEAD + c)

                    def hidden(e):
                        for h in range(KB):
                            pe.wait_ge(sem(f"{st}_act"), AHEAD + (c * 8 + e) * 2 + h + 1 - 2)
                            for s in range(2):
                                for b in range(KB):
                                    mm = pe.matmul(PB[2 + 2 * h + s][:, 0:HALF], WA[:, (e * KB + b) * D + h * P:(e * KB + b) * D + (h + 1) * P],
                                                   XT[:, b * CW + s * HALF:b * CW + (s + 1) * HALF], start=(b == 0), stop=(b == KB - 1))
                            mm.then_inc(sem(f"{st}_hid"), 1)

                    def outputs(e):
                        pe.wait_ge(sem(f"{st}_act"), AHEAD + (c * 8 + e) * 2 + 2)
                        for j in range(CH):
                            pe.wait_ge(sem(f"{st}_out"), AHEAD + (c * 8 + e) * CH + j + 1 - 2)
                            for h in range(KB):
                                mm = pe.matmul(PB[6 + (e * CH + j) % 2][:, 0:D], HT[:, ((e % 2) * KB + h) * CW + j * P:((e % 2) * KB + h) * CW + (j + 1) * P],
                                               WB[:, (e * KB + h) * D:(e * KB + h + 1) * D], start=(h == 0), stop=(h == KB - 1))
                            mm.then_inc(sem(f"{st}_y"), 1)
                    hidden(0)
                    for e in range(1, 8):
                        hidden(e)
                        outputs(e - 1)
                    pe.wait_ge(sem(f"{st}_comb"), c + 1)
                    if more:
                        turned(c + 1)
                    pe.wait_ge(sem(f"{st}_act"), AHEAD + c * 16 + 16)
                    pe.transpose(PB[2][:, 0:P], COMBW, IDENT[:, :]).then_inc(sem(f"{st}_combT"), 1)
                    outputs(7)
                    pe.wait_ge(sem(f"{st}_combTc"), c + 1)
                    for k in range(3):
                        w = min(512, CH * D - k * 512)
                        mm = pe.matmul(PB[3 + k][:, 0:w], COMBT, B2D[:, k * 512:k * 512 + w], start=True, stop=True)
                    mm.then_inc(sem(f"{st}_b2y"), 1)
                turned(0)
                chunks(pe, body)

            pe.wait_ge(sem("ld_m2"), 16 * 9)
            experts("m2")

            def sum_attended(st):
                regs = [pe.alloc_register(f"{st}_win{k}") for k in range(GRP)]

                def turned(g, r, first):
                    pe.wait_ge(sem(f"{st}_oh"), g + 1)
                    for s in range(2):
                        if not first:
                            pe.wait_ge(sem(f"{st}_tpc"), 2 * g + s - 1)
                        for k in range(4):
                            o = (r * GRP + s * 4 + k) * P
                            mm = pe.transpose(PB[4 + s][:, k * P:(k + 1) * P], OH4[:, o:o + P], IDENT[:, :])
                        mm.then_inc(sem(f"{st}_turned"), 1)

                def terms(g, r, n0):
                    pe.wait_ge(sem(f"{st}_tpc"), 2 * g + 2)
                    pe.wait_ge(sem(f"{st}_z"), g)
                    pe.load(regs, WHEAD[0:1, ds(n0, GRP)] if not isinstance(n0, int) else WHEAD[0:1, n0:n0 + GRP])
                    for k in range(GRP):
                        w = pe.snap(regs[k], min_val=0, max_val=(NT - 1) * 8)
                        mm = pe.matmul(PB[6 + r % 2][:, k * 16:k * 16 + 16].rearrange("p (a h) -> p a h", a=2), OHT[:, ((r % 2) * GRP + k) * P:((r % 2) * GRP + k + 1) * P],
                                       AD.rearrange("p (a n) -> p a n", a=2)[:, :, ds(w, 8)], start=True, stop=True)
                    mm.then_inc(sem(f"{st}_ad"), 1)

                pe.sem_inc(sem(f"{st}_mm"), BODY)
                turned(0, 0, True)
                pe.wait_ge(sem("g3_ad"), 1)
                turned(1, 1, False)
                terms(0, 0, 0)
                with pe.Fori(0, TURNS) as i:
                    for q in range(NG):
                        g = i * NG + q
                        terms(g + 1, q + 1, (g + 1) * GRP)
                        pe.wait_ge(sem(f"{st}_scaled"), g + 1)
                        for k in range(GRP):
                            if k == 4:
                                turned(g + 2, (q + 2) % NG, False)
                            n = i * BODY + q * GRP + k
                            pe.wait_ge(sem(f"{st}_acc"), BODY + n + 1 - 4)
                            pe.matmul(PB[k % 4][:, 0:ROW], OH4[:, (q * GRP + k) * P:(q * GRP + k + 1) * P],
                                      G[:, (q * GRP + k) * ROW:(q * GRP + k + 1) * ROW], start=True, stop=True).then_inc(sem(f"{st}_mm"), 1)

            pe.wait_ge(sem("g3_weights"), 1)
            project("g3", 272)
            pe.wait_ge(sem("g3_umax"), 1)
            pe.transpose(PB[0][0:8, 0:P], SMALL[:, 800:808], IDENT[:, :]).then_inc(sem("g3_uT"), 1)
            pe.wait_ge(sem("g3_udiag"), 1)
            pe.matmul(PB[0][:, 0:8], ONES[0:8, :], SMALL[0:8, 816:824], start=True, stop=True).then_inc(sem("g3_u"), 1)
            sum_attended("a3")

            pe.wait_ge(sem("f3_stats"), 1)
            for b in range(KB):
                for t in range(NT):
                    pe.matmul(PB[b][:, 0:1], X[:, t * D + b * P:t * D + (b + 1) * P], RSTD[:, t:t + 1], start=(t == 0), stop=False)
                mm = pe.matmul(PB[b][:, 0:1], ONES[:, :], SMALL[:, 0:1], start=False, stop=True)
            mm.then_inc(sem("f3_mean"), 1)
            pe.wait_ge(sem("f3_meanb"), 1)
            pe.wait_ge(sem("ld_wr"), 32)
            for b in range(KB):
                mm = pe.matmul(PB[2][:, 0:8], OH[:, b * P:(b + 1) * P], WR[:, b * 8:b * 8 + 8], start=(b == 0), stop=(b == KB - 1))
            mm.then_inc(sem("f3_logits"), 1)
            pe.wait_ge(sem("f3_weights"), 1)
            ffn("f3", WA, WB)

        @block.scalar
        def _(act):
            act.sem_inc(sem("xt"), AHEAD)
            def ln_root(st):
                act.wait_ge(sem("var"), ORDER.index(st) + 1)
                act.activation(T1[:, :], VAR[:, :], ACT.Sqrt).then_inc(sem("std"), 1)

            def to_xt(st, c, j):
                act.wait_ge(sem("tp"), tiles_before(st) + AHEAD + c * CH + j + 1)
                act.activation(XT[:, :].rearrange("p (b n) -> p b n", b=KB)[:, :, j * P:(j + 1) * P],
                               PB[j % 2][:, 0:D].rearrange("p (b n) -> p b n", b=KB), ACT.Copy).then_inc(sem("xt"), 1)

            def project(st):
                with act.Fori(0, NC) as c:
                    for j in range(CH):
                        act.wait_ge(sem(f"{st}_mm"), AHEAD + c * CH + j + 1 - CH)
                        to_xt(st, c, j)

            def ffn(st, func):
                act.sem_inc(sem(f"{st}_act"), AHEAD)

                def body(c, more):
                    for h in range(8):
                        act.wait_ge(sem(f"{st}_hid"), AHEAD + c * 8 + h + 1)
                        k = 2 + 2 * (h % 2)
                        for s in range(2):
                            ins = act.activation(HT[:, h * CW + s * HALF:h * CW + (s + 1) * HALF], PB[k + s][:, 0:HALF], func, bias=B1[:, h:h + 1])
                        ins.then_inc(sem(f"{st}_act"), 1)
                    if more:
                        for j in range(CH):
                            to_xt(st, c + 1, j)
                for j in range(CH):
                    to_xt(st, 0, j)
                chunks(act, body)

            ln_root("g0")
            project("g0")
            act.wait_ge(sem("deg"), 1)
            act.activation(DINV[:, :], VAR[:, :], ACT.Sqrt).then_inc(sem("dinv"), 1)
            act.wait_ge(sem("g0_logit"), 1)
            act.activation(ADS[:, 0:4 * NT], ADS[:, 0:4 * NT], ACT.Exp).then_inc(sem("g0_exp"), 1)
            ln_root("f0")
            act.wait_ge(sem("f0_scoreP"), 1)
            act.activation(TMP[0:NT, 0:P], PB[2][0:NT, 0:P], ACT.Copy).then_inc(sem("f0_scoreT"), 1)
            ffn("f0", ACT.Gelu_apprx_tanh)
            ln_root("g1")
            project("g1")
            def slices(st):
                act.sem_inc(sem(f"{st}_swt"), AHEAD)
                with act.Fori(0, NC) as c:
                    for j in range(CH):
                        act.wait_ge(sem(f"{st}_lg"), AHEAD + c * CH + j + 1 - CH)
                        to_xt(st, c, j)
                    for j in range(CH):
                        n = c * CH + j
                        w = SW[:, j * 512:(j + 1) * 512]
                        act.wait_ge(sem(f"{st}_sub"), n + 1)
                        act.activation(w, w, ACT.Exp).then_inc(sem(f"{st}_exp"), 1)
                        if j:
                            to_swt(st, n - 1)
                    to_swt(st, c * CH + CH - 1)
                act.wait_ge(sem(f"{st}_sub2"), 1)
                act.activation(ATT, ATT, ACT.Exp, scale=0.125).then_inc(sem(f"{st}_exp2"), 1)
                act.sem_inc(sem(f"{st}_ob"), AHEAD)
                with act.Fori(0, NC) as c:
                    act.wait_ge(sem(f"{st}_y"), AHEAD + c * CH)
                    for i in range(4):
                        f, half = i // 2, i % 2
                        act.wait_ge(sem(f"{st}_o"), AHEAD + c * 4 + i + 1)
                        act.activation(XT[:, f * CW + half * HALF:f * CW + (half + 1) * HALF], PB[i][:, 0:HALF], ACT.Identity,
                                       bias=BOUT[:, f:f + 1]).then_inc(sem(f"{st}_ob"), 1)

            def to_swt(st, n):
                act.wait_ge(sem(f"{st}_tok"), AHEAD + n + 1)
                act.activation(SWT.rearrange("p (b n) -> p b n", b=4)[:, :, ds(n * P, P)], PB[7][:, :].rearrange("p (b n) -> p b n", b=4),
                               ACT.Copy).then_inc(sem(f"{st}_swt"), 1)

            ln_root("t1")
            slices("t1")
            ln_root("g2")
            project("g2")

            st = "m2"
            ln_root(st)
            act.sem_inc(sem(f"{st}_act"), AHEAD)

            def body(c, more):
                act.wait_ge(sem(f"{st}_sub"), c + 1)
                act.activation(COMB, COMB, ACT.Exp).then_inc(sem(f"{st}_exp"), 1)
                for h in range(16):
                    act.wait_ge(sem(f"{st}_hid"), AHEAD + c * 16 + h + 1)
                    for s in range(2):
                        ins = act.activation(HT[:, (h % 4) * CW + s * HALF:(h % 4) * CW + (s + 1) * HALF], PB[2 + 2 * (h % 2) + s][:, 0:HALF],
                                             ACT.Gelu, bias=B1[:, h:h + 1])
                    ins.then_inc(sem(f"{st}_act"), 1)
                if more:
                    for j in range(CH):
                        to_xt(st, c + 1, j)
            for j in range(CH):
                to_xt(st, 0, j)
            chunks(act, body)

            ln_root("g3")
            project("g3")
            st = "a3"
            act.sem_inc(sem(f"{st}_z"), 1)

            def copy_turned(g, r):
                for s in range(2):
                    act.wait_ge(sem(f"{st}_turned"), 2 * g + s + 1)
                    act.activation(OHT[:, (r * 2 + s) * 512:(r * 2 + s + 1) * 512], PB[4 + s][:, :], ACT.Copy).then_inc(sem(f"{st}_tpc"), 1)

            def exps(g, r):
                act.wait_ge(sem(f"{st}_z"), g + 2)
                act.activation(G[:, r * GRP * ROW:(r + 1) * GRP * ROW].rearrange("p (k c) -> p k c", c=ROW)[:, :, D:D + 8],
                               TMP[:, (r % 2) * 64:(r % 2 + 1) * 64].rearrange("p (k h) -> p k h", k=GRP), ACT.Exp).then_inc(sem(f"{st}_exp"), 1)
            copy_turned(0, 0)
            copy_turned(1, 1)
            exps(0, 0)
            with act.Fori(0, TURNS) as i:
                for q in range(NG):
                    g = i * NG + q
                    copy_turned(g + 2, q % 2)
                    exps(g + 1, (q + 1) % NG)

            ln_root("f3")
            act.wait_ge(sem("f3_sub"), 1)
            act.activation(SMALL[:, 16:24], SMALL[:, 16:24], ACT.Exp).then_inc(sem("f3_exp"), 1)
            act.wait_ge(sem("f3_sub"), 2)
            act.activation(SMALL[:, 16:24], SMALL[:, 16:24], ACT.Exp).then_inc(sem("f3_exp"), 1)
            act.wait_ge(sem("f3_sub"), 3)
            act.activation(SMALL[:, 48:49], SMALL[:, 48:49], ACT.Exp).then_inc(sem("f3_exp"), 1)
            ffn("f3", ACT.Gelu)
            act.wait_ge(sem("var"), ORDER.index("n3") + 1)
            act.activation(T1[:, :], VAR[:, :], ACT.Sqrt).then_inc(sem("std"), 1)

        @block.vector
        def _(v):
            line = dvec
            v.sem_inc(sem("rows"), AHEAD)
            v.memset(X[:, (NT - 1) * D:NT * D], 0.0).then_inc(sem("x_padded"), 1)
            line.mark(v.memset(ZEROB[:, :], 0.0))
            v.wait_ge(sem("cst"), 6)
            line.sync(v)
            v.tensor_copy(IOTAB[:, :], IOTA[:, :]).then_inc(sem("iotab"), 1)
            def ln_stats(st):
                with v.Fori(0, NC) as c:
                    chunk_stats(c)
                moments(st)

            def chunk_stats(c):
                for j in range(CH):
                    v.bn_stats(tile(ST6, c * CH + j, 6, 6), tile(X, c * CH + j)).then_inc(sem("bn"), 1)

            def chunk(buf, c, w=D, stride=D):
                return buf[:, ds(c * CH * stride, CH * stride)].rearrange("p (t c) -> p t c", c=stride)[:, :, 0:w]

            def moments(st):
                v.wait_ge(sem("bn"), tiles_before(st) + NT)
                s6 = ST6[:, :].rearrange("p (t k) -> p k t", k=6)
                line.mark(v.tensor_tensor(T1[:, :], s6[:, 1, :], s6[:, 4, :], ALU.subtract))
                line.mark(v.tensor_tensor(MEAN[:, :], s6[:, 1, :], s6[:, 4, :], ALU.add))
                line.step(v, v.tensor_tensor(T2[:, :], s6[:, 2, :], s6[:, 5, :], ALU.add))
                line.step(v, v.tensor_tensor(T1[:, :], T1[:, :], T1[:, :], ALU.mult))
                line.mark(v.tensor_scalar(MEAN[:, :], MEAN[:, :], 0.5, None, ALU.mult))
                line.mark(v.tensor_scalar(T1[:, :], T1[:, :], 0.25, LN_EPS, ALU.mult, ALU.add))
                line.sync(v)
                v.scalar_tensor_tensor(VAR[:, :], T2[:, :], 1.0 / D, T1[:, :], ALU.mult, ALU.add).then_inc(sem("var"), 1)
                v.wait_ge(sem("std"), ORDER.index(st) + 1)
                line.step(v, v.reciprocal(RSTD[:, :], T1[:, :]))
                line.step(v, v.tensor_tensor(RSTD[:, :], RSTD[:, :], MASK[:, :], ALU.mult))
                line.step(v, v.scalar_tensor_tensor(NMR[:, :], MEAN[:, :], -1.0, RSTD[:, :], ALU.mult, ALU.mult))
                line.step(v, v.tensor_scalar(ONEP[:, :], RSTD[:, :], 1.0, None, ALU.add))

            def ln_apply(st, c, j, keep):
                t = c * CH + j
                v.wait_ge(sem("tp"), tiles_before(st) + AHEAD + t + 1 - CH)
                v.tensor_scalar(XS[:, j * D:(j + 1) * D], tile(X, t), MEAN[:, ds(t, 1)], RSTD[:, ds(t, 1)],
                                ALU.subtract, ALU.mult).then_inc(sem("xs"), 1)
                if keep:
                    line.mark(v.tensor_scalar(tile(X, t), tile(X, t), ONEP[:, ds(t, 1)], NMR[:, ds(t, 1)], ALU.mult, ALU.add))

            def attention_columns(dst, left, right, w, done):
                for b in range(KB):
                    for k, vec in ((0, left), (1, right)):
                        line.step(v, v.tensor_tensor(TMP[:, 0:D], WG[:, b * GW:b * GW + D], vec, ALU.mult))
                        line.step(v, v.tensor_reduce(dst(b, k), TMP[:, 0:D].rearrange("p (h d) -> p h d", h=w), AX.X, ALU.add))
                v.sem_inc(sem(done), 1)

            v.wait_ge(sem("ld_x"), 32)
            v.wait_ge(sem("x_padded"), 1)
            ln_stats("g0")
            v.wait_ge(sem("ld_w0"), 16 * 3)
            attention_columns(lambda b, k: WG[:, b * GW + D + 4 * k:b * GW + D + 4 * k + 4], CSTB[:, 0:D], CSTB[:, D:2 * D], 4, "g0_weights")

            def project(st, width, scaled):
                with v.Fori(0, NC) as c:
                    for j in range(CH):
                        ln_apply(st, c, j, False)
                    for j in range(CH):
                        t = c * CH + j
                        v.wait_ge(sem(f"{st}_mm"), AHEAD + t + 1)
                        if scaled:
                            ins = v.tensor_scalar(tile(ACC, t, width, ROW), PB[2 + j][:, 0:width], DINV[:, ds(t, 1)], None, ALU.mult)
                        else:
                            ins = v.tensor_copy(tile(ACC, t, min(width, ROW), ROW), PB[2 + j][:, 0:min(width, ROW)])
                            if width > ROW:
                                ins = v.tensor_copy(AD[:, ds(t * 8, 8)], PB[2 + j][:, ROW:width])
                        ins.then_inc(sem("rows"), 1)

            project("g0", ROW, False)
            v.wait_ge(sem("ld_dst"), 16)
            line.mark(v.tensor_scalar(dlo, dst2, P - 1, None, ALU.bitwise_and))
            line.step(v, v.tensor_scalar(dhi, dst2, 7, None, ALU.arith_shift_right))
            line.mark(v.tensor_copy(dlob, dlo))
            line.step(v, v.tensor_copy(dhib, dhi))
            v.wait_ge(sem("iotab"), 1)
            with v.Fori(0, ET // (2 * HB)) as i:
                for r in range(2):
                    v.wait_ge(sem("h_used"), i * 2 + r + 1)
                    v.tensor_tensor(ob[:, r * HB * P:(r + 1) * HB * P].rearrange("p (k n) -> p k n", k=HB),
                                    IOTAB[:, :].unsqueeze(1).to_broadcast([P, HB, P]),
                                    dlob[:, ds(i * 2 * HB + r * HB, HB)].unsqueeze(2).to_broadcast([P, HB, P]), ALU.is_equal)
                    v.tensor_tensor(oa[:, r * HB * NT:(r + 1) * HB * NT].rearrange("p (k n) -> p k n", k=HB),
                                    IOTAB[:, 0:NT].unsqueeze(1).to_broadcast([P, HB, NT]),
                                    dhib[:, ds(i * 2 * HB + r * HB, HB)].unsqueeze(2).to_broadcast([P, HB, NT]),
                                    ALU.is_equal).then_inc(sem("h_onehot"), 1)
            v.wait_ge(sem("hist"), 1)
            v.tensor_copy(T1[:, :], PB[7][:, 0:NT]).then_inc(sem("hist_sb"), 1)
            v.wait_ge(sem("hist_sb"), 1)
            line.step(v, v.tensor_scalar(T2[:, :], T1[:, :], 1.0, None, ALU.add))
            v.reciprocal(VAR[:, :], T2[:, :]).then_inc(sem("deg"), 1)
            v.wait_ge(sem("totals"), 1)
            line.step(v, v.tensor_copy(SMALL[:, 0:NT], PB[6][:, 0:NT]))
            line.step(v, v.tensor_tensor_scan(SMALL[:, 32:32 + NT], SMALL[:, 0:NT], SMALL[:, 0:NT], 0.0, ALU.add, ALU.bypass))
            line.step(v, v.tensor_copy(SMALL[:, 64:64 + NT].bitcast(I32), SMALL[:, 32:32 + NT]))
            line.step(v, v.tensor_scalar(SMALL[:, 96:96 + NT].bitcast(I32), SMALL[:, 64:64 + NT].bitcast(I32), 7, None, ALU.arith_shift_right))
            line.step(v, v.tensor_copy(SMALL[:, 128:128 + NT], SMALL[:, 96:96 + NT].bitcast(I32)))
            line.step(v, v.scalar_tensor_tensor(SMALL[:, 160:160 + NT - 1], IOTA[:, 0:NT - 1], 1.0, SMALL[:, 128:128 + NT - 1], ALU.add, ALU.add))
            rank = SMALL[:, 160:160 + NT - 1].unsqueeze(1).to_broadcast([P, 4, NT - 1])
            le = SMALL[:, 200:200 + 4 * (NT - 1)].rearrange("p (k w) -> p k w", k=4)
            line.step(v, v.tensor_tensor(le, rank, IOTAP[:, :].unsqueeze(2).to_broadcast([P, 4, NT - 1]), ALU.is_le))
            line.step(v, v.tensor_reduce(SLF[:, 0:4], le, AX.X, ALU.add))
            line.step(v, v.tensor_tensor(SLF[:, 8:12], IOTAP[:, :], SLF[:, 0:4], ALU.subtract))
            line.step(v, v.tensor_scalar(SLF[:, 8:12], SLF[:, 8:12], float(ET - 1), None, ALU.min))
            v.tensor_copy(SLI[:, :], SLF[:, 8:12]).then_inc(sem("slot_tile"), 1)
            line.mark(v.tensor_scalar(SLF[:, 4:8], SLF[:, 0:4], float(ROW), None, ALU.mult))
            line.step(v, v.tensor_scalar(SLF[:, 0:4], SLF[:, 0:4], float(P), None, ALU.mult))
            v.wait_ge(sem("ld_slots"), 8 * 16)
            line.mark(v.tensor_copy(slot_srcf, slot_src))
            line.step(v, v.tensor_copy(slot_dstf, slot_dst))
            for k in range(4):
                ins = v.tensor_scalar(slot_dstf[:, k * P:(k + 1) * P], slot_dstf[:, k * P:(k + 1) * P], SLF[:, k:k + 1], None, ALU.subtract)
            ins.then_inc(sem("slot_rows"), 1)
            v.wait_ge(sem("slotsT"), 1)
            v.tensor_copy(SRCI[:, 0:SLOTS], PB[4][:, 0:SLOTS])
            v.tensor_copy(DREL[:, 0:SLOTS], PB[5][:, 0:SLOTS])
            v.memset(SRCI[:, SLOTS:], 0)
            v.memset(DREL[:, SLOTS:], -1.0)
            v.tensor_copy(WROW[:, :], PB[6][0:1, 0:512]).then_inc(sem("slots_ready"), 1)
            v.wait_ge(sem("slots_ready"), 1)

            v.wait_ge(sem("g0_gathered"), 16 * 2 * NT)
            heads = lambda buf: buf.rearrange("p (t c) -> p t c", c=ROW)
            al = ADS[:, 0:4 * NT].rearrange("p (t h) -> p t h", h=4)
            z2 = SMALL[:, 200:200 + 4 * NT].rearrange("p (t h) -> p t h", h=4)
            line.step(v, v.tensor_tensor(al, heads(ACC[:, :])[:, :, D:D + 4], heads(BIG[:, 0:NT * ROW])[:, :, D + 4:D + 8], ALU.add))
            line.step(v, v.tensor_scalar(z2, al, 0.01, None, ALU.mult))
            line.step(v, v.tensor_tensor(al, al, z2, ALU.max))
            line.step(v, v.tensor_reduce(T1[:, :], al, AX.X, ALU.max))
            v.tensor_tensor(al, al, T1[:, :].unsqueeze(2).to_broadcast([P, NT, 4]), ALU.subtract).then_inc(sem("g0_logit"), 1)
            v.wait_ge(sem("g0_exp"), 1)
            line.step(v, v.tensor_reduce(T1[:, :], al, AX.X, ALU.add))
            line.step(v, v.reciprocal(T2[:, :], T1[:, :]))
            line.step(v, v.tensor_tensor(T2[:, :], T2[:, :], MASK[:, :], ALU.mult))
            line.step(v, v.tensor_tensor(al, al, T2[:, :].unsqueeze(2).to_broadcast([P, NT, 4]), ALU.mult))
            per = 3
            byhead = lambda buf, h: buf.rearrange("p t (h d) -> p t h d", h=h)
            with v.Fori(0, NC) as c:
                line.enter(c, per)
                XS4 = byhead(XS[:, :].rearrange("p (t c) -> p t c", t=CH), 4)
                XC4 = byhead(chunk(X, c), 4)
                mean4 = TMP[:, 0:CH * 64].rearrange("p (t d) -> p t d", t=CH)
                line.step(v, v.tensor_tensor(XS4, byhead(chunk(BIG, c, D, ROW), 4),
                                             ADS[:, ds(c * CH * 4, CH * 4)].rearrange("p (t h) -> p t h", h=4).unsqueeze(3).to_broadcast([P, CH, 4, 64]), ALU.mult))
                line.step(v, v.tensor_reduce(mean4, XS4.rearrange("p t h d -> p t d h"), AX.X, ALU.add))
                line.step(v, v.tensor_tensor(XC4, XC4, mean4.unsqueeze(2).to_broadcast([P, CH, 4, 64]), ALU.add))
                chunk_stats(c)
            line.leave(NC, per)

            moments("f0")
            v.wait_ge(sem("ld_f0"), 16 * 6)
            with v.Fori(0, NC) as c:
                line.enter(c, CH)
                for j in range(CH):
                    t = c * CH + j
                    line.mark(v.scalar_tensor_tensor(XS[:, j * D:(j + 1) * D], tile(X, t), MEAN[:, ds(t, 1)], CSTB[:, 3 * D:4 * D], ALU.subtract, ALU.mult,
                                                     accum_out=T1[:, ds(t, 1)]))
                line.sync(v)
            line.leave(NC, CH)
            line.step(v, v.tensor_tensor(T1[:, :], T1[:, :], RSTD[:, :], ALU.mult))
            line.mark(v.tensor_scalar(T2[:, :], MASK[:, :], BIG_NUM, -BIG_NUM, ALU.mult, ALU.add))
            line.step(v, v.tensor_scalar(T1[:, :], T1[:, :], SLF[:, 15:16], None, ALU.add))
            v.tensor_tensor(COEF[:, :], T1[:, :], T2[:, :], ALU.add).then_inc(sem("f0_score"), 1)
            SC = SMALL[:, 400:400 + 3 * NT]
            line.step(v, v.memset(SC, 0.0))
            NODE_SCORE = SMALL[:, 500:500 + NT]
            line.step(v, v.tensor_copy(NODE_SCORE, COEF[:, :]))

            def coefficients(c):
                for t in range(c * CH, (c + 1) * CH):
                    score = NODE_SCORE[:, t:t + 1]
                    line.mark(v.tensor_scalar(JUNK[:, t * P:NT * P], RANKROW[:, t * P:NT * P], score, 0.0, ALU.is_gt, ALU.add, accum_out=SC[:, t:t + 1]))
                    if t:
                        line.mark(v.tensor_scalar(JUNK[:, 0:t * P], RANKROW[:, 0:t * P], score, 0.0, ALU.is_ge, ALU.add, accum_out=SC[:, NT + t:NT + t + 1]))
                    line.step(v, v.scalar_tensor_tensor(OH[:, 0:P], RANKROW[:, t * P:(t + 1) * P], score, LOWER[:, :], ALU.is_equal, ALU.mult,
                                                        accum_out=SC[:, 2 * NT + t:2 * NT + t + 1]))
                cs = slice(c * CH, (c + 1) * CH)
                line.step(v, v.tensor_tensor(T1[:, cs], SC[:, 0:NT][:, cs], SC[:, NT:2 * NT][:, cs], ALU.add))
                line.step(v, v.tensor_tensor(T1[:, cs], T1[:, cs], SC[:, 2 * NT:3 * NT][:, cs], ALU.add))
                line.step(v, v.tensor_scalar(T1[:, cs], T1[:, cs], float(KSEL), None, ALU.is_lt))
                line.step(v, v.tensor_tensor(COEF[:, cs], T1[:, cs], NODE_SCORE[:, cs], ALU.mult))
            v.sem_inc(sem("f0_out"), AHEAD)
            for j in range(CH):
                ln_apply("f0", 0, j, True)
            for c in range(NC):
                if c + 1 < NC:
                    for j in range(CH):
                        ln_apply("f0", c + 1, j, True)
                if c == 0:
                    v.wait_ge(sem("f0_rankrow"), 16)
                coefficients(c)
                for j in range(CH):
                    t = c * CH + j
                    v.wait_ge(sem("f0_y"), t + 1)
                    v.tensor_tensor(TMP[:, (j % 2) * D:(j % 2 + 1) * D], PB[6 + j % 2][:, 0:D], CSTB[:, 2 * D:3 * D], ALU.add).then_inc(sem("f0_out"), 1)
                    v.wait_ge(sem("f0_out"), AHEAD + t + 1)
                    line.step(v, v.scalar_tensor_tensor(tile(X, t), TMP[:, (j % 2) * D:(j % 2 + 1) * D], COEF[:, t:t + 1], tile(X, t), ALU.mult, ALU.add))
                chunk_stats(c)

            def sum_slots(st, width):
                v.sem_inc(sem(f"{st}_acc"), BODY)

                def onehot(half, first):
                    v.tensor_tensor(OH[:, half * GRP * P:(half + 1) * GRP * P].rearrange("p (k n) -> p k n", k=GRP),
                                    IOTA[:, :].unsqueeze(1).to_broadcast([P, GRP, P]),
                                    DREL[:, ds(first, GRP)].unsqueeze(2).to_broadcast([P, GRP, P]), ALU.is_equal).then_inc(sem(f"{st}_oh"), 1)
                onehot(0, 0)
                regs = [v.alloc_register(f"{st}_row{k}") for k in range(GRP)]
                with v.Fori(0, TURNS) as i:
                    for q in range(NG):
                        n0 = i * BODY + q * GRP
                        v.wait_ge(sem(f"{st}_mm"), BODY + n0)
                        onehot((q + 1) % 2, n0 + GRP)
                        v.load(regs, WROW[0:1, ds(n0, GRP)])
                        for k in range(GRP):
                            row = v.snap(regs[k], min_val=0, max_val=(NT - 1) * ROW)
                            v.wait_ge(sem(f"{st}_mm"), BODY + n0 + k + 1)
                            v.wait_ge(sem(f"{st}_acc"), BODY + n0 + k)
                            dst = ACC[:, ds(row, width)]
                            v.tensor_tensor(dst, dst, PB[k][:, 0:width], ALU.add).then_inc(sem(f"{st}_acc"), 1)
                v.wait_ge(sem(f"{st}_acc"), BODY + SLOTS)
                for r in regs:
                    v.free_register(r)

            def gcn(st, sums, bias):
                moments(st)
                project(st, D, True)
                v.wait_ge(sem("table_stored"), (GNNS.index(st) + 1) * NC * 16)
                v.wait_ge(sem("rows"), rows_before(st) + AHEAD + NT)
                sum_slots(sums, D)
                per = CH + 1
                v.wait_ge(sem("ld_bias"), 16 * 5)
                with v.Fori(0, NC) as c:
                    line.enter(c, per)
                    for j in range(CH):
                        t = c * CH + j
                        line.mark(v.scalar_tensor_tensor(XS[:, j * D:(j + 1) * D], tile(ACC, t, D, ROW), DINV[:, ds(t, 1)], bias, ALU.mult, ALU.add))
                    line.sync(v)
                    line.step(v, v.scalar_tensor_tensor(chunk(X, c), XS[:, :].rearrange("p (t c) -> p t c", t=CH), 0.0, chunk(X, c), ALU.max, ALU.add))
                    chunk_stats(c)
                line.leave(NC, per)

            gcn("g1", "a1", CSTB[:, 4 * D:5 * D])

            st = "t1"
            moments(st)
            v.wait_ge(sem("ld_t1"), 16 * 12)
            line.mark(v.tensor_copy(BXR.rearrange("p (h n) -> p h n", h=8), BX.unsqueeze(2).to_broadcast([64, 8, P])))
            line.mark(v.memset(TMP[:, 0:512], 0.0))
            line.mark(v.memset(WSUM, 0.0))
            line.step(v, v.tensor_scalar(TEMPC, TEMPC, 0.1, 5.0, ALU.max, ALU.min))
            v.reciprocal(RTEMP, TEMPC).then_inc(sem(f"{st}_bxr"), 1)
            v.wait_ge(sem(f"{st}_bxr"), 1)
            v.wait_ge(sem(f"{st}_wxs"), 1)
            g8 = lambda buf: buf.rearrange("p (h g) -> p h g", h=8)
            rt = RTEMP.unsqueeze(2).to_broadcast([P, 8, 64])
            line.mark(v.tensor_tensor(g8(WXS[:, 0:512]), g8(PB[0][:, :]), rt, ALU.mult))
            line.mark(v.tensor_tensor(g8(WXS[:, 512:1024]), g8(PB[1][:, :]), rt, ALU.mult))
            line.step(v, v.tensor_tensor(g8(LBIAS), g8(PB[2][:, :]), BSL.unsqueeze(1).to_broadcast([P, 8, 64]), ALU.add))
            v.tensor_tensor(g8(LBIAS), g8(LBIAS), rt, ALU.mult).then_inc(sem(f"{st}_fold"), 1)
            v.wait_ge(sem(f"{st}_fold"), 1)
            v.sem_inc(sem(f"{st}_lgc"), AHEAD)
            per = 4 * CH
            with v.Fori(0, NC) as c:
                line.enter(c, per)
                for j in range(CH):
                    v.wait_ge(sem(f"{st}_tok"), AHEAD + c * CH + j + 1 - CH)
                    ln_apply(st, c, j, False)

                def shift(j):
                    n = c * CH + j
                    w = SW[:, j * 512:(j + 1) * 512]
                    v.wait_ge(sem(f"{st}_lg"), AHEAD + n + 1)
                    v.tensor_tensor(w, PB[2 + j % 2][:, :], LBIAS, ALU.add).then_inc(sem(f"{st}_lgc"), 1)
                    v.wait_ge(sem(f"{st}_lgc"), AHEAD + n + 1)
                    line.step(v, v.tensor_reduce(SMALL[:, j * 8:j * 8 + 8], g8(w), AX.X, ALU.max))
                    v.tensor_tensor(g8(w), g8(w), SMALL[:, j * 8:j * 8 + 8].unsqueeze(2).to_broadcast([P, 8, 64]), ALU.subtract).then_inc(sem(f"{st}_sub"), 1)

                def normalise(j):
                    n = c * CH + j
                    w = SW[:, j * 512:(j + 1) * 512]
                    sm = SMALL[:, 64 + j * 8:64 + j * 8 + 8]
                    v.wait_ge(sem(f"{st}_exp"), n + 1)
                    line.step(v, v.tensor_reduce(sm, g8(w), AX.X, ALU.add))
                    line.step(v, v.reciprocal(sm, sm))
                    v.tensor_scalar(sm, sm, MASK[:, ds(n, 1)], None, ALU.mult).then_inc(sem(f"{st}_rs"), 1)
                    v.wait_ge(sem(f"{st}_rs"), n + 1)
                    v.tensor_tensor(g8(w), g8(w), sm.unsqueeze(2).to_broadcast([P, 8, 64]), ALU.mult).then_inc(sem(f"{st}_sw"), 1)
                    v.wait_ge(sem(f"{st}_sw"), n + 1)
                    line.step(v, v.tensor_tensor(WSUM, WSUM, w, ALU.add))
                shift(0)
                for j in range(1, CH):
                    shift(j)
                    normalise(j - 1)
                normalise(CH - 1)
            line.leave(NC, per)
            line.sync(v)
            v.sem_inc(sem(f"{st}_wsum"), 1)
            v.wait_ge(sem(f"{st}_sums"), 1)
            line.mark(v.tensor_copy(TOKT[:, 0:512], PB[4][:, :]))
            line.mark(v.tensor_copy(TOKT[:, 512:1024], PB[5][:, :]))
            line.step(v, v.tensor_copy(NORM, PB[6][0:1, :]))
            line.step(v, v.tensor_scalar(RN, NORM, 1e-5, None, ALU.add))
            v.reciprocal(RN, RN).then_inc(sem(f"{st}_norm"), 1)
            v.wait_ge(sem(f"{st}_tokens"), 1)
            line.step(v, v.tensor_copy(RNB, PB[1][0:64, :]))
            v.tensor_tensor(TOK, PB[0][0:64, :], RNB, ALU.mult).then_inc(sem(f"{st}_token"), 1)
            v.wait_ge(sem(f"{st}_qkv"), 1)
            line.mark(v.tensor_copy(QT, PB[2][0:64, :]))
            line.step(v, v.tensor_copy(KT, PB[3][0:64, :]))
            v.tensor_copy(VT, PB[4][0:64, :]).then_inc(sem(f"{st}_qkvc"), 1)
            v.wait_ge(sem(f"{st}_att"), 1)
            sm = SMALL[0:64, 0:8]
            smb = sm.unsqueeze(2).to_broadcast([64, 8, 64])
            line.step(v, v.tensor_reduce(sm, g8(PB[5][0:64, :]), AX.X, ALU.max))
            v.tensor_tensor(g8(ATT), g8(PB[5][0:64, :]), smb, ALU.subtract).then_inc(sem(f"{st}_sub2"), 1)
            v.wait_ge(sem(f"{st}_vw"), 1)
            for k in range(4):
                line.mark(v.tensor_copy(VW[:, k * 512:(k + 1) * 512], PB[k][0:64, :]))
            v.wait_ge(sem(f"{st}_exp2"), 1)
            line.step(v, v.tensor_reduce(sm, g8(ATT), AX.X, ALU.add))
            line.step(v, v.reciprocal(sm, sm))
            v.tensor_tensor(g8(ATT), g8(ATT), smb, ALU.mult).then_inc(sem(f"{st}_soft"), 1)
            v.wait_ge(sem(f"{st}_attT"), 1)
            v.tensor_copy(ATTT, PB[6][0:64, :]).then_inc(sem(f"{st}_attc"), 1)
            v.wait_ge(sem(f"{st}_m"), 1)
            for k in range(4):
                line.mark(v.tensor_copy(MM[0:64, k * D:(k + 1) * D], PB[k][0:64, 0:D]))
                ins = v.tensor_copy(MO[:, k * D:(k + 1) * D], PB[k][0:64, D:2 * D])
            ins.then_inc(sem(f"{st}_mout"), 1)
            v.sem_inc(sem(f"{st}_out"), AHEAD)
            with v.Fori(0, NC) as c:
                for j in range(CH):
                    n = c * CH + j
                    v.wait_ge(sem(f"{st}_y"), AHEAD + n + 1)
                    v.tensor_tensor(tile(X, n), tile(X, n), PB[4 + j % 2][:, 0:D], ALU.add).then_inc(sem(f"{st}_out"), 1)
                v.wait_ge(sem(f"{st}_out"), AHEAD + (c + 1) * CH)
                chunk_stats(c)
            v.wait_ge(sem(f"{st}_out"), AHEAD + NT)

            gcn("g2", "a2", CSTB[:, 5 * D:6 * D])

            def first_of(row, best, onehot, tmp, n):
                r8 = lambda buf: buf.rearrange("p (n e) -> p n e", e=8)
                wide = lambda buf: buf.unsqueeze(2).to_broadcast([P, n, 8])
                iota8 = IOTA[:, 0:8].unsqueeze(1).to_broadcast([P, n, 8])
                line.step(v, v.tensor_reduce(best, r8(row), AX.X, ALU.max))
                line.step(v, v.tensor_tensor(r8(tmp), r8(row), wide(best), ALU.is_lt))
                line.step(v, v.scalar_tensor_tensor(r8(tmp), r8(tmp), 8.0, iota8, ALU.mult, ALU.add))
                line.step(v, v.tensor_reduce(onehot[:, 0:n], r8(tmp), AX.X, ALU.min))
                line.step(v, v.tensor_tensor(r8(tmp), iota8, wide(onehot[:, 0:n]), ALU.is_equal))
                line.step(v, v.tensor_copy(onehot, tmp))

            st = "m2"
            line.step(v, v.memset(COMBW, 0.0))
            v.memset(ACC[:, 0:CH * D], 0.0).then_inc(sem(f"{st}_b2zero"), 1)
            moments(st)
            v.wait_ge(sem("ld_m2"), 16 * 9)
            v.sem_inc(sem(f"{st}_out"), AHEAD)
            v.sem_inc(sem(f"{st}_b2"), AHEAD)
            r8 = lambda buf: buf.rearrange("p (n e) -> p n e", e=8)
            wide = lambda buf: buf.unsqueeze(2).to_broadcast([P, CH, 8])
            BEST, TOT, BEST2 = SMALL[:, 64:64 + CH], SMALL[:, 72:72 + CH], SMALL[:, 80:80 + CH]
            F1, F2, W8 = SMALL[:, 120:160], SMALL[:, 160:200], SMALL[:, 200:240]
            PROB = SMALL[:, 240:280]
            per = CH + 22
            for j in range(CH):
                ln_apply(st, 0, j, True)

            def body(c, more):
                if more:
                    for j in range(CH):
                        ln_apply(st, c + 1, j, True)
                v.wait_ge(sem(f"{st}_logits"), c + 1)
                line.step(v, v.tensor_reduce(BEST, r8(PB[1][:, 0:8 * CH]), AX.X, ALU.max))
                v.tensor_tensor(r8(COMB), r8(PB[1][:, 0:8 * CH]), wide(BEST), ALU.subtract).then_inc(sem(f"{st}_sub"), 1)
                v.wait_ge(sem(f"{st}_exp"), c + 1)
                line.step(v, v.tensor_reduce(TOT, r8(COMB), AX.X, ALU.add))
                line.step(v, v.reciprocal(TOT, TOT))
                line.step(v, v.tensor_tensor(r8(PROB), r8(COMB), wide(TOT), ALU.mult))
                first_of(PROB, BEST, F1, W8, CH)
                line.step(v, v.scalar_tensor_tensor(COMB, F1, -2.0, PROB, ALU.mult, ALU.add))
                first_of(COMB, BEST2, F2, W8, CH)
                line.step(v, v.tensor_tensor(TOT, BEST, BEST2, ALU.add))
                line.step(v, v.tensor_scalar(TOT, TOT, 1e-12, None, ALU.max))
                line.step(v, v.reciprocal(TOT, TOT))
                line.step(v, v.tensor_tensor(F1, F1, F2, ALU.add))
                line.step(v, v.tensor_tensor(F1, F1, PROB, ALU.mult))
                v.tensor_tensor(r8(COMB), r8(F1), wide(TOT), ALU.mult).then_inc(sem(f"{st}_comb"), 1)
                v.wait_ge(sem(f"{st}_comb"), c + 1)
                for e in range(8):
                    if e == 7:
                        v.wait_ge(sem(f"{st}_combT"), c + 1)
                        v.tensor_copy(COMBT, PB[2][0:8 * CH, 0:P]).then_inc(sem(f"{st}_combTc"), 1)
                    for j in range(CH):
                        n = (c * 8 + e) * CH + j
                        v.wait_ge(sem(f"{st}_y"), n + 1)
                        v.wait_ge(sem(f"{st}_out"), AHEAD + n + 1 - CH)
                        v.scalar_tensor_tensor(tile(X, c * CH + j), PB[6 + (e * CH + j) % 2][:, 0:D], COMB[:, j * 8 + e:j * 8 + e + 1], tile(X, c * CH + j),
                                               ALU.mult, ALU.add).then_inc(sem(f"{st}_out"), 1)
                v.wait_ge(sem(f"{st}_b2y"), c + 1)
                v.wait_ge(sem(f"{st}_out"), AHEAD + (c + 1) * 8 * CH)
                for k in range(3):
                    w = min(512, CH * D - k * 512)
                    xx = X[:, ds(c * CH * D + k * 512, w)]
                    ins = v.tensor_tensor(xx, xx, PB[3 + k][:, 0:w], ALU.add)
                ins.then_inc(sem(f"{st}_b2"), 1)
                v.wait_ge(sem(f"{st}_b2"), AHEAD + c + 1)
                chunk_stats(c)
            with v.Fori(0, NC - 1) as c:
                line.enter(c, per)
                body(c, True)
            line.leave(NC - 1, per)
            body(NC - 1, False)
            line.sync(v)

            st = "g3"
            v.tensor_scalar(WHEAD[:, :], WROW[:, :], 255, None, ALU.bitwise_and).then_inc(sem(f"{st}_whead"), 1)
            moments(st)
            v.wait_ge(sem("ld_w3"), 16 * 3)
            attention_columns(lambda b, k: WG[:, b * GW + D + 8 * k:b * GW + D + 8 * k + 8], CSTB[:, 0:D], CSTB[:, D:2 * D], 8, "g3_weights")
            project(st, 272, False)
            v.wait_ge(sem("rows"), rows_before(st) + AHEAD + NT)
            UM = SMALL[:, 800:808]
            line.step(v, v.tensor_reduce(UM, ACC[:, :].rearrange("p (t c) -> p c t", c=ROW)[:, D:D + 8, :], AX.X, ALU.max))
            v.sem_inc(sem(f"{st}_umax"), 1)
            v.wait_ge(sem(f"{st}_uT"), 1)
            line.step(v, v.tensor_reduce(SMALL[0:8, 808:809], PB[0][0:8, 0:P], AX.X, ALU.max))
            v.tensor_scalar(SMALL[0:8, 816:824], IDENT[0:8, 0:8], SMALL[0:8, 808:809], None, ALU.mult).then_inc(sem(f"{st}_udiag"), 1)
            v.wait_ge(sem(f"{st}_u"), 1)
            line.step(v, v.tensor_copy(UM, PB[0][:, 0:8]))
            h8 = lambda buf: buf.rearrange("p (t h) -> p t h", h=8)
            a_dst, bound, slope = AD[:, 0:8 * NT], AD[:, 8 * NT:16 * NT], SMALL[:, 850:850 + 8 * NT]
            line.step(v, v.tensor_tensor(h8(bound), h8(a_dst), UM.unsqueeze(1).to_broadcast([P, NT, 8]), ALU.add))
            line.step(v, v.tensor_scalar(slope, bound, 0.2, None, ALU.mult))
            v.tensor_tensor(bound, bound, slope, ALU.max).then_inc(sem(f"{st}_ad"), 1)
            v.wait_ge(sem("table_stored"), (GNNS.index(st) + 1) * NC * 16)
            line.step(v, v.memset(ACC[:, :], 0.0))

            st = "a3"
            v.sem_inc(sem(f"{st}_acc"), BODY)
            r8 = lambda buf: buf.rearrange("p (k h) -> p k h", h=8)

            def onehot(r, first):
                v.tensor_tensor(OH4[:, r * GRP * P:(r + 1) * GRP * P].rearrange("p (k n) -> p k n", k=GRP),
                                IOTA[:, :].unsqueeze(1).to_broadcast([P, GRP, P]),
                                DREL[:, ds(first, GRP)].unsqueeze(2).to_broadcast([P, GRP, P]), ALU.is_equal).then_inc(sem(f"{st}_oh"), 1)

            def logits(g, r, gathered):
                v.wait_ge(sem(f"{st}_in{r}"), gathered)
                v.wait_ge(sem(f"{st}_ad"), g + 1)
                rows = G[:, r * GRP * ROW:(r + 1) * GRP * ROW].rearrange("p (k c) -> p k c", c=ROW)
                terms = PB[6 + r % 2][:, 0:16 * GRP].rearrange("p (k c) -> p k c", c=16)
                z, low = r8(TMP[:, (r % 2) * 64:(r % 2 + 1) * 64]), r8(TMP[:, 128:192])
                line.step(v, v.tensor_tensor(z, rows[:, :, D:D + 8], terms[:, :, 0:8], ALU.add))
                line.step(v, v.tensor_scalar(low, z, 0.2, None, ALU.mult))
                line.step(v, v.tensor_tensor(z, z, low, ALU.max))
                v.tensor_tensor(z, z, terms[:, :, 8:16], ALU.subtract).then_inc(sem(f"{st}_z"), 1)

            def scale(g, r, first, count):
                if first == 0:
                    v.wait_ge(sem(f"{st}_exp"), g + 1)
                for k in range(first, first + count):
                    row = G[:, (r * GRP + k) * ROW:(r * GRP + k + 1) * ROW]
                    chans = row[:, 0:D].rearrange("p (h d) -> p h d", h=8)
                    ins = v.tensor_tensor(chans, chans, row[:, D:D + 8].unsqueeze(2).to_broadcast([P, 8, 32]), ALU.mult)
                if first + count == GRP:
                    ins.then_inc(sem(f"{st}_scaled"), 1)

            for r in range(3):
                onehot(r, r * GRP)
            logits(0, 0, 16 * GRP)
            scale(0, 0, 0, GRP)
            regs = [v.alloc_register(f"{st}_row{k}") for k in range(GRP)]
            per = 3
            with v.Fori(0, TURNS) as i:
                line.enter(i, per * NG)
                for q in range(NG):
                    g = i * NG + q
                    n0 = i * BODY + q * GRP
                    v.wait_ge(sem(f"{st}_mm"), BODY + n0)
                    onehot((q + 3) % NG, n0 + 3 * GRP)
                    v.load(regs, WROW[0:1, ds(n0, GRP)])
                    for k in range(GRP):
                        if k == 2:
                            logits(g + 1, (q + 1) % NG, 16 * GRP * (i + 1 + (q + 1) // NG))
                        elif k > 3:
                            scale(g + 1, (q + 1) % NG, (k - 4) * 2, 2)
                        row = v.snap(regs[k], min_val=0, max_val=(NT - 1) * ROW)
                        v.wait_ge(sem(f"{st}_mm"), BODY + n0 + k + 1)
                        v.wait_ge(sem(f"{st}_acc"), BODY + n0 + k)
                        dst = ACC[:, ds(row, ROW)]
                        v.tensor_tensor(dst, dst, PB[k % 4][:, 0:ROW], ALU.add).then_inc(sem(f"{st}_acc"), 1)
            line.leave(TURNS, per * NG)
            v.wait_ge(sem(f"{st}_acc"), BODY + SLOTS)
            for r in regs:
                v.free_register(r)
            DEN = SMALL[:, 400:400 + 8 * NT]
            line.step(v, v.tensor_scalar(h8(DEN), ACC[:, :].rearrange("p (t c) -> p t c", c=ROW)[:, :, D:D + 8], 1e-16, None, ALU.add))
            line.step(v, v.reciprocal(DEN, DEN))
            per = 3
            with v.Fori(0, NC) as c:
                line.enter(c, per)
                XSC = XS[:, :].rearrange("p (t c) -> p t c", t=CH)
                line.step(v, v.tensor_tensor(byhead(XSC, 8), byhead(chunk(ACC, c, D, ROW), 8),
                                             DEN[:, ds(c * CH * 8, CH * 8)].rearrange("p (t h) -> p t h", h=8).unsqueeze(3).to_broadcast([P, CH, 8, 32]), ALU.mult))
                line.step(v, v.tensor_tensor(XSC, XSC, CSTB[:, 6 * D:7 * D].unsqueeze(1).to_broadcast([P, CH, D]), ALU.add))
                line.step(v, v.scalar_tensor_tensor(chunk(X, c), XSC, 0.0, chunk(X, c), ALU.max, ALU.add))
                chunk_stats(c)
            line.leave(NC, per)

            st = "f3"
            moments(st)
            line.sync(v)
            v.tensor_reduce(SMALL[:, 0:1], NMR[:, :], AX.X, ALU.add).then_inc(sem(f"{st}_stats"), 1)
            v.wait_ge(sem(f"{st}_mean"), 1)
            for b in range(KB):
                ins = v.tensor_scalar(OH[:, b * P:(b + 1) * P], ONES[:, :], PB[b][:, 0:1], 1.0 / N_NODES, ALU.mult, ALU.mult)
            ins.then_inc(sem(f"{st}_meanb"), 1)
            R, S1, P2 = SMALL[:, 16:24], SMALL[:, 24:25], SMALL[:, 32:40]
            v.wait_ge(sem(f"{st}_logits"), 1)
            v.wait_ge(sem("ld_wr"), 32)

            def softmax8(n):
                line.step(v, v.tensor_reduce(S1, R, AX.X, ALU.max))
                v.tensor_scalar(R, R, S1, None, ALU.subtract).then_inc(sem(f"{st}_sub"), 1)
                v.wait_ge(sem(f"{st}_exp"), n)
                line.step(v, v.tensor_reduce(S1, R, AX.X, ALU.add))
                line.step(v, v.reciprocal(S1, S1))
                line.step(v, v.tensor_scalar(R, R, S1, None, ALU.mult))
            line.step(v, v.tensor_tensor(R, PB[2][:, 0:8], BR, ALU.add))
            softmax8(1)
            line.step(v, v.tensor_scalar(P2, R, float(N_NODES), None, ALU.mult))
            line.step(v, v.reciprocal(P2, P2))
            line.step(v, v.tensor_scalar(P2, P2, CAP3, 1.0, ALU.mult, ALU.min))
            line.step(v, v.tensor_tensor(R, R, P2, ALU.mult))
            softmax8(2)
            B1_, B2_, F1, F2, W8 = SMALL[:, 40:41], SMALL[:, 41:42], SMALL[:, 64:72], SMALL[:, 72:80], SMALL[:, 80:88]
            first_of(R, B1_, F1, W8, 1)
            line.step(v, v.scalar_tensor_tensor(R, F1, -2.0, R, ALU.mult, ALU.add))
            first_of(R, B2_, F2, W8, 1)
            for k, F in ((0, F1), (1, F2)):
                line.step(v, v.tensor_tensor(W8, F, IOTA[:, 0:8], ALU.mult))
                line.step(v, v.tensor_reduce(SMALL[:, 42 + k:43 + k], W8, AX.X, ALU.add))
            v.tensor_copy(CHOSEN[:, :], SMALL[0:1, 42:44]).then_inc(sem(f"{st}_chosen"), 1)
            v.tensor_scalar(SMALL[:, 48:49], B2_, B1_, None, ALU.subtract).then_inc(sem(f"{st}_sub"), 1)
            v.wait_ge(sem(f"{st}_exp"), 3)
            line.step(v, v.tensor_scalar(SMALL[:, 49:50], SMALL[:, 48:49], 1.0, None, ALU.add))
            line.step(v, v.reciprocal(SMALL[:, 50:51], SMALL[:, 49:50]))
            line.step(v, v.tensor_tensor(SMALL[:, 51:52], SMALL[:, 48:49], SMALL[:, 50:51], ALU.mult))
            v.wait_ge(sem("ld_f3"), 16 * 8)
            for k in range(2):
                w = WB[:, k * 1024:(k + 1) * 1024]
                line.mark(v.tensor_scalar(w, w, SMALL[:, 50 + k:51 + k], None, ALU.mult))
            line.step(v, v.tensor_scalar(CSTB[:, 0:D], CSTB[:, 0:D], SMALL[:, 50:51], None, ALU.mult))
            v.scalar_tensor_tensor(CSTB[:, 0:D], CSTB[:, D:2 * D], SMALL[:, 51:52], CSTB[:, 0:D], ALU.mult, ALU.add).then_inc(sem(f"{st}_weights"), 1)
            v.wait_ge(sem(f"{st}_weights"), 1)
            v.sem_inc(sem(f"{st}_out"), AHEAD)
            for j in range(CH):
                ln_apply(st, 0, j, False)
            per = CH

            def body(c, more):
                v.wait_ge(sem("xs"), tiles_before(st) + c * CH + CH)
                for j in range(CH):
                    line.mark(v.tensor_tensor(tile(ACC, c * CH + j, D, ROW), XS[:, j * D:(j + 1) * D], CSTB[:, 0:D], ALU.add))
                line.sync(v)
                if more:
                    for j in range(CH):
                        ln_apply(st, c + 1, j, False)
                for j in range(CH):
                    t = c * CH + j
                    o = tile(ACC, t, D, ROW)
                    v.wait_ge(sem(f"{st}_y"), t + 1)
                    v.tensor_tensor(o, PB[6 + j % 2][:, 0:D], o, ALU.add).then_inc(sem(f"{st}_out"), 1)
                    v.wait_ge(sem(f"{st}_out"), AHEAD + t + 1)
                    v.bn_stats(tile(ST6, t, 6, 6), o).then_inc(sem("bn"), 1)
            with v.Fori(0, NC - 1) as c:
                line.enter(c, per)
                body(c, True)
            line.leave(NC - 1, per)
            body(NC - 1, False)
            moments("n3")
            per = CH + 2
            with v.Fori(0, NC) as c:
                line.enter(c, per)
                XSC = XS[:, :].rearrange("p (t c) -> p t c", t=CH)
                wide = lambda n: CSTB[:, n * D:(n + 1) * D].unsqueeze(1).to_broadcast([P, CH, D])
                for j in range(CH):
                    t = c * CH + j
                    line.mark(v.tensor_scalar(XS[:, j * D:(j + 1) * D], tile(ACC, t, D, ROW), MEAN[:, ds(t, 1)], RSTD[:, ds(t, 1)], ALU.subtract, ALU.mult))
                line.sync(v)
                line.step(v, v.tensor_tensor(XSC, XSC, wide(7), ALU.mult))
                line.step(v, v.tensor_tensor(XSC, XSC, wide(8), ALU.add))
                v.tensor_tensor(chunk(X, c), chunk(X, c), XSC, ALU.add).then_inc(sem("finished"), 1)
                v.wait_ge(sem("finished"), c + 1)
            line.leave(NC, per)




def kernel(**inputs):
    import numpy as _np
    import concourse.bacc as _bacc
    from concourse import mybir as _mybir
    from concourse.bass_utils import run_bass_kernel_spmd as _run

    nc = _bacc.Bacc("TRN2", target_bir_lowering=False, num_devices=1)
    pad = ET * P - N_EDGES
    laid = dict(inputs)
    laid["src"] = _np.concatenate([inputs["src"], _np.zeros(pad, _np.int32)])
    laid["dst"] = _np.concatenate([inputs["dst"], _np.full(pad, 4095, _np.int32)])
    laid["L1_ffn_W_xT"] = _np.transpose(inputs["L1_ffn_W_x"])
    laid["L2_ffn_router_wT"] = _np.transpose(inputs["L2_ffn_router_w"])
    arrays, args = {}, {}
    for name in laid:
        x = _np.ascontiguousarray(laid[name])
        arrays[f"in_{name}"] = x
        args[name] = nc.dram_tensor(f"in_{name}", x.shape, _mybir.dt.from_np(x.dtype), kind="ExternalInput").ap()
    out = nc.dram_tensor("out_0", (N_NODES, D), F32, kind="ExternalOutput").ap()
    build(nc, args, out)
    r = _run(nc, [arrays], core_ids=[0])
    return r.results[0]["out_0"]
```

```python
import concourse.bass as bass
from concourse import mybir
from contextlib import ExitStack

F32 = mybir.dt.float32
I32 = mybir.dt.int32
BF16 = mybir.dt.bfloat16
ALU = mybir.AluOpType
ACT = mybir.ActivationFunctionType
AX = mybir.AxisListType
ds = bass.ds

P = 128
D = 256
KB = D // P
N_NODES = 3125
N_EDGES = 50000
NT = (N_NODES + P - 1) // P
REST = N_NODES - (NT - 1) * P
CH = 5
NC = NT // CH
CW = CH * P
HALF = CW // 2
ROW = 264
ET = 392
SLOTS = 416
GRP = 8
NG = 4
BODY = GRP * NG
TG = 6
RING = TG * GRP
TURNS = SLOTS // BODY
T_GROUPS = ET // GRP
S_GROUPS = SLOTS // GRP
LN_EPS = 1e-5
KSEL = 1561
CAP3 = float(-(-N_NODES * 5 // 4 // 8))
ORDER = ("g0", "f0", "g1", "t1", "g2", "m2", "g3", "f3", "n3")
GNNS = ("g0", "g1", "g2", "g3")
BIG_NUM = 3.0e38
AHEAD = 5


def tiles_before(st):
    return NT * ORDER.index(st)


def groups_at(q):
    return (T_GROUPS - q + TG - 1) // TG


def rows_before(st):
    return NT * GNNS.index(st)


class Chain:

    def __init__(self, sem):
        self.sem, self.done, self.turn = sem, 0, 0

    def mark(self, ins):
        ins.then_inc(self.sem, 1)
        self.done += 1

    def sync(self, eng):
        eng.wait_ge(self.sem, self.turn + self.done)

    def step(self, eng, ins):
        self.mark(ins)
        self.sync(eng)

    def enter(self, i, per):
        self.turn, self.first = i * per, self.done

    def leave(self, n, per):
        assert self.done - self.first == per, (self.done - self.first, per)
        self.done, self.turn = self.first + n * per, 0


def build(nc, a, out):
    ctx = ExitStack()
    with ctx:
        def sb(name, shape, dt=F32):
            return ctx.enter_context(nc.sbuf_tensor(name, shape, dt))

        sems = {}

        def sem(name):
            if name not in sems:
                sems[name] = ctx.enter_context(nc.semaphore(name))
            return sems[name]

        X = sb("X", [P, NT * D])
        ACC = sb("ACC", [P, NT * ROW])
        BIG = sb("BIG", [P, 12800])
        XS = sb("XS", [P, CH * D])
        XT = sb("XT", [P, KB * CW])
        WA = sb("WA", [P, 4096])
        WB = sb("WB", [P, 4096])
        WG = sb("WG", [P, KB * 272])
        SW = sb("SW", [P, CH * 512])
        OH = sb("OH", [P, 2 * GRP * P])
        SRCI = sb("SRCI", [P, SLOTS + GRP * NG], I32)
        DREL = sb("DREL", [P, SLOTS + GRP * NG])
        IDX = sb("IDX", [P, TG * GRP], I32)
        WROW = sb("WROW", [1, 512], I32)
        TROW = sb("TROW", [1, 512], I32)
        IDENT = sb("IDENT", [P, P])
        ONES = sb("ONES", [P, P])
        IOTA = sb("IOTA", [P, P])
        IOTAB = sb("IOTAB", [P, P], BF16)
        ZEROB = sb("ZEROB", [P, NT], BF16)
        IOTAP = sb("IOTAP", [P, 4])
        LOWER = sb("LOWER", [P, P])
        MASK = sb("MASK", [P, NT])
        ST6 = sb("ST6", [P, NT * 6])
        MEAN = sb("MEAN", [P, NT])
        VAR = sb("VAR", [P, NT])
        RSTD = sb("RSTD", [P, NT])
        NMR = sb("NMR", [P, NT])
        ONEP = sb("ONEP", [P, NT])
        T1 = sb("T1", [P, NT])
        T2 = sb("T2", [P, NT])
        DINV = sb("DINV", [P, NT])
        DEG = sb("DEG", [P, NT])
        SMALL = sb("SMALL", [P, 6 * 200])
        IDN = sb("IDN", [P, 2 * NT], I32)
        SLI = sb("SLI", [P, 4], I32)
        SLF = sb("SLF", [P, 16])
        TMP = sb("TMP", [P, 2 * ROW])
        COEF = sb("COEF", [P, NT])
        CSTB = sb("CSTB", [P, 13 * D])
        B1 = sb("B1", [P, 16])
        PB = [ctx.enter_context(nc.psum_tensor(f"PB{i}", [P, 512], F32)) for i in range(8)]

        table = nc.dram_tensor("table", (NT * P, ROW), F32, kind="Internal").ap()
        wtab = nc.dram_tensor("wtab", (1, NT * P), F32, kind="Internal").ap()

        G = BIG[:, 0:BODY * ROW]
        GT = BIG[:, 0:RING * ROW]
        TSRC = CSTB[:, 0:ET + GRP].bitcast(I32)
        tile_src = SW[:, 2048:2560].bitcast(I32)
        tile_srcf = SW[:, 0:512]
        RANKROW = BIG[:, 5120:5120 + NT * P]
        JUNK = BIG[:, 5120 + NT * P:5120 + 2 * NT * P]
        HT = BIG[:, 0:8 * CW]
        dst2 = SW[:, 0:ET].bitcast(I32)
        dlo = SW[:, ET:2 * ET].bitcast(I32)
        dhi = SW[:, 2 * ET:3 * ET].bitcast(I32)
        dlob = SW[:, 3 * ET:3 * ET + ET // 2].bitcast(BF16)
        dhib = SW[:, 4 * ET:4 * ET + ET // 2].bitcast(BF16)
        HB = 7
        H_TURNS = ET // (2 * HB)
        H_EARLY = 8
        ob = OH[:, 0:HB * P].bitcast(BF16)
        oa = TMP[:, 0:HB * NT].bitcast(BF16)
        slot_src = SW[:, 0:512].bitcast(I32)
        slot_dst = SW[:, 512:1024].bitcast(I32)
        slot_srcf = SW[:, 1024:1536]
        slot_dstf = SW[:, 1536:2048]
        ADS = SMALL[:, 0:200]

        def tile(buf, t, w=D, stride=D):
            return buf[:, ds(t * stride, w)]

        GW = 272
        WXS, WFX = WA[:, 0:1024], WA[:, 1024:2048]
        WXT = WA[0:64, 2048:4096]
        WSL, WQ, WK, WV = (WB[0:64, 64 * n:64 * n + 64] for n in range(4))
        WOUT = WB[0:64, 256:2304]
        BX, BXR = WB[0:64, 2304:2312], WB[0:64, 2312:3336]
        BFX, TEMPC = WB[0:1, 3336:3848], WB[:, 3850:3858]
        BSL, RTEMP = WB[:, 3858:3922], WB[:, 3922:3930]
        BOUTB = CSTB[:, 11 * D:12 * D]
        LBIAS = CSTB[:, 9 * D:11 * D]
        SWT = BIG[:, :]
        VW, MO, MM = ACC[0:64, 0:2048], ACC[0:64, 2048:3072], ACC[:, 4096:5120]
        TOKT = XS[:, 0:1024]
        WSUM = SMALL[:, 200:712]
        NORM, RN, RNB, KT, VT = SW[0:1, 0:512], SW[0:1, 512:1024], SW[0:64, 512:1024], SW[0:64, 1024:1536], SW[0:64, 1536:2048]
        TOK, QT, ATT, ATTT = XT[0:64, 0:512], XT[0:64, 512:1024], SW[0:64, 0:512], SW[0:64, 2048:2560]
        ROUTER = CSTB[:, 12 * D:12 * D + 16]
        B2D = ACC[0:8 * CH, 0:CH * D]
        COMBW = SMALL[:, 960:960 + P]
        COMB = COMBW[:, 0:8 * CH]
        COMBT = SMALL[0:8 * CH, 800:800 + P]
        AD = SMALL[:, 0:16 * NT]
        OH4, OHT = WA, WB
        WHEAD = XS[0:1, 0:512].bitcast(I32)
        WR, BR = CSTB[:, 12 * D + 16:12 * D + 32], CSTB[:, 12 * D + 32:12 * D + 40]
        CHOSEN = sb("CHOSEN", [1, 2], I32)
        line = Chain(sem("dve_line"))

        def chunks(eng, body):
            with eng.Fori(0, NC - 1) as c:
                body(c, True)
            body(NC - 1, False)

        def turns(eng, body):
            with eng.Fori(0, TURNS - 1) as i:
                body(i, 2 * NG)
            body(TURNS - 1, NG)

        def ahead(c, j, k, more):
            if j + k < CH:
                return c, j + k
            return (c + 1, j + k - CH) if more else None

        block = ctx.enter_context(nc.Block())

        @block.sync
        def _(sp):
            sp.dma_start(dst2, a["dst"].rearrange("(p c) -> p c", p=P)).then_inc(sem("ld_dst"), 16)
            sp.wait_ge(sem("x_padded"), 2)
            sp.dma_start(X[:, 0:(NT - 1) * D].rearrange("p (t c) -> p t c", c=D),
                         a["x"][0:(NT - 1) * P, :].rearrange("(t p) c -> p t c", p=P)).then_inc(sem("ld_x"), 16)
            sp.dma_start(X[0:REST, (NT - 1) * D:NT * D], a["x"][(NT - 1) * P:N_NODES, :]).then_inc(sem("ld_x"), 16)
            with nc.allow_non_contiguous_dma(reason="edge index columns"):
                sp.dma_start(IDN[:, 0:NT], a["dst"][0:NT * P].rearrange("(t p) -> p t", p=P)).then_inc(sem("ld_idn"), 16)
                sp.dma_start(IDN[:, NT:2 * NT], a["src"][0:NT * P].rearrange("(t p) -> p t", p=P)).then_inc(sem("ld_idn"), 16)
            sp.dma_start(tile_src[:, 0:3 * P].rearrange("p (k e) -> p k e", k=3), a["src"][0:3 * P * P].rearrange("(k p e) -> p k e", k=3, p=P)).then_inc(sem("ld_tsrc"), 16)
            sp.dma_start(tile_src[0:ET - 3 * P, 3 * P:4 * P], a["src"][3 * P * P:ET * P].rearrange("(p e) -> p e", e=P)).then_inc(sem("ld_tsrc"), 16)
            wg = WG[:, :].rearrange("p (b c) -> p b c", b=KB)
            sp.dma_start(wg[:, :, 0:D], a["L0_gnn_weight"].rearrange("(b p) c -> p b c", p=P)).then_inc(sem("ld_w0"), 16)
            sp.dma_start(CSTB[:, 0:D], a["L0_gnn_attn_l"].rearrange("h d -> (h d)").partition_broadcast(P)).then_inc(sem("ld_w0"), 16)
            sp.dma_start(CSTB[:, D:2 * D], a["L0_gnn_attn_r"].rearrange("h d -> (h d)").partition_broadcast(P)).then_inc(sem("ld_w0"), 16)

            def store_table(st):
                for c in range(NC):
                    sp.wait_ge(sem("rows"), rows_before(st) + AHEAD + (c + 1) * CH)
                    sp.dma_start(table[c * CW:(c + 1) * CW, :].rearrange("(t p) c -> p t c", p=P),
                                 ACC[:, c * CH * ROW:(c + 1) * CH * ROW].rearrange("p (t c) -> p t c", c=ROW)).then_inc(sem("table_stored"), 16)
                    sp.wait_ge(sem("table_stored"), (GNNS.index(st) * NC + c + 1) * 16)
            store_table("g0")

            sp.dma_start(WA[:, 0:KB * 1024].rearrange("p (b c) -> p b c", b=KB), a["L0_ffn_w1"].rearrange("(b p) c -> p b c", p=P)).then_inc(sem("ld_f0"), 16)
            sp.dma_start(WB[:, 0:8 * D].rearrange("p (b c) -> p b c", b=8), a["L0_ffn_w2"].rearrange("(b p) c -> p b c", p=P)).then_inc(sem("ld_f0"), 16)
            with nc.allow_non_contiguous_dma(reason="bias columns"):
                sp.dma_start(B1[:, 0:8], a["L0_ffn_b1"].rearrange("(b p) -> p b", p=P)).then_inc(sem("ld_f0"), 16)
            sp.dma_start(CSTB[:, 2 * D:3 * D], a["L0_ffn_b2"].partition_broadcast(P)).then_inc(sem("ld_f0"), 16)
            sp.dma_start(CSTB[:, 3 * D:4 * D], a["L0_ffn_wr"].rearrange("a b -> (a b)").partition_broadcast(P)).then_inc(sem("ld_f0"), 16)
            sp.dma_start(SLF[:, 15:16], a["L0_ffn_br"].partition_broadcast(P)).then_inc(sem("ld_f0"), 16)
            sp.wait_ge(sem("f0_scoreT"), 1)
            sp.dma_start(wtab.rearrange("a (t p) -> (a t) p", p=P), TMP[0:NT, 0:P]).then_inc(sem("f0_wtab"), 16)
            sp.wait_ge(sem("f0_wtab"), 16)
            sp.dma_start(RANKROW, wtab.rearrange("a b -> (a b)").partition_broadcast(P)).then_inc(sem("f0_rankrow"), 16)

            for n, name in ((4, "L1_gnn_b"), (5, "L2_gnn_b"), (6, "L3_gnn_bias"), (7, "L3_ffn_gamma"), (8, "L3_ffn_beta")):
                sp.dma_start(CSTB[:, n * D:(n + 1) * D], a[name].partition_broadcast(P)).then_inc(sem("ld_bias"), 16)
            sp.wait_ge(sem("g0_mm"), AHEAD + NT)
            sp.dma_start(wg[:, :, 0:D], a["L1_gnn_W"].rearrange("(b p) c -> p b c", p=P)).then_inc(sem("ld_wg"), 16)
            store_table("g1")

            sp.wait_ge(sem("f0_y"), NT)
            sp.dma_start(WA[:, 1024:2048].rearrange("p (b c) -> p b c", b=KB), a["L1_ffn_W_fx"].rearrange("(b p) c -> p b c", p=P)).then_inc(sem("ld_t1"), 16)
            sp.dma_start(WA[0:64, 2048:4096].rearrange("p (h c) -> p h c", h=8), a["L1_ffn_W_xT"].rearrange("(h p) c -> p h c", p=64)).then_inc(sem("ld_t1"), 16)
            for n, name in enumerate(("W_slice", "W_q", "W_k", "W_v")):
                sp.dma_start(WB[0:64, 64 * n:64 * n + 64], a["L1_ffn_" + name]).then_inc(sem("ld_t1"), 16)
            sp.dma_start(WB[0:64, 256:2304].rearrange("p (h c) -> p h c", h=8), a["L1_ffn_W_out"].rearrange("(h p) c -> p h c", p=64)).then_inc(sem("ld_t1"), 16)
            with nc.allow_non_contiguous_dma(reason="bias columns"):
                sp.dma_start(BX, a["L1_ffn_b_x"].rearrange("(h p) -> p h", p=64)).then_inc(sem("ld_t1"), 16)
            sp.dma_start(BOUTB, a["L1_ffn_b_out"].partition_broadcast(P)).then_inc(sem("ld_t1"), 16)
            sp.dma_start(BFX, a["L1_ffn_b_fx"].rearrange("(a n) -> a n", a=1)).then_inc(sem("ld_t1"), 16)
            sp.dma_start(TEMPC, a["L1_ffn_temperature"].rearrange("a h b c -> (a h b c)").partition_broadcast(P)).then_inc(sem("ld_t1"), 16)
            sp.dma_start(BSL, a["L1_ffn_b_slice"].partition_broadcast(P)).then_inc(sem("ld_t1"), 16)
            sp.wait_ge(sem("t1_mout"), 1)
            sp.dma_start(MM[64:P, :], MO).then_inc(sem("t1_moved"), 16)

            sp.wait_ge(sem("g1_mm"), AHEAD + NT)
            sp.dma_start(wg[:, :, 0:D], a["L2_gnn_W"].rearrange("(b p) c -> p b c", p=P)).then_inc(sem("ld_wg"), 16)
            store_table("g2")

            sp.wait_ge(sem("t1_out"), NT)
            sp.dma_start(WA[:, :].rearrange("p (e b c) -> p e b c", e=8, b=KB), a["L2_ffn_w1"].rearrange("e (b p) c -> p e b c", p=P)).then_inc(sem("ld_m2"), 16)
            sp.dma_start(WB[:, :].rearrange("p (e b c) -> p e b c", e=8, b=KB), a["L2_ffn_w2"].rearrange("e (b p) c -> p e b c", p=P)).then_inc(sem("ld_m2"), 16)
            with nc.allow_non_contiguous_dma(reason="bias columns"):
                sp.dma_start(B1[:, :].rearrange("p (e b) -> p e b", e=8), a["L2_ffn_b1"].rearrange("e (b p) -> p e b", p=P)).then_inc(sem("ld_m2"), 16)
            sp.dma_start(ROUTER.rearrange("p (b e) -> p b e", b=KB), a["L2_ffn_router_wT"].rearrange("(b p) e -> p b e", p=P)).then_inc(sem("ld_m2"), 16)
            sp.wait_ge(sem("m2_b2zero"), 1)
            for j in range(CH):
                sp.dma_start(B2D[j * 8:(j + 1) * 8, j * D:(j + 1) * D], a["L2_ffn_b2"]).then_inc(sem("ld_m2"), 16)

            sp.wait_ge(sem("g2_mm"), AHEAD + NT)
            sp.dma_start(wg[:, :, 0:D], a["L3_gnn_W"].rearrange("(b p) h d -> p b (h d)", p=P)).then_inc(sem("ld_wg"), 16)
            sp.wait_ge(sem("a2_ix"), T_GROUPS + 1)
            sp.dma_start(CSTB[:, 0:D], a["L3_gnn_att_src"].rearrange("h d -> (h d)").partition_broadcast(P)).then_inc(sem("ld_wg"), 16)
            sp.dma_start(CSTB[:, D:2 * D], a["L3_gnn_att_dst"].rearrange("h d -> (h d)").partition_broadcast(P)).then_inc(sem("ld_wg"), 16)
            store_table("g3")

            sp.dma_start(WR.rearrange("p (b e) -> p b e", b=KB), a["L3_ffn_Wr"].rearrange("(b p) e -> p b e", p=P)).then_inc(sem("ld_wr"), 16)
            sp.dma_start(BR, a["L3_ffn_br"].partition_broadcast(P)).then_inc(sem("ld_wr"), 16)
            sp.wait_ge(sem("f3_chosen"), 1)
            e = [sp.value_load(CHOSEN[0:1, k:k + 1], min_val=0, max_val=7) for k in range(2)]
            one = lambda name, k: a[name][ds(e[k], 1)]
            for k in range(2):
                sp.dma_start(WA[:, :].rearrange("p (b k f) -> p b k f", b=4, k=2)[:, 0:KB, k, :],
                             one("L3_ffn_W1", k).rearrange("e (b p) f -> p (e b) f", p=P)).then_inc(sem("ld_f3a"), 16)
                with nc.allow_non_contiguous_dma(reason="bias columns"):
                    sp.dma_start(B1[:, k * 4:(k + 1) * 4], one("L3_ffn_b1", k).rearrange("e (b p) -> p (e b)", p=P)).then_inc(sem("ld_f3a"), 16)
            for k in range(2):
                sp.dma_start(WB[:, k * 1024:(k + 1) * 1024].rearrange("p (b c) -> p b c", b=4),
                             one("L3_ffn_W2", k).rearrange("e (b p) c -> p (e b) c", p=P)).then_inc(sem("ld_f3b"), 16)
                sp.dma_start(CSTB[:, k * D:(k + 1) * D], one("L3_ffn_b2", k).rearrange("e c -> (e c)").partition_broadcast(P)).then_inc(sem("ld_f3b"), 16)

            for c in range(NC):
                sp.wait_ge(sem("finished"), c + 1)
                full = min(CH, NT - 1 - c * CH)
                sp.dma_start(out[c * CW:c * CW + full * P, :].rearrange("(t p) c -> p t c", p=P),
                             X[:, c * CH * D:(c * CH + full) * D].rearrange("p (t c) -> p t c", c=D)).then_inc(sem("stored"), 16)
            sp.dma_start(out[(NT - 1) * P:N_NODES, :], X[0:REST, (NT - 1) * D:NT * D]).then_inc(sem("stored"), 16)
            sp.wait_ge(sem("stored"), (NC + 1) * 16)

        @block.gpsimd
        def _(g):
            g.iota(IOTA[:, :], pattern=[[1, P]], base=0, channel_multiplier=0, allow_small_or_imprecise_dtypes=True).then_inc(sem("cst"), 1)
            g.iota(IOTAP[:, :], pattern=[[P, 4]], base=0, channel_multiplier=1, allow_small_or_imprecise_dtypes=True).then_inc(sem("cst"), 1)
            g.memset(ONES[:, :], 1.0).then_inc(sem("cst"), 1)
            g.wait_ge(sem("cst"), 3)
            g.affine_select(out=IDENT[:, :], in_=ONES[:, :], compare_op=ALU.is_equal, fill=0.0, base=0,
                            pattern=[[-1, P]], channel_multiplier=1).then_inc(sem("cst"), 1)
            g.affine_select(out=LOWER[:, :], in_=ONES[:, :], compare_op=ALU.is_gt, fill=0.0, base=0,
                            pattern=[[-1, P]], channel_multiplier=1).then_inc(sem("cst"), 1)
            g.affine_select(out=MASK[:, :], in_=ONES[:, 0:NT], compare_op=ALU.is_gt, fill=0.0, base=N_NODES,
                            pattern=[[-P, NT]], channel_multiplier=-1).then_inc(sem("cst"), 1)
            g.wait_ge(sem("table_stored"), 16 * NC)
            g.wait_ge(sem("ld_idn"), 32)
            for t in range(NT):
                g.indirect_dma_start(out=BIG[:, t * ROW:(t + 1) * ROW], out_offset=None, in_=table,
                                     in_offset=bass.IndirectOffsetOnAxis(ap=IDN[:, t:t + 1], axis=0)).then_inc(sem("g0_gathered"), 16)
                g.indirect_dma_start(out=ACC[:, t * ROW:(t + 1) * ROW], out_offset=None, in_=table,
                                     in_offset=bass.IndirectOffsetOnAxis(ap=IDN[:, NT + t:NT + t + 1], axis=0)).then_inc(sem("g0_gathered"), 16)

            g.wait_ge(sem("slot_tile"), 1)
            for k in range(4):
                g.indirect_dma_start(out=slot_src[:, k * P:(k + 1) * P], out_offset=None, in_=a["src"].rearrange("(t e) -> t e", e=P),
                                     in_offset=bass.IndirectOffsetOnAxis(ap=SLI[:, k:k + 1], axis=0)).then_inc(sem("ld_slots"), 16)
                g.indirect_dma_start(out=slot_dst[:, k * P:(k + 1) * P], out_offset=None, in_=a["dst"].rearrange("(t e) -> t e", e=P),
                                     in_offset=bass.IndirectOffsetOnAxis(ap=SLI[:, k:k + 1], axis=0)).then_inc(sem("ld_slots"), 16)
            def gather_slots(tb, st):
                g.wait_ge(sem("table_stored"), (GNNS.index(tb) + 1) * NC * 16)
                g.wait_ge(sem("slots_ready"), 1)
                g.tensor_copy(IDX[:, 0:GRP], SRCI[:, 0:GRP]).then_inc(sem(f"{st}_ix"), 1)
                with g.Fori(0, TURNS) as i:
                    for q in range(NG):
                        n = i * BODY + q * GRP
                        r = (q + 1) % NG
                        g.wait_ge(sem(f"{st}_mm"), BODY + n - 2 * GRP)
                        g.wait_ge(sem(f"{st}_ix"), i * NG + q + 1)
                        g.tensor_copy(IDX[:, r * GRP:(r + 1) * GRP], SRCI[:, ds(n + GRP, GRP)]).then_inc(sem(f"{st}_ix"), 1)
                        for k in range(q * GRP, (q + 1) * GRP):
                            g.indirect_dma_start(out=G[:, k * ROW:(k + 1) * ROW], out_offset=None, in_=table,
                                                 in_offset=bass.IndirectOffsetOnAxis(ap=IDX[:, k:k + 1], axis=0)).then_inc(sem(f"{st}_in{q}"), 16)
                g.wait_ge(sem(f"{st}_ix"), TURNS * NG + 1)

            def gather_tiles(tb, st):
                g.wait_ge(sem("table_stored"), (GNNS.index(tb) + 1) * NC * 16)
                g.wait_ge(sem("slots_ready"), 1)
                g.tensor_copy(IDX[:, 0:GRP], TSRC[:, 0:GRP]).then_inc(sem(f"{st}_ix"), 1)

                def body(i, groups):
                    for q in range(groups):
                        n = (i * TG + q) * GRP
                        r = (q + 1) % TG
                        g.wait_ge(sem(f"{st}_mm"), BODY + n - 2 * GRP)
                        g.wait_ge(sem(f"{st}_ix"), i * TG + q + 1)
                        g.tensor_copy(IDX[:, r * GRP:(r + 1) * GRP], TSRC[:, ds(n + GRP, GRP)]).then_inc(sem(f"{st}_ix"), 1)
                        for k in range(q * GRP, (q + 1) * GRP):
                            g.indirect_dma_start(out=GT[:, k * ROW:(k + 1) * ROW], out_offset=None, in_=table,
                                                 in_offset=bass.IndirectOffsetOnAxis(ap=IDX[:, k:k + 1], axis=0)).then_inc(sem(f"tiles_in{q}"), 16)
                with g.Fori(0, T_GROUPS // TG) as i:
                    body(i, TG)
                body(T_GROUPS // TG, T_GROUPS % TG)
                g.wait_ge(sem(f"{st}_ix"), T_GROUPS + 1)

            gather_tiles("g1", "a1")
            g.sem_inc(sem("t1_wsum"), AHEAD)
            g.wait_ge(sem("t1_fold"), 1)
            with g.Fori(0, NC) as c:
                for j in range(CH):
                    n = c * CH + j
                    g.wait_ge(sem("t1_sw"), n + 1)
                    g.wait_ge(sem("t1_wsum"), AHEAD + n)
                    g.tensor_tensor(WSUM, WSUM, SW[:, j * 512:(j + 1) * 512], ALU.add).then_inc(sem("t1_wsum"), 1)
            gather_tiles("g2", "a2")
            gather_slots("g3", "a3")
            with g.Fori(0, NC) as c:
                g.wait_ge(sem("a3_out"), c + 1)
                acc = ACC[:, ds(c * CH * ROW, CH * ROW)].rearrange("p (t c) -> p t c", c=ROW)[:, :, 0:D]
                g.tensor_tensor(acc, acc, CSTB[:, 6 * D:7 * D].unsqueeze(1).to_broadcast([P, CH, D]), ALU.add).then_inc(sem("a3_biased"), 1)

        @block.tensor
        def _(pe):
            pe.sem_inc(sem("tp"), AHEAD)
            pe.wait_ge(sem("cst"), 6)
            def turn(st, c, j):
                n = c * CH + j
                pe.wait_ge(sem("xs"), tiles_before(st) + n + 1)
                pe.wait_ge(sem("xt"), tiles_before(st) + AHEAD + n + 1 - (1 if j == 0 else 2))
                for b in range(KB):
                    mm = pe.transpose(PB[j % 2][:, b * P:(b + 1) * P], XS[:, j * D + b * P:j * D + (b + 1) * P], IDENT[:, :])
                mm.then_inc(sem("tp"), 1)

            def project(st, width):
                pe.sem_inc(sem(f"{st}_mm"), AHEAD)

                def body(c, more):
                    for j in range(CH):
                        at = ahead(c, j, 2, more)
                        if at:
                            turn(st, *at)
                        n = c * CH + j
                        pe.wait_ge(sem("xt"), tiles_before(st) + AHEAD + n + 1)
                        pe.wait_ge(sem("rows"), rows_before(st) + AHEAD + n + 1 - CH)
                        for b in range(KB):
                            mm = pe.matmul(PB[2 + j][:, 0:width], XT[:, b * CW + j * P:b * CW + (j + 1) * P],
                                           WG[:, b * GW:b * GW + width], start=(b == 0), stop=(b == KB - 1))
                        mm.then_inc(sem(f"{st}_mm"), 1)
                turn(st, 0, 0)
                turn(st, 0, 1)
                chunks(pe, body)

            hist = PB[7][:, 0:NT]

            def count(first, turns):
                with pe.Fori(0, turns) as i:
                    for r in range(2):
                        pe.wait_ge(sem("h_onehot"), (first + i) * 2 + r + 1)
                        for k in range(HB):
                            mm = pe.matmul(hist, ob[:, (r * HB + k) * P:(r * HB + k + 1) * P], oa[:, (r * HB + k) * NT:(r * HB + k + 1) * NT],
                                           start=False, stop=False, skip_group_check=True)
                        mm.then_inc(sem("h_used"), 1)
            pe.wait_ge(sem("iotab"), 1)
            pe.sem_inc(sem("h_used"), 2)
            pe.matmul(hist, IOTAB[:, :], ZEROB[:, :], start=True, stop=False, skip_group_check=True)
            count(0, H_EARLY)
            pe.wait_ge(sem("g0_weights"), 1)
            project("g0", ROW)
            count(H_EARLY, H_TURNS - H_EARLY)

            pe.matmul(hist, IOTAB[:, :], ZEROB[:, :], start=False, stop=True, skip_group_check=True).then_inc(sem("hist"), 1)
            pe.wait_ge(sem("hist_sb"), 1)
            pe.matmul(PB[6][:, 0:NT], ONES[:, :], T1[:, :], start=True, stop=True).then_inc(sem("totals"), 1)
            pe.wait_ge(sem("slot_rows"), 1)
            for k in range(4):
                pe.transpose(PB[4][:, k * P:(k + 1) * P], slot_srcf[:, k * P:(k + 1) * P], IDENT[:, :])
                pe.transpose(PB[5][:, k * P:(k + 1) * P], slot_dstf[:, k * P:(k + 1) * P], IDENT[:, :])
                mm = pe.matmul(PB[6][0:1, k * P:(k + 1) * P], SLF[:, 4 + k:5 + k], IDENT[:, :], start=True, stop=True)
                pe.matmul(PB[3][0:1, k * P:(k + 1) * P], SLF[:, 8 + k:9 + k], IDENT[:, :], start=True, stop=True)
            pe.wait_ge(sem("tile_rows"), 1)
            for k in range(4):
                mm = pe.transpose(PB[7][:, k * P:(k + 1) * P], tile_srcf[:, k * P:(k + 1) * P], IDENT[:, :])
            mm.then_inc(sem("slotsT"), 1)

            def ffn(st, w1, w2, ready1, ready2):
                pe.sem_inc(sem(f"{st}_hid"), AHEAD)

                def body(c, more):
                    pe.wait_ge(sem("xt"), tiles_before(st) + AHEAD + c * CH + CH)
                    pe.wait_ge(*ready1)
                    for h in range(8):
                        n = c * 8 + h
                        pe.wait_ge(sem(f"{st}_act"), AHEAD + n + 1 - 2)
                        for s in range(2):
                            for b in range(KB):
                                mm = pe.matmul(PB[2 + 2 * (h % 2) + s][:, 0:HALF], w1[:, b * 1024 + h * P:b * 1024 + (h + 1) * P],
                                               XT[:, b * CW + s * HALF:b * CW + (s + 1) * HALF], start=(b == 0), stop=(b == KB - 1))
                        mm.then_inc(sem(f"{st}_hid"), 1)
                    if more:
                        for j in range(CH):
                            turn(st, c + 1, j)
                    pe.wait_ge(sem(f"{st}_act"), AHEAD + c * 8 + 8)
                    pe.wait_ge(*ready2)
                    for j in range(CH):
                        n = c * CH + j
                        pe.wait_ge(sem(f"{st}_out"), AHEAD + n + 1 - (1 if j == 0 else 2))
                        for h in range(8):
                            mm = pe.matmul(PB[6 + j % 2][:, 0:D], HT[:, h * CW + j * P:h * CW + (j + 1) * P], w2[:, h * D:(h + 1) * D],
                                           start=(h == 0), stop=(h == 7))
                        mm.then_inc(sem(f"{st}_y"), 1)
                for j in range(CH):
                    turn(st, 0, j)
                chunks(pe, body)

            pe.wait_ge(sem("f0_score"), 1)
            pe.transpose(PB[2][0:NT, 0:P], COEF[:, :], IDENT[:, :]).then_inc(sem("f0_scoreP"), 1)
            pe.wait_ge(sem("ld_f0"), 16 * 6)
            pe.wait_ge(sem("f0_scoreT"), 1)
            ffn("f0", WA, WB, (sem("ld_f0"), 16 * 6), (sem("ld_f0"), 16 * 6))

            def sum_slots(st, width):
                pe.sem_inc(sem(f"{st}_mm"), BODY)
                regs = [pe.alloc_register(f"{st}_tile{k}") for k in range(GRP)]

                def body(i, groups, tiles):
                    for q in range(groups):
                        n0 = (i * TG + q) * GRP
                        if q < tiles:
                            pe.wait_ge(sem(f"tiles_in{q}"), 16 * GRP * (i + 1 + (st == "a2") * groups_at(q)))
                        pe.wait_ge(sem(f"{st}_oh"), i * TG + q + 1)
                        pe.load(regs, TROW[0:1, ds(n0, GRP)])
                        for k in range(GRP):
                            t = pe.snap(regs[k], min_val=0, max_val=(RING - 1) * ROW)
                            pe.wait_ge(sem(f"{st}_acc"), BODY + n0 + k + 1 - GRP)
                            pe.matmul(PB[k][:, 0:width], OH[:, ((q % 2) * GRP + k) * P:((q % 2) * GRP + k + 1) * P],
                                      GT[:, ds(t, width)], start=True, stop=True).then_inc(sem(f"{st}_mm"), 1)
                with pe.Fori(0, S_GROUPS // TG) as i:
                    body(i, TG, TG)
                body(S_GROUPS // TG, S_GROUPS % TG, T_GROUPS % TG)
                for r in regs:
                    pe.free_register(r)

            pe.wait_ge(sem("ld_wg"), 16)
            project("g1", D)
            sum_slots("a1", D)

            def slices(st):
                pe.wait_ge(sem("ld_t1"), 16 * 12)
                pe.wait_ge(sem("a1_acc"), BODY + SLOTS)
                for b in range(KB):
                    for h in range(8):
                        pe.matmul(PB[b][:, h * 64:h * 64 + 64], WXT[:, h * D + b * P:h * D + (b + 1) * P], WSL, start=True, stop=True)
                pe.wait_ge(sem(f"{st}_bxr"), 1)
                for h in range(8):
                    mm = pe.matmul(PB[2][:, h * 64:h * 64 + 64], BXR[:, h * P:(h + 1) * P], WSL, start=True, stop=True)
                mm.then_inc(sem(f"{st}_wxs"), 1)
                pe.sem_inc(sem(f"{st}_lg"), AHEAD)
                pe.sem_inc(sem(f"{st}_tok"), AHEAD)
                pe.wait_ge(sem(f"{st}_fold"), 1)
                for k in (4, 5):
                    pe.matmul(PB[k][:, :], ONES[:, :], TMP[:, 0:512], start=True, stop=False, skip_group_check=True)

                def logits(c, j):
                    n = c * CH + j
                    pe.wait_ge(sem("xt"), tiles_before(st) + AHEAD + n + 1)
                    pe.wait_ge(sem(f"{st}_lgc"), AHEAD + n + 1 - (1 if j == 0 else 2))
                    for b in range(KB):
                        mm = pe.matmul(PB[2 + j % 2][:, :], XT[:, b * CW + j * P:b * CW + (j + 1) * P], WXS[:, b * 512:(b + 1) * 512],
                                       start=(b == 0), stop=(b == KB - 1))
                    mm.then_inc(sem(f"{st}_lg"), 1)

                def tokens(c, j):
                    n = c * CH + j
                    w = SW[:, j * 512:(j + 1) * 512]
                    pe.wait_ge(sem(f"{st}_sw"), n + 1)
                    for b in range(KB):
                        pe.matmul(PB[4 + b][:, :], XS[:, j * D + b * P:j * D + (b + 1) * P], w, start=False, stop=False, skip_group_check=True)
                    pe.wait_ge(sem(f"{st}_swt"), AHEAD + n + 1 - 1)
                    for b in range(4):
                        mm = pe.transpose(PB[7][:, b * P:(b + 1) * P], w[:, b * P:(b + 1) * P], IDENT[:, :])
                    mm.then_inc(sem(f"{st}_tok"), 1)

                def body(c, more):
                    for j in range(CH):
                        for k, part in ((2, lambda cc, jj: turn(st, cc, jj)), (1, logits)):
                            at = ahead(c, j, k, more)
                            if at:
                                part(*at)
                        tokens(c, j)
                turn(st, 0, 0)
                turn(st, 0, 1)
                logits(0, 0)
                chunks(pe, body)
                for k in (4, 5):
                    pe.matmul(PB[k][:, :], ONES[:, :], TMP[:, 0:512], start=False, stop=True, skip_group_check=True)
                pe.wait_ge(sem(f"{st}_wsum"), AHEAD + NT)
                pe.matmul(PB[6][0:1, :], ONES[:, 0:1], WSUM, start=True, stop=True).then_inc(sem(f"{st}_sums"), 1)
                pe.wait_ge(sem(f"{st}_norm"), 1)
                for h in range(8):
                    o = slice(h * 64, h * 64 + 64)
                    for b in range(KB):
                        pe.matmul(PB[0][0:64, o], WFX[:, b * 512 + h * 64:b * 512 + h * 64 + 64], TOKT[:, b * 512 + h * 64:b * 512 + h * 64 + 64], start=(b == 0), stop=False)
                    pe.matmul(PB[0][0:64, o], BFX[:, o], NORM[:, o], start=False, stop=True)
                pe.matmul(PB[1][0:64, :], ONES[0:1, 0:64], RN, start=True, stop=True).then_inc(sem(f"{st}_tokens"), 1)
                pe.wait_ge(sem(f"{st}_token"), 1)
                for k, w in ((2, WQ), (3, WK), (4, WV)):
                    mm = pe.matmul(PB[k][0:64, :], w, TOK, start=True, stop=True)
                mm.then_inc(sem(f"{st}_qkv"), 1)
                pe.wait_ge(sem(f"{st}_qkvc"), 1)
                for h in range(8):
                    o = slice(h * 64, h * 64 + 64)
                    mm = pe.matmul(PB[5][0:64, o], QT[:, o], KT[:, o], start=True, stop=True)
                mm.then_inc(sem(f"{st}_att"), 1)
                for h in range(8):
                    mm = pe.matmul(PB[h // 2][0:64, (h % 2) * D:(h % 2 + 1) * D], VT[:, h * 64:h * 64 + 64], WOUT[:, h * D:(h + 1) * D], start=True, stop=True)
                mm.then_inc(sem(f"{st}_vw"), 1)
                pe.wait_ge(sem(f"{st}_soft"), 1)
                for h in range(8):
                    o = slice(h * 64, h * 64 + 64)
                    mm = pe.transpose(PB[6][0:64, o], ATT[:, o], IDENT[0:64, 0:64])
                mm.then_inc(sem(f"{st}_attT"), 1)
                pe.wait_ge(sem(f"{st}_attc"), 1)
                for h in range(8):
                    mm = pe.matmul(PB[h // 2][0:64, (h % 2) * D:(h % 2 + 1) * D], ATTT[:, h * 64:h * 64 + 64], VW[:, h * D:(h + 1) * D], start=True, stop=True)
                mm.then_inc(sem(f"{st}_m"), 1)
                pe.wait_ge(sem(f"{st}_moved"), 16)
                pe.wait_ge(sem(f"{st}_mout"), 1)
                for n in range(NT):
                    if n > 1:
                        pe.wait_ge(sem(f"{st}_out"), n - 1)
                    for b in range(4):
                        mm = pe.matmul(PB[4 + n % 2][:, 0:D], SWT[:, b * NT * P + n * P:b * NT * P + (n + 1) * P], MM[:, b * D:(b + 1) * D],
                                       start=(b == 0), stop=(b == 3))
                    mm.then_inc(sem(f"{st}_y"), 1)

            slices("t1")
            pe.wait_ge(sem("ld_wg"), 32)
            project("g2", D)
            sum_slots("a2", D)

            def experts(st):
                pe.sem_inc(sem(f"{st}_hid"), AHEAD)

                def turned(c):
                    for j in range(CH):
                        turn(st, c, j)
                    pe.wait_ge(sem("xt"), tiles_before(st) + AHEAD + c * CH + CH)
                    for j in range(CH):
                        for b in range(KB):
                            mm = pe.matmul(PB[1][:, j * 8:j * 8 + 8], XT[:, b * CW + j * P:b * CW + (j + 1) * P], ROUTER[:, b * 8:b * 8 + 8],
                                           start=(b == 0), stop=(b == KB - 1))
                    mm.then_inc(sem(f"{st}_logits"), 1)

                def body(c, more):
                    pe.wait_ge(sem(f"{st}_b2"), AHEAD + c)

                    def hidden(e):
                        for h in range(KB):
                            pe.wait_ge(sem(f"{st}_act"), AHEAD + (c * 8 + e) * 2 + h + 1 - 2)
                            for s in range(2):
                                for b in range(KB):
                                    mm = pe.matmul(PB[2 + 2 * h + s][:, 0:HALF], WA[:, (e * KB + b) * D + h * P:(e * KB + b) * D + (h + 1) * P],
                                                   XT[:, b * CW + s * HALF:b * CW + (s + 1) * HALF], start=(b == 0), stop=(b == KB - 1))
                            mm.then_inc(sem(f"{st}_hid"), 1)

                    def outputs(e):
                        pe.wait_ge(sem(f"{st}_act"), AHEAD + (c * 8 + e) * 2 + 2)
                        for j in range(CH):
                            pe.wait_ge(sem(f"{st}_out"), AHEAD + (c * 8 + e) * CH + j + 1 - 2)
                            for h in range(KB):
                                mm = pe.matmul(PB[6 + (e * CH + j) % 2][:, 0:D], HT[:, ((e % 2) * KB + h) * CW + j * P:((e % 2) * KB + h) * CW + (j + 1) * P],
                                               WB[:, (e * KB + h) * D:(e * KB + h + 1) * D], start=(h == 0), stop=(h == KB - 1))
                            mm.then_inc(sem(f"{st}_y"), 1)
                    hidden(0)
                    for e in range(1, 8):
                        hidden(e)
                        outputs(e - 1)
                    pe.wait_ge(sem(f"{st}_comb"), c + 1)
                    if more:
                        turned(c + 1)
                    pe.wait_ge(sem(f"{st}_act"), AHEAD + c * 16 + 16)
                    pe.transpose(PB[2][:, 0:P], COMBW, IDENT[:, :]).then_inc(sem(f"{st}_combT"), 1)
                    outputs(7)
                    pe.wait_ge(sem(f"{st}_combTc"), c + 1)
                    for k in range(3):
                        w = min(512, CH * D - k * 512)
                        mm = pe.matmul(PB[3 + k][:, 0:w], COMBT, B2D[:, k * 512:k * 512 + w], start=True, stop=True)
                    mm.then_inc(sem(f"{st}_b2y"), 1)
                turned(0)
                chunks(pe, body)

            pe.wait_ge(sem("ld_m2"), 16 * 9)
            experts("m2")

            def sum_attended(st):
                regs = [pe.alloc_register(f"{st}_win{k}") for k in range(GRP)]

                def turned(g, r, first):
                    pe.wait_ge(sem(f"{st}_oh"), g + 1)
                    for s in range(2):
                        if not first:
                            pe.wait_ge(sem(f"{st}_tpc"), 2 * g + s - 1)
                        for k in range(4):
                            o = (r * GRP + s * 4 + k) * P
                            mm = pe.transpose(PB[4 + s][:, k * P:(k + 1) * P], OH4[:, o:o + P], IDENT[:, :])
                        mm.then_inc(sem(f"{st}_turned"), 1)

                def terms(g, r, n0):
                    pe.wait_ge(sem(f"{st}_tpc"), 2 * g + 2)
                    pe.wait_ge(sem(f"{st}_z"), g)
                    pe.load(regs, WHEAD[0:1, ds(n0, GRP)])
                    for k in range(GRP):
                        w = pe.snap(regs[k], min_val=0, max_val=(NT - 1) * 8)
                        mm = pe.matmul(PB[6 + r % 2][:, k * 16:k * 16 + 16].rearrange("p (a h) -> p a h", a=2), OHT[:, ((r % 2) * GRP + k) * P:((r % 2) * GRP + k + 1) * P],
                                       AD.rearrange("p (a n) -> p a n", a=2)[:, :, ds(w, 8)], start=True, stop=True)
                    mm.then_inc(sem(f"{st}_ad"), 1)

                pe.sem_inc(sem(f"{st}_mm"), BODY)
                turned(0, 0, True)
                pe.wait_ge(sem("g3_ad"), 1)
                turned(1, 1, False)
                terms(0, 0, 0)

                def body(i, end):
                    for q in range(NG):
                        g = i * NG + q
                        if q + 1 < end:
                            terms(g + 1, q + 1, (g + 1) * GRP)
                        pe.wait_ge(sem(f"{st}_scaled"), g + 1)
                        for k in range(GRP):
                            if k == 4 and q + 2 < end:
                                turned(g + 2, (q + 2) % NG, False)
                            n = i * BODY + q * GRP + k
                            pe.wait_ge(sem(f"{st}_acc"), BODY + n + 1 - 4)
                            pe.matmul(PB[k % 4][:, 0:ROW], OH4[:, (q * GRP + k) * P:(q * GRP + k + 1) * P],
                                      G[:, (q * GRP + k) * ROW:(q * GRP + k + 1) * ROW], start=True, stop=True).then_inc(sem(f"{st}_mm"), 1)
                turns(pe, body)

            pe.wait_ge(sem("g3_weights"), 1)
            project("g3", 272)
            pe.wait_ge(sem("g3_umax"), 1)
            pe.transpose(PB[0][0:8, 0:P], SMALL[:, 800:808], IDENT[:, :]).then_inc(sem("g3_u"), 1)
            pe.wait_ge(sem("g3_umax"), 2)
            pe.matmul(PB[0][:, 0:8], ONES[0:8, :], SMALL[0:8, 816:824], start=True, stop=True).then_inc(sem("g3_u"), 1)
            sum_attended("a3")

            pe.wait_ge(sem("f3_stats"), 1)
            mean = PB[0][0:1, 0:D]
            for t in range(NT):
                pe.matmul(mean, RSTD[:, t:t + 1], X[:, t * D:(t + 1) * D], start=(t == 0), stop=False)
            for b in range(KB):
                mm = pe.matmul(PB[0][0:1, b * P:(b + 1) * P], SMALL[:, 0:1], ONES[:, :], start=False, stop=(b == KB - 1))
            mm.then_inc(sem("f3_mean"), 1)
            pe.wait_ge(sem("f3_mean_sb"), 1)
            for b in range(KB):
                mm = pe.matmul(PB[3 + b][:, 0:P], OH[0:1, D + b * P:D + (b + 1) * P], ONES[0:1, :], start=True, stop=True)
            mm.then_inc(sem("f3_mean"), 1)
            pe.wait_ge(sem("f3_mean_sb"), 2)
            pe.wait_ge(sem("ld_wr"), 32)
            for b in range(KB):
                mm = pe.matmul(PB[2][:, 0:8], OH[:, b * P:(b + 1) * P], WR[:, b * 8:b * 8 + 8], start=(b == 0), stop=(b == KB - 1))
            mm.then_inc(sem("f3_logits"), 1)
            ffn("f3", WA, WB, (sem("ld_f3a"), 16 * 4), (sem("f3_weights"), 1))

        @block.scalar
        def _(act):
            act.sem_inc(sem("xt"), AHEAD)
            def ln_root(st):
                act.wait_ge(sem("var"), ORDER.index(st) + 1)
                act.activation(T1[:, :], VAR[:, :], ACT.Sqrt).then_inc(sem("std"), 1)

            def to_xt(st, c, j):
                act.wait_ge(sem("tp"), tiles_before(st) + AHEAD + c * CH + j + 1)
                act.activation(XT[:, :].rearrange("p (b n) -> p b n", b=KB)[:, :, j * P:(j + 1) * P],
                               PB[j % 2][:, 0:D].rearrange("p (b n) -> p b n", b=KB), ACT.Copy).then_inc(sem("xt"), 1)

            def project(st):
                with act.Fori(0, NC) as c:
                    for j in range(CH):
                        act.wait_ge(sem(f"{st}_mm"), AHEAD + c * CH + j + 1 - CH)
                        to_xt(st, c, j)

            def relus(st):
                act.wait_ge(sem(f"{st}_acc"), BODY + SLOTS)
                with act.Fori(0, NT) as t:
                    act.activation(BIG[:, ds(t * D, D)], ACC[:, ds(t * ROW, D)], ACT.Relu, scale=DINV[:, ds(t, 1)]).then_inc(sem(f"{st}_relu"), 1)

            def ffn(st, func, root=None):
                act.sem_inc(sem(f"{st}_act"), AHEAD)

                def body(c, more, first=False):
                    for h in range(8):
                        act.wait_ge(sem(f"{st}_hid"), AHEAD + c * 8 + h + 1)
                        k = 2 + 2 * (h % 2)
                        for s in range(2):
                            ins = act.activation(HT[:, h * CW + s * HALF:h * CW + (s + 1) * HALF], PB[k + s][:, 0:HALF], func, bias=B1[:, h:h + 1])
                        ins.then_inc(sem(f"{st}_act"), 1)
                        if h == 1 and root and not first:
                            root(c - 1)
                    if more:
                        for j in range(CH):
                            to_xt(st, c + 1, j)
                for j in range(CH):
                    to_xt(st, 0, j)
                if root:
                    body(0, True, True)
                    with act.Fori(0, NC - 2) as i:
                        body(i + 1, True)
                    body(NC - 1, False)
                else:
                    chunks(act, body)

            ln_root("g0")
            project("g0")
            act.wait_ge(sem("deg"), 1)
            act.activation(DINV[:, :], VAR[:, :], ACT.Sqrt).then_inc(sem("dinv"), 1)
            act.wait_ge(sem("g0_logit"), 1)
            act.activation(ADS[:, 0:4 * NT], ADS[:, 0:4 * NT], ACT.Exp).then_inc(sem("g0_exp"), 1)
            ln_root("f0")
            act.wait_ge(sem("f0_scoreP"), 1)
            act.activation(TMP[0:NT, 0:P], PB[2][0:NT, 0:P], ACT.Copy).then_inc(sem("f0_scoreT"), 1)
            ffn("f0", ACT.Gelu_apprx_tanh)
            ln_root("g1")
            project("g1")
            def slices(st):
                act.sem_inc(sem(f"{st}_swt"), AHEAD)

                def turned(c, j):
                    act.wait_ge(sem(f"{st}_lg"), AHEAD + c * CH + j + 1 - CH)
                    to_xt(st, c, j)

                def exps(c, j):
                    w = SW[:, j * 512:(j + 1) * 512]
                    act.wait_ge(sem(f"{st}_sub"), c * CH + j + 1)
                    act.activation(w, w, ACT.Exp).then_inc(sem(f"{st}_exp"), 1)

                def body(c, more):
                    for j in range(CH):
                        for k, part in ((2, turned), (1, exps)):
                            at = ahead(c, j, k, more)
                            if at:
                                part(*at)
                        to_swt(st, c * CH + j)
                turned(0, 0)
                turned(0, 1)
                exps(0, 0)
                chunks(act, body)
                act.wait_ge(sem(f"{st}_sub2"), 1)
                act.activation(ATT, ATT, ACT.Exp, scale=0.125).then_inc(sem(f"{st}_exp2"), 1)

            def to_swt(st, n):
                act.wait_ge(sem(f"{st}_tok"), AHEAD + n + 1)
                act.activation(SWT.rearrange("p (b n) -> p b n", b=4)[:, :, ds(n * P, P)], PB[7][:, :].rearrange("p (b n) -> p b n", b=4),
                               ACT.Copy).then_inc(sem(f"{st}_swt"), 1)

            relus("a1")
            ln_root("t1")
            slices("t1")
            ln_root("g2")
            project("g2")
            relus("a2")

            st = "m2"
            ln_root(st)
            act.sem_inc(sem(f"{st}_act"), AHEAD)

            def body(c, more):
                act.wait_ge(sem(f"{st}_sub"), c + 1)
                act.activation(COMB, COMB, ACT.Exp).then_inc(sem(f"{st}_exp"), 1)
                for h in range(16):
                    act.wait_ge(sem(f"{st}_hid"), AHEAD + c * 16 + h + 1)
                    for s in range(2):
                        ins = act.activation(HT[:, (h % 4) * CW + s * HALF:(h % 4) * CW + (s + 1) * HALF], PB[2 + 2 * (h % 2) + s][:, 0:HALF],
                                             ACT.Gelu, bias=B1[:, h:h + 1])
                    ins.then_inc(sem(f"{st}_act"), 1)
                if more:
                    for j in range(CH):
                        to_xt(st, c + 1, j)
            for j in range(CH):
                to_xt(st, 0, j)
            chunks(act, body)

            ln_root("g3")
            project("g3")
            st = "a3"
            act.sem_inc(sem(f"{st}_z"), 1)

            def copy_turned(g, r):
                for s in range(2):
                    act.wait_ge(sem(f"{st}_turned"), 2 * g + s + 1)
                    act.activation(OHT[:, (r * 2 + s) * 512:(r * 2 + s + 1) * 512], PB[4 + s][:, :], ACT.Copy).then_inc(sem(f"{st}_tpc"), 1)

            def exps(g, r):
                act.wait_ge(sem(f"{st}_z"), g + 2)
                act.activation(G[:, r * GRP * ROW:(r + 1) * GRP * ROW].rearrange("p (k c) -> p k c", c=ROW)[:, :, D:D + 8],
                               TMP[:, (r % 2) * 64:(r % 2 + 1) * 64].rearrange("p (k h) -> p k h", k=GRP), ACT.Exp).then_inc(sem(f"{st}_exp"), 1)
            copy_turned(0, 0)
            copy_turned(1, 1)
            exps(0, 0)

            def body(i, end):
                for q in range(NG):
                    g = i * NG + q
                    if q + 2 < end:
                        copy_turned(g + 2, q % 2)
                    if q + 1 < end:
                        exps(g + 1, (q + 1) % NG)
            turns(act, body)

            ln_root("f3")
            act.wait_ge(sem("f3_sub"), 1)
            act.activation(SMALL[:, 16:24], SMALL[:, 16:24], ACT.Exp).then_inc(sem("f3_exp"), 1)
            act.wait_ge(sem("f3_sub"), 2)
            act.activation(SMALL[:, 16:24], SMALL[:, 16:24], ACT.Exp).then_inc(sem("f3_exp"), 1)
            act.wait_ge(sem("f3_sub"), 3)
            act.activation(SMALL[:, 48:49], SMALL[:, 48:49], ACT.Exp).then_inc(sem("f3_exp"), 1)

            def root(c):
                act.wait_ge(sem("var"), ORDER.index("n3") + c + 1)
                act.activation(SMALL[:, 116:116 + CH], SMALL[:, 108:108 + CH], ACT.Sqrt).then_inc(sem("std"), 1)
            ffn("f3", ACT.Gelu, root)
            root(NC - 1)

        @block.vector
        def _(v):
            v.sem_inc(sem("rows"), AHEAD)
            v.memset(X[:, (NT - 1) * D:NT * D], 0.0).then_inc(sem("x_padded"), 1)
            v.memset(tile_src, 0).then_inc(sem("x_padded"), 1)
            line.mark(v.memset(ZEROB[:, :], 0.0))
            v.wait_ge(sem("cst"), 6)
            line.sync(v)
            v.tensor_copy(IOTAB[:, :], IOTA[:, :]).then_inc(sem("iotab"), 1)
            v.wait_ge(sem("ld_dst"), 16)
            line.mark(v.tensor_scalar(dlo, dst2, P - 1, None, ALU.bitwise_and))
            line.step(v, v.tensor_scalar(dhi, dst2, 7, None, ALU.arith_shift_right))
            line.mark(v.tensor_copy(dlob, dlo))
            line.step(v, v.tensor_copy(dhib, dhi))
            v.wait_ge(sem("iotab"), 1)

            def count(first, turns):
                with v.Fori(0, turns) as i:
                    for r in range(2):
                        v.wait_ge(sem("h_used"), (first + i) * 2 + r + 1)
                        at = (first + i) * 2 * HB + r * HB
                        v.tensor_tensor(ob[:, r * HB * P:(r + 1) * HB * P].rearrange("p (k n) -> p k n", k=HB),
                                        IOTAB[:, :].unsqueeze(1).to_broadcast([P, HB, P]),
                                        dlob[:, ds(at, HB)].unsqueeze(2).to_broadcast([P, HB, P]), ALU.is_equal)
                        v.tensor_tensor(oa[:, r * HB * NT:(r + 1) * HB * NT].rearrange("p (k n) -> p k n", k=HB),
                                        IOTAB[:, 0:NT].unsqueeze(1).to_broadcast([P, HB, NT]),
                                        dhib[:, ds(at, HB)].unsqueeze(2).to_broadcast([P, HB, NT]),
                                        ALU.is_equal).then_inc(sem("h_onehot"), 1)
            count(0, H_EARLY)
            def ln_stats(st):
                with v.Fori(0, NC) as c:
                    chunk_stats(c)
                moments(st)

            def chunk_stats(c):
                for j in range(CH):
                    v.bn_stats(tile(ST6, c * CH + j, 6, 6), tile(X, c * CH + j)).then_inc(sem("bn"), 1)

            def chunk(buf, c, w=D, stride=D):
                return buf[:, ds(c * CH * stride, CH * stride)].rearrange("p (t c) -> p t c", c=stride)[:, :, 0:w]

            def moments(st):
                v.wait_ge(sem("bn"), tiles_before(st) + NT)
                s6 = ST6[:, :].rearrange("p (t k) -> p k t", k=6)
                line.mark(v.tensor_tensor(T1[:, :], s6[:, 1, :], s6[:, 4, :], ALU.subtract))
                line.mark(v.tensor_tensor(MEAN[:, :], s6[:, 1, :], s6[:, 4, :], ALU.add))
                line.step(v, v.tensor_tensor(T2[:, :], s6[:, 2, :], s6[:, 5, :], ALU.add))
                line.step(v, v.tensor_tensor(T1[:, :], T1[:, :], T1[:, :], ALU.mult))
                line.mark(v.tensor_scalar(MEAN[:, :], MEAN[:, :], 0.5, None, ALU.mult))
                line.mark(v.tensor_scalar(T1[:, :], T1[:, :], 0.25, LN_EPS, ALU.mult, ALU.add))
                line.sync(v)
                v.scalar_tensor_tensor(VAR[:, :], T2[:, :], 1.0 / D, T1[:, :], ALU.mult, ALU.add).then_inc(sem("var"), 1)
                v.wait_ge(sem("std"), ORDER.index(st) + 1)
                line.step(v, v.reciprocal(RSTD[:, :], T1[:, :]))
                line.step(v, v.tensor_tensor(RSTD[:, :], RSTD[:, :], MASK[:, :], ALU.mult))
                line.step(v, v.scalar_tensor_tensor(NMR[:, :], MEAN[:, :], -1.0, RSTD[:, :], ALU.mult, ALU.mult))
                line.step(v, v.tensor_scalar(ONEP[:, :], RSTD[:, :], 1.0, None, ALU.add))

            def ln_apply(st, c, j, keep):
                t = c * CH + j
                v.wait_ge(sem("tp"), tiles_before(st) + AHEAD + t + 1 - CH)
                v.tensor_scalar(XS[:, j * D:(j + 1) * D], tile(X, t), MEAN[:, ds(t, 1)], RSTD[:, ds(t, 1)],
                                ALU.subtract, ALU.mult).then_inc(sem("xs"), 1)
                if keep:
                    line.mark(v.tensor_scalar(tile(X, t), tile(X, t), ONEP[:, ds(t, 1)], NMR[:, ds(t, 1)], ALU.mult, ALU.add))

            def attention_columns(dst, left, right, w, done):
                for b in range(KB):
                    for k, vec in ((0, left), (1, right)):
                        line.step(v, v.tensor_tensor(TMP[:, 0:D], WG[:, b * GW:b * GW + D], vec, ALU.mult))
                        line.step(v, v.tensor_reduce(dst(b, k), TMP[:, 0:D].rearrange("p (h d) -> p h d", h=w), AX.X, ALU.add))
                v.sem_inc(sem(done), 1)

            v.wait_ge(sem("ld_x"), 32)
            v.wait_ge(sem("x_padded"), 1)
            ln_stats("g0")
            v.wait_ge(sem("ld_w0"), 16 * 3)
            v.wait_ge(sem("h_used"), 2 + 2 * H_EARLY)
            attention_columns(lambda b, k: WG[:, b * GW + D + 4 * k:b * GW + D + 4 * k + 4], CSTB[:, 0:D], CSTB[:, D:2 * D], 4, "g0_weights")

            def project(st, width, scaled):
                def body(c, more):
                    for j in range(CH):
                        at = ahead(c, j, 3, more)
                        if at:
                            ln_apply(st, *at, False)
                        t = c * CH + j
                        v.wait_ge(sem(f"{st}_mm"), AHEAD + t + 1)
                        if scaled:
                            ins = v.tensor_scalar(tile(ACC, t, width, ROW), PB[2 + j][:, 0:width], DINV[:, ds(t, 1)], None, ALU.mult)
                        else:
                            ins = v.tensor_copy(tile(ACC, t, min(width, ROW), ROW), PB[2 + j][:, 0:min(width, ROW)])
                            if width > ROW:
                                ins = v.tensor_copy(AD[:, ds(t * 8, 8)], PB[2 + j][:, ROW:width])
                        ins.then_inc(sem("rows"), 1)
                for j in range(3):
                    ln_apply(st, 0, j, False)
                chunks(v, body)

            project("g0", ROW, False)
            count(H_EARLY, H_TURNS - H_EARLY)
            v.wait_ge(sem("hist"), 1)
            v.tensor_copy(T1[:, :], PB[7][:, 0:NT]).then_inc(sem("hist_sb"), 1)
            v.wait_ge(sem("hist_sb"), 1)
            line.step(v, v.tensor_scalar(DEG[:, :], T1[:, :], 1.0, None, ALU.add))
            v.reciprocal(VAR[:, :], DEG[:, :]).then_inc(sem("deg"), 1)
            v.wait_ge(sem("totals"), 1)
            line.step(v, v.tensor_copy(SMALL[:, 0:NT], PB[6][:, 0:NT]))
            line.step(v, v.tensor_tensor_scan(SMALL[:, 32:32 + NT], SMALL[:, 0:NT], SMALL[:, 0:NT], 0.0, ALU.add, ALU.bypass))
            line.step(v, v.tensor_copy(SMALL[:, 64:64 + NT].bitcast(I32), SMALL[:, 32:32 + NT]))
            line.step(v, v.tensor_scalar(SMALL[:, 96:96 + NT].bitcast(I32), SMALL[:, 64:64 + NT].bitcast(I32), 7, None, ALU.arith_shift_right))
            line.step(v, v.tensor_copy(SMALL[:, 128:128 + NT], SMALL[:, 96:96 + NT].bitcast(I32)))
            line.step(v, v.scalar_tensor_tensor(SMALL[:, 160:160 + NT - 1], IOTA[:, 0:NT - 1], 1.0, SMALL[:, 128:128 + NT - 1], ALU.add, ALU.add))
            rank = SMALL[:, 160:160 + NT - 1].unsqueeze(1).to_broadcast([P, 4, NT - 1])
            le = SMALL[:, 200:200 + 4 * (NT - 1)].rearrange("p (k w) -> p k w", k=4)
            line.step(v, v.tensor_tensor(le, rank, IOTAP[:, :].unsqueeze(2).to_broadcast([P, 4, NT - 1]), ALU.is_le))
            line.step(v, v.tensor_reduce(SLF[:, 0:4], le, AX.X, ALU.add))
            line.step(v, v.tensor_tensor(SLF[:, 8:12], IOTAP[:, :], SLF[:, 0:4], ALU.subtract))
            line.step(v, v.tensor_scalar(SLF[:, 8:12], SLF[:, 8:12], float(ET - 1), None, ALU.min))
            v.tensor_copy(SLI[:, :], SLF[:, 8:12]).then_inc(sem("slot_tile"), 1)
            line.step(v, v.tensor_scalar(SMALL[:, 0:4], SLF[:, 8:12], 1366.0, None, ALU.mult))
            line.step(v, v.tensor_copy(SMALL[:, 4:8].bitcast(I32), SMALL[:, 0:4]))
            line.step(v, v.tensor_scalar(SMALL[:, 8:12].bitcast(I32), SMALL[:, 4:8].bitcast(I32), 16, None, ALU.arith_shift_right))
            line.step(v, v.tensor_copy(SMALL[:, 0:4], SMALL[:, 8:12].bitcast(I32)))
            line.step(v, v.scalar_tensor_tensor(SLF[:, 8:12], SMALL[:, 0:4], -float(RING), SLF[:, 8:12], ALU.mult, ALU.add))
            line.mark(v.tensor_scalar(SLF[:, 8:12], SLF[:, 8:12], float(ROW), None, ALU.mult))
            line.mark(v.tensor_scalar(SLF[:, 4:8], SLF[:, 0:4], float(ROW), None, ALU.mult))
            line.step(v, v.tensor_scalar(SLF[:, 0:4], SLF[:, 0:4], float(P), None, ALU.mult))
            v.wait_ge(sem("ld_slots"), 8 * 16)
            line.mark(v.tensor_copy(slot_srcf, slot_src))
            line.step(v, v.tensor_copy(slot_dstf, slot_dst))
            for k in range(4):
                ins = v.tensor_scalar(slot_dstf[:, k * P:(k + 1) * P], slot_dstf[:, k * P:(k + 1) * P], SLF[:, k:k + 1], None, ALU.subtract)
            ins.then_inc(sem("slot_rows"), 1)
            v.wait_ge(sem("ld_tsrc"), 32)
            v.tensor_copy(tile_srcf, tile_src).then_inc(sem("tile_rows"), 1)
            v.wait_ge(sem("slotsT"), 1)
            v.tensor_copy(SRCI[:, 0:SLOTS], PB[4][:, 0:SLOTS])
            v.tensor_copy(DREL[:, 0:SLOTS], PB[5][:, 0:SLOTS])
            v.tensor_copy(TSRC[:, 0:ET + GRP], PB[7][:, 0:ET + GRP])
            v.tensor_copy(TROW[:, :], PB[3][0:1, 0:512])
            v.memset(SRCI[:, SLOTS:], 0)
            v.memset(DREL[:, SLOTS:], -1.0)
            v.tensor_copy(WROW[:, :], PB[6][0:1, 0:512]).then_inc(sem("slots_ready"), 1)
            v.wait_ge(sem("slots_ready"), 1)

            v.wait_ge(sem("g0_gathered"), 16 * 2 * NT)
            heads = lambda buf: buf.rearrange("p (t c) -> p t c", c=ROW)
            al = ADS[:, 0:4 * NT].rearrange("p (t h) -> p t h", h=4)
            z2 = SMALL[:, 200:200 + 4 * NT].rearrange("p (t h) -> p t h", h=4)
            line.step(v, v.tensor_tensor(al, heads(ACC[:, :])[:, :, D:D + 4], heads(BIG[:, 0:NT * ROW])[:, :, D + 4:D + 8], ALU.add))
            line.step(v, v.tensor_scalar(z2, al, 0.01, None, ALU.mult))
            line.step(v, v.tensor_tensor(al, al, z2, ALU.max))
            line.step(v, v.tensor_reduce(T1[:, :], al, AX.X, ALU.max))
            v.tensor_tensor(al, al, T1[:, :].unsqueeze(2).to_broadcast([P, NT, 4]), ALU.subtract).then_inc(sem("g0_logit"), 1)
            v.wait_ge(sem("g0_exp"), 1)
            line.step(v, v.tensor_reduce(T1[:, :], al, AX.X, ALU.add))
            line.step(v, v.reciprocal(T2[:, :], T1[:, :]))
            line.step(v, v.tensor_tensor(T2[:, :], T2[:, :], MASK[:, :], ALU.mult))
            line.step(v, v.tensor_tensor(al, al, T2[:, :].unsqueeze(2).to_broadcast([P, NT, 4]), ALU.mult))
            per = 3
            byhead = lambda buf, h: buf.rearrange("p t (h d) -> p t h d", h=h)
            with v.Fori(0, NC) as c:
                line.enter(c, per)
                XS4 = byhead(XS[:, :].rearrange("p (t c) -> p t c", t=CH), 4)
                XC4 = byhead(chunk(X, c), 4)
                mean4 = TMP[:, 0:CH * 64].rearrange("p (t d) -> p t d", t=CH)
                line.step(v, v.tensor_tensor(XS4, byhead(chunk(BIG, c, D, ROW), 4),
                                             ADS[:, ds(c * CH * 4, CH * 4)].rearrange("p (t h) -> p t h", h=4).unsqueeze(3).to_broadcast([P, CH, 4, 64]), ALU.mult))
                line.step(v, v.tensor_reduce(mean4, XS4.rearrange("p t h d -> p t d h"), AX.X, ALU.add))
                line.step(v, v.tensor_tensor(XC4, XC4, mean4.unsqueeze(2).to_broadcast([P, CH, 4, 64]), ALU.add))
                chunk_stats(c)
            line.leave(NC, per)

            moments("f0")
            v.wait_ge(sem("ld_f0"), 16 * 6)
            with v.Fori(0, NC) as c:
                line.enter(c, CH)
                for j in range(CH):
                    t = c * CH + j
                    line.mark(v.scalar_tensor_tensor(XS[:, j * D:(j + 1) * D], tile(X, t), MEAN[:, ds(t, 1)], CSTB[:, 3 * D:4 * D], ALU.subtract, ALU.mult,
                                                     accum_out=T1[:, ds(t, 1)]))
                line.sync(v)
            line.leave(NC, CH)
            line.step(v, v.tensor_tensor(T1[:, :], T1[:, :], RSTD[:, :], ALU.mult))
            line.mark(v.tensor_scalar(T2[:, :], MASK[:, :], BIG_NUM, -BIG_NUM, ALU.mult, ALU.add))
            line.step(v, v.tensor_scalar(T1[:, :], T1[:, :], SLF[:, 15:16], None, ALU.add))
            v.tensor_tensor(COEF[:, :], T1[:, :], T2[:, :], ALU.add).then_inc(sem("f0_score"), 1)
            SC = SMALL[:, 400:400 + 3 * NT]
            line.step(v, v.memset(SC, 0.0))
            NODE_SCORE = SMALL[:, 500:500 + NT]
            line.step(v, v.tensor_copy(NODE_SCORE, COEF[:, :]))

            def coefficients(c):
                for t in range(c * CH, (c + 1) * CH):
                    score = NODE_SCORE[:, t:t + 1]
                    line.mark(v.tensor_scalar(JUNK[:, t * P:NT * P], RANKROW[:, t * P:NT * P], score, 0.0, ALU.is_gt, ALU.add, accum_out=SC[:, t:t + 1]))
                    if t:
                        line.mark(v.tensor_scalar(JUNK[:, 0:t * P], RANKROW[:, 0:t * P], score, 0.0, ALU.is_ge, ALU.add, accum_out=SC[:, NT + t:NT + t + 1]))
                    line.step(v, v.scalar_tensor_tensor(OH[:, 0:P], RANKROW[:, t * P:(t + 1) * P], score, LOWER[:, :], ALU.is_equal, ALU.mult,
                                                        accum_out=SC[:, 2 * NT + t:2 * NT + t + 1]))
                cs = slice(c * CH, (c + 1) * CH)
                line.step(v, v.tensor_tensor(T1[:, cs], SC[:, 0:NT][:, cs], SC[:, NT:2 * NT][:, cs], ALU.add))
                line.step(v, v.tensor_tensor(T1[:, cs], T1[:, cs], SC[:, 2 * NT:3 * NT][:, cs], ALU.add))
                line.step(v, v.tensor_scalar(T1[:, cs], T1[:, cs], float(KSEL), None, ALU.is_lt))
                line.step(v, v.tensor_tensor(COEF[:, cs], T1[:, cs], NODE_SCORE[:, cs], ALU.mult))
            v.sem_inc(sem("f0_out"), AHEAD)
            for j in range(CH):
                ln_apply("f0", 0, j, True)
            for c in range(NC):
                if c + 1 < NC:
                    for j in range(CH):
                        ln_apply("f0", c + 1, j, True)
                if c == 0:
                    v.wait_ge(sem("f0_rankrow"), 16)
                coefficients(c)
                for j in range(CH):
                    t = c * CH + j
                    v.wait_ge(sem("f0_y"), t + 1)
                    v.tensor_tensor(TMP[:, (j % 2) * D:(j % 2 + 1) * D], PB[6 + j % 2][:, 0:D], CSTB[:, 2 * D:3 * D], ALU.add).then_inc(sem("f0_out"), 1)
                    v.wait_ge(sem("f0_out"), AHEAD + t + 1)
                    line.step(v, v.scalar_tensor_tensor(tile(X, t), TMP[:, (j % 2) * D:(j % 2 + 1) * D], COEF[:, t:t + 1], tile(X, t), ALU.mult, ALU.add))
                chunk_stats(c)

            def sum_slots(st, width):
                v.sem_inc(sem(f"{st}_acc"), BODY)

                def onehot(half, first):
                    v.tensor_tensor(OH[:, half * GRP * P:(half + 1) * GRP * P].rearrange("p (k n) -> p k n", k=GRP),
                                    IOTA[:, :].unsqueeze(1).to_broadcast([P, GRP, P]),
                                    DREL[:, ds(first, GRP)].unsqueeze(2).to_broadcast([P, GRP, P]), ALU.is_equal).then_inc(sem(f"{st}_oh"), 1)
                onehot(0, 0)
                regs = [v.alloc_register(f"{st}_row{k}") for k in range(GRP)]
                def body(i, groups):
                    for q in range(groups):
                        n0 = (i * TG + q) * GRP
                        v.wait_ge(sem(f"{st}_mm"), BODY + n0)
                        onehot((q + 1) % 2, n0 + GRP)
                        v.load(regs, WROW[0:1, ds(n0, GRP)])
                        for k in range(GRP):
                            row = v.snap(regs[k], min_val=0, max_val=(NT - 1) * ROW)
                            v.wait_ge(sem(f"{st}_mm"), BODY + n0 + k + 1)
                            v.wait_ge(sem(f"{st}_acc"), BODY + n0 + k)
                            dst = ACC[:, ds(row, width)]
                            v.tensor_tensor(dst, dst, PB[k][:, 0:width], ALU.add).then_inc(sem(f"{st}_acc"), 1)
                with v.Fori(0, S_GROUPS // TG) as i:
                    body(i, TG)
                body(S_GROUPS // TG, S_GROUPS % TG)
                v.wait_ge(sem(f"{st}_acc"), BODY + SLOTS)
                for r in regs:
                    v.free_register(r)

            def gcn(st, sums, bias):
                moments(st)
                v.wait_ge(sem("dinv"), 1)
                project(st, D, True)
                v.wait_ge(sem("table_stored"), (GNNS.index(st) + 1) * NC * 16)
                v.wait_ge(sem("rows"), rows_before(st) + AHEAD + NT)
                v.wait_ge(sem("ld_bias"), 16 * 5)
                line.step(v, v.tensor_tensor(T1[:, :], DEG[:, :], DINV[:, :], ALU.mult))
                with v.Fori(0, NC) as c:
                    line.enter(c, CH)
                    for j in range(CH):
                        t = c * CH + j
                        line.mark(v.scalar_tensor_tensor(tile(ACC, t, D, ROW), bias, T1[:, ds(t, 1)], tile(ACC, t, D, ROW), ALU.mult, ALU.add))
                line.leave(NC, CH)
                line.sync(v)
                sum_slots(sums, D)
                with v.Fori(0, NC) as c:
                    line.enter(c, 1)
                    v.wait_ge(sem(f"{sums}_relu"), (c + 1) * CH)
                    line.step(v, v.tensor_tensor(chunk(X, c), chunk(X, c), chunk(BIG, c), ALU.add))
                    chunk_stats(c)
                line.leave(NC, 1)

            gcn("g1", "a1", CSTB[:, 4 * D:5 * D])

            st = "t1"
            moments(st)
            v.wait_ge(sem("ld_t1"), 16 * 12)
            line.mark(v.tensor_copy(BXR.rearrange("p (h n) -> p h n", h=8), BX.unsqueeze(2).to_broadcast([64, 8, P])))
            line.mark(v.memset(TMP[:, 0:512], 0.0))
            line.mark(v.memset(WSUM, 0.0))
            line.step(v, v.tensor_scalar(TEMPC, TEMPC, 0.1, 5.0, ALU.max, ALU.min))
            v.reciprocal(RTEMP, TEMPC).then_inc(sem(f"{st}_bxr"), 1)
            v.wait_ge(sem(f"{st}_bxr"), 1)
            v.wait_ge(sem(f"{st}_wxs"), 1)
            g8 = lambda buf: buf.rearrange("p (h g) -> p h g", h=8)
            rt = RTEMP.unsqueeze(2).to_broadcast([P, 8, 64])
            line.mark(v.tensor_tensor(g8(WXS[:, 0:512]), g8(PB[0][:, :]), rt, ALU.mult))
            line.mark(v.tensor_tensor(g8(WXS[:, 512:1024]), g8(PB[1][:, :]), rt, ALU.mult))
            line.step(v, v.tensor_tensor(g8(LBIAS), g8(PB[2][:, :]), BSL.unsqueeze(1).to_broadcast([P, 8, 64]), ALU.add))
            v.tensor_tensor(g8(LBIAS), g8(LBIAS), rt, ALU.mult).then_inc(sem(f"{st}_fold"), 1)
            v.wait_ge(sem(f"{st}_fold"), 1)
            v.sem_inc(sem(f"{st}_lgc"), AHEAD)

            def apply(c, j):
                v.wait_ge(sem(f"{st}_tok"), AHEAD + c * CH + j + 1 - CH)
                ln_apply(st, c, j, False)

            def shift(c, j):
                n = c * CH + j
                w = SW[:, j * 512:(j + 1) * 512]
                v.wait_ge(sem(f"{st}_wsum"), AHEAD + n + 1 - CH)
                v.wait_ge(sem(f"{st}_lg"), AHEAD + n + 1)
                v.tensor_tensor(w, PB[2 + j % 2][:, :], LBIAS, ALU.add).then_inc(sem(f"{st}_lgc"), 1)
                v.wait_ge(sem(f"{st}_lgc"), AHEAD + n + 1)
                line.step(v, v.tensor_reduce(SMALL[:, j * 8:j * 8 + 8], g8(w), AX.X, ALU.max))
                v.tensor_tensor(g8(w), g8(w), SMALL[:, j * 8:j * 8 + 8].unsqueeze(2).to_broadcast([P, 8, 64]), ALU.subtract).then_inc(sem(f"{st}_sub"), 1)

            def normalise(c, j):
                n = c * CH + j
                w = SW[:, j * 512:(j + 1) * 512]
                sm = SMALL[:, 64 + j * 8:64 + j * 8 + 8]
                v.wait_ge(sem(f"{st}_exp"), n + 1)
                line.step(v, v.tensor_reduce(sm, g8(w), AX.X, ALU.add))
                line.step(v, v.reciprocal(sm, sm))
                v.tensor_scalar(sm, sm, MASK[:, ds(n, 1)], None, ALU.mult).then_inc(sem(f"{st}_rs"), 1)
                v.wait_ge(sem(f"{st}_rs"), n + 1)
                v.tensor_tensor(g8(w), g8(w), sm.unsqueeze(2).to_broadcast([P, 8, 64]), ALU.mult).then_inc(sem(f"{st}_sw"), 1)

            def body(c, more):
                for j in range(CH):
                    at = ahead(c, j, 3, more)
                    if at:
                        apply(*at)
                    normalise(c, j)
                    at = ahead(c, j, 1, more)
                    if at:
                        shift(*at)
            for j in range(3):
                apply(0, j)
            shift(0, 0)
            per = 3 * CH
            with v.Fori(0, NC - 1) as c:
                line.enter(c, per)
                body(c, True)
            line.leave(NC - 1, per)
            body(NC - 1, False)
            v.wait_ge(sem(f"{st}_sums"), 1)
            line.mark(v.tensor_copy(TOKT[:, 0:512], PB[4][:, :]))
            line.mark(v.tensor_copy(TOKT[:, 512:1024], PB[5][:, :]))
            line.step(v, v.tensor_copy(NORM, PB[6][0:1, :]))
            line.step(v, v.tensor_scalar(RN, NORM, 1e-5, None, ALU.add))
            v.reciprocal(RN, RN).then_inc(sem(f"{st}_norm"), 1)
            v.wait_ge(sem(f"{st}_tokens"), 1)
            line.step(v, v.tensor_copy(RNB, PB[1][0:64, :]))
            v.tensor_tensor(TOK, PB[0][0:64, :], RNB, ALU.mult).then_inc(sem(f"{st}_token"), 1)
            v.wait_ge(sem(f"{st}_qkv"), 1)
            line.mark(v.tensor_copy(QT, PB[2][0:64, :]))
            line.step(v, v.tensor_copy(KT, PB[3][0:64, :]))
            v.tensor_copy(VT, PB[4][0:64, :]).then_inc(sem(f"{st}_qkvc"), 1)
            v.wait_ge(sem(f"{st}_att"), 1)
            sm = SMALL[0:64, 0:8]
            smb = sm.unsqueeze(2).to_broadcast([64, 8, 64])
            line.step(v, v.tensor_reduce(sm, g8(PB[5][0:64, :]), AX.X, ALU.max))
            v.tensor_tensor(g8(ATT), g8(PB[5][0:64, :]), smb, ALU.subtract).then_inc(sem(f"{st}_sub2"), 1)
            v.wait_ge(sem(f"{st}_vw"), 1)
            for k in range(4):
                line.mark(v.tensor_copy(VW[:, k * 512:(k + 1) * 512], PB[k][0:64, :]))
            v.wait_ge(sem(f"{st}_exp2"), 1)
            line.step(v, v.tensor_reduce(sm, g8(ATT), AX.X, ALU.add))
            line.step(v, v.reciprocal(sm, sm))
            v.tensor_tensor(g8(ATT), g8(ATT), smb, ALU.mult).then_inc(sem(f"{st}_soft"), 1)
            v.wait_ge(sem(f"{st}_attT"), 1)
            v.tensor_copy(ATTT, PB[6][0:64, :]).then_inc(sem(f"{st}_attc"), 1)
            v.wait_ge(sem(f"{st}_m"), 1)
            for k in range(4):
                line.mark(v.tensor_copy(MM[0:64, k * D:(k + 1) * D], PB[k][0:64, 0:D]))
                ins = v.tensor_copy(MO[:, k * D:(k + 1) * D], PB[k][0:64, D:2 * D])
            ins.then_inc(sem(f"{st}_mout"), 1)
            def outputs(c, odd):
                for j in range(CH):
                    n = c * CH + j
                    v.wait_ge(sem(f"{st}_y"), n + 1)
                    v.tensor_tensor(tile(X, n), tile(X, n), PB[4 + (odd + j) % 2][:, 0:D], ALU.add).then_inc(sem(f"{st}_out"), 1)
                v.wait_ge(sem(f"{st}_out"), (c + 1) * CH)
                xc = chunk(X, c)
                line.step(v, v.tensor_tensor(xc, xc, BOUTB.unsqueeze(1).to_broadcast([P, CH, D]), ALU.add))
                chunk_stats(c)
            for c in range(NC):
                outputs(c, c % 2)

            gcn("g2", "a2", CSTB[:, 5 * D:6 * D])

            def first_of(row, best, onehot, tmp, n):
                r8 = lambda buf: buf.rearrange("p (n e) -> p n e", e=8)
                wide = lambda buf: buf.unsqueeze(2).to_broadcast([P, n, 8])
                iota8 = IOTA[:, 0:8].unsqueeze(1).to_broadcast([P, n, 8])
                line.step(v, v.tensor_reduce(best, r8(row), AX.X, ALU.max))
                line.step(v, v.tensor_tensor(r8(tmp), r8(row), wide(best), ALU.is_lt))
                line.step(v, v.scalar_tensor_tensor(r8(tmp), r8(tmp), 8.0, iota8, ALU.mult, ALU.add))
                line.step(v, v.tensor_reduce(onehot[:, 0:n], r8(tmp), AX.X, ALU.min))
                line.step(v, v.tensor_tensor(r8(tmp), iota8, wide(onehot[:, 0:n]), ALU.is_equal))
                line.step(v, v.tensor_copy(onehot, tmp))

            st = "m2"
            line.step(v, v.memset(COMBW, 0.0))
            v.memset(ACC[:, 0:CH * D], 0.0).then_inc(sem(f"{st}_b2zero"), 1)
            moments(st)
            v.wait_ge(sem("ld_m2"), 16 * 9)
            v.sem_inc(sem(f"{st}_out"), AHEAD)
            v.sem_inc(sem(f"{st}_b2"), AHEAD)
            r8 = lambda buf: buf.rearrange("p (n e) -> p n e", e=8)
            wide = lambda buf: buf.unsqueeze(2).to_broadcast([P, CH, 8])
            BEST, TOT, BEST2 = SMALL[:, 64:64 + CH], SMALL[:, 72:72 + CH], SMALL[:, 80:80 + CH]
            F1, F2, W8 = SMALL[:, 120:160], SMALL[:, 160:200], SMALL[:, 200:240]
            PROB = SMALL[:, 240:280]
            per = CH + 22
            for j in range(CH):
                ln_apply(st, 0, j, True)

            def body(c, more):
                v.wait_ge(sem(f"{st}_logits"), c + 1)
                line.step(v, v.tensor_reduce(BEST, r8(PB[1][:, 0:8 * CH]), AX.X, ALU.max))
                v.tensor_tensor(r8(COMB), r8(PB[1][:, 0:8 * CH]), wide(BEST), ALU.subtract).then_inc(sem(f"{st}_sub"), 1)
                v.wait_ge(sem(f"{st}_exp"), c + 1)
                line.step(v, v.tensor_reduce(TOT, r8(COMB), AX.X, ALU.add))
                line.step(v, v.reciprocal(TOT, TOT))
                line.step(v, v.tensor_tensor(r8(PROB), r8(COMB), wide(TOT), ALU.mult))
                first_of(PROB, BEST, F1, W8, CH)
                line.step(v, v.scalar_tensor_tensor(COMB, F1, -2.0, PROB, ALU.mult, ALU.add))
                first_of(COMB, BEST2, F2, W8, CH)
                line.step(v, v.tensor_tensor(TOT, BEST, BEST2, ALU.add))
                line.step(v, v.tensor_scalar(TOT, TOT, 1e-12, None, ALU.max))
                line.step(v, v.reciprocal(TOT, TOT))
                line.step(v, v.tensor_tensor(F1, F1, F2, ALU.add))
                line.step(v, v.tensor_tensor(F1, F1, PROB, ALU.mult))
                v.tensor_tensor(r8(COMB), r8(F1), wide(TOT), ALU.mult).then_inc(sem(f"{st}_comb"), 1)
                v.wait_ge(sem(f"{st}_comb"), c + 1)
                for e in range(8):
                    if e == 3 and more:
                        for j in range(CH):
                            ln_apply(st, c + 1, j, True)
                    if e == 7:
                        v.wait_ge(sem(f"{st}_combT"), c + 1)
                        v.tensor_copy(COMBT, PB[2][0:8 * CH, 0:P]).then_inc(sem(f"{st}_combTc"), 1)
                    for j in range(CH):
                        n = (c * 8 + e) * CH + j
                        v.wait_ge(sem(f"{st}_y"), n + 1)
                        v.wait_ge(sem(f"{st}_out"), AHEAD + n + 1 - CH)
                        v.scalar_tensor_tensor(tile(X, c * CH + j), PB[6 + (e * CH + j) % 2][:, 0:D], COMB[:, j * 8 + e:j * 8 + e + 1], tile(X, c * CH + j),
                                               ALU.mult, ALU.add).then_inc(sem(f"{st}_out"), 1)
                v.wait_ge(sem(f"{st}_b2y"), c + 1)
                v.wait_ge(sem(f"{st}_out"), AHEAD + (c + 1) * 8 * CH)
                for k in range(3):
                    w = min(512, CH * D - k * 512)
                    xx = X[:, ds(c * CH * D + k * 512, w)]
                    ins = v.tensor_tensor(xx, xx, PB[3 + k][:, 0:w], ALU.add)
                ins.then_inc(sem(f"{st}_b2"), 1)
                v.wait_ge(sem(f"{st}_b2"), AHEAD + c + 1)
                chunk_stats(c)
            with v.Fori(0, NC - 1) as c:
                line.enter(c, per)
                body(c, True)
            line.leave(NC - 1, per)
            body(NC - 1, False)
            line.sync(v)

            st = "g3"
            moments(st)
            v.wait_ge(sem("ld_wg"), 16 * 5)
            attention_columns(lambda b, k: WG[:, b * GW + D + 8 * k:b * GW + D + 8 * k + 8], CSTB[:, 0:D], CSTB[:, D:2 * D], 8, "g3_weights")
            project(st, 272, False)
            v.wait_ge(sem("rows"), rows_before(st) + AHEAD + NT)
            line.step(v, v.tensor_scalar(WHEAD, WROW[:, :], 255, None, ALU.bitwise_and))
            UM = SMALL[:, 800:808]
            line.step(v, v.tensor_reduce(UM, ACC[:, :].rearrange("p (t c) -> p c t", c=ROW)[:, D:D + 8, :], AX.X, ALU.max))
            v.sem_inc(sem(f"{st}_umax"), 1)
            v.wait_ge(sem(f"{st}_u"), 1)
            line.step(v, v.tensor_reduce(SMALL[0:8, 808:809], PB[0][0:8, 0:P], AX.X, ALU.max))
            v.tensor_scalar(SMALL[0:8, 816:824], IDENT[0:8, 0:8], SMALL[0:8, 808:809], None, ALU.mult).then_inc(sem(f"{st}_umax"), 1)
            v.wait_ge(sem(f"{st}_u"), 2)
            line.step(v, v.tensor_copy(UM, PB[0][:, 0:8]))
            h8 = lambda buf: buf.rearrange("p (t h) -> p t h", h=8)
            a_dst, bound, slope = AD[:, 0:8 * NT], AD[:, 8 * NT:16 * NT], SMALL[:, 850:850 + 8 * NT]
            line.step(v, v.tensor_tensor(h8(bound), h8(a_dst), UM.unsqueeze(1).to_broadcast([P, NT, 8]), ALU.add))
            line.step(v, v.tensor_scalar(slope, bound, 0.2, None, ALU.mult))
            v.tensor_tensor(bound, bound, slope, ALU.max).then_inc(sem(f"{st}_ad"), 1)
            v.wait_ge(sem("table_stored"), (GNNS.index(st) + 1) * NC * 16)
            line.step(v, v.memset(ACC[:, :], 0.0))

            st = "a3"
            v.sem_inc(sem(f"{st}_acc"), BODY)
            r8 = lambda buf: buf.rearrange("p (k h) -> p k h", h=8)

            def onehot(r, first):
                v.tensor_tensor(OH4[:, r * GRP * P:(r + 1) * GRP * P].rearrange("p (k n) -> p k n", k=GRP),
                                IOTA[:, :].unsqueeze(1).to_broadcast([P, GRP, P]),
                                DREL[:, ds(first, GRP)].unsqueeze(2).to_broadcast([P, GRP, P]), ALU.is_equal).then_inc(sem(f"{st}_oh"), 1)

            def logits(g, r, gathered):
                v.wait_ge(sem(f"{st}_in{r}"), gathered)
                v.wait_ge(sem(f"{st}_ad"), g + 1)
                rows = G[:, r * GRP * ROW:(r + 1) * GRP * ROW].rearrange("p (k c) -> p k c", c=ROW)
                terms = PB[6 + r % 2][:, 0:16 * GRP].rearrange("p (k c) -> p k c", c=16)
                z, low = r8(TMP[:, (r % 2) * 64:(r % 2 + 1) * 64]), r8(TMP[:, 128:192])
                line.step(v, v.tensor_tensor(z, rows[:, :, D:D + 8], terms[:, :, 0:8], ALU.add))
                line.step(v, v.tensor_scalar(low, z, 0.2, None, ALU.mult))
                line.step(v, v.tensor_tensor(z, z, low, ALU.max))
                v.tensor_tensor(z, z, terms[:, :, 8:16], ALU.subtract).then_inc(sem(f"{st}_z"), 1)

            def scale(g, r, first, count):
                if first == 0:
                    v.wait_ge(sem(f"{st}_exp"), g + 1)
                for k in range(first, first + count):
                    row = G[:, (r * GRP + k) * ROW:(r * GRP + k + 1) * ROW]
                    chans = row[:, 0:D].rearrange("p (h d) -> p h d", h=8)
                    ins = v.tensor_tensor(chans, chans, row[:, D:D + 8].unsqueeze(2).to_broadcast([P, 8, 32]), ALU.mult)
                if first + count == GRP:
                    ins.then_inc(sem(f"{st}_scaled"), 1)

            for r in range(3):
                onehot(r, r * GRP)
            logits(0, 0, 16 * GRP)
            scale(0, 0, 0, GRP)
            regs = [v.alloc_register(f"{st}_row{k}") for k in range(GRP)]
            per = 3

            def body(i, end):
                for q in range(NG):
                    g = i * NG + q
                    n0 = i * BODY + q * GRP
                    v.wait_ge(sem(f"{st}_mm"), BODY + n0)
                    if q + 3 < end:
                        onehot((q + 3) % NG, n0 + 3 * GRP)
                    v.load(regs, WROW[0:1, ds(n0, GRP)])
                    for k in range(GRP):
                        if q + 1 == end:
                            pass
                        elif k == 2:
                            logits(g + 1, (q + 1) % NG, 16 * GRP * (i + 1 + (q + 1) // NG))
                        elif k > 3:
                            scale(g + 1, (q + 1) % NG, (k - 4) * 2, 2)
                        row = v.snap(regs[k], min_val=0, max_val=(NT - 1) * ROW)
                        v.wait_ge(sem(f"{st}_mm"), BODY + n0 + k + 1)
                        v.wait_ge(sem(f"{st}_acc"), BODY + n0 + k)
                        dst = ACC[:, ds(row, ROW)]
                        v.tensor_tensor(dst, dst, PB[k % 4][:, 0:ROW], ALU.add).then_inc(sem(f"{st}_acc"), 1)
            with v.Fori(0, TURNS - 1) as i:
                line.enter(i, per * NG)
                body(i, 2 * NG)
            line.leave(TURNS - 1, per * NG)
            body(TURNS - 1, NG)
            v.wait_ge(sem(f"{st}_acc"), BODY + SLOTS)
            for r in regs:
                v.free_register(r)
            DEN = SMALL[:, 400:400 + 8 * NT]
            line.step(v, v.tensor_scalar(h8(DEN), ACC[:, :].rearrange("p (t c) -> p t c", c=ROW)[:, :, D:D + 8], 1e-16, None, ALU.add))
            line.step(v, v.reciprocal(DEN, DEN))
            def scaled_sums(c):
                acc = byhead(chunk(ACC, c, D, ROW), 8)
                v.tensor_tensor(acc, acc, DEN[:, ds(c * CH * 8, CH * 8)].rearrange("p (t h) -> p t h", h=8).unsqueeze(3).to_broadcast([P, CH, 8, 32]),
                                ALU.mult).then_inc(sem("a3_out"), 1)

            def body(c, more):
                if more:
                    scaled_sums(c + 1)
                v.wait_ge(sem("a3_biased"), c + 1)
                line.step(v, v.scalar_tensor_tensor(chunk(X, c), chunk(ACC, c, D, ROW), 0.0, chunk(X, c), ALU.max, ALU.add))
                chunk_stats(c)
            scaled_sums(0)
            with v.Fori(0, NC - 1) as c:
                line.enter(c, 1)
                body(c, True)
            line.leave(NC - 1, 1)
            body(NC - 1, False)

            st = "f3"
            moments(st)
            line.sync(v)
            v.tensor_reduce(SMALL[:, 0:1], NMR[:, :], AX.X, ALU.add).then_inc(sem(f"{st}_stats"), 1)
            v.wait_ge(sem(f"{st}_mean"), 1)
            v.tensor_scalar(OH[0:1, D:2 * D], PB[0][0:1, 0:D], 1.0 / N_NODES, None, ALU.mult).then_inc(sem(f"{st}_mean_sb"), 1)
            v.wait_ge(sem(f"{st}_mean"), 2)
            for b in range(KB):
                ins = v.tensor_copy(OH[:, b * P:(b + 1) * P], PB[3 + b][:, 0:P])
            ins.then_inc(sem(f"{st}_mean_sb"), 1)
            R, S1, P2 = SMALL[:, 16:24], SMALL[:, 24:25], SMALL[:, 32:40]
            v.wait_ge(sem(f"{st}_logits"), 1)
            v.wait_ge(sem("ld_wr"), 32)

            def softmax8(n):
                line.step(v, v.tensor_reduce(S1, R, AX.X, ALU.max))
                v.tensor_scalar(R, R, S1, None, ALU.subtract).then_inc(sem(f"{st}_sub"), 1)
                v.wait_ge(sem(f"{st}_exp"), n)
                line.step(v, v.tensor_reduce(S1, R, AX.X, ALU.add))
                line.step(v, v.reciprocal(S1, S1))
                line.step(v, v.tensor_scalar(R, R, S1, None, ALU.mult))
            line.step(v, v.tensor_tensor(R, PB[2][:, 0:8], BR, ALU.add))
            softmax8(1)
            line.step(v, v.tensor_scalar(P2, R, float(N_NODES), None, ALU.mult))
            line.step(v, v.reciprocal(P2, P2))
            line.step(v, v.tensor_scalar(P2, P2, CAP3, 1.0, ALU.mult, ALU.min))
            line.step(v, v.tensor_tensor(R, R, P2, ALU.mult))
            softmax8(2)
            B1_, B2_, F1, F2, W8 = SMALL[:, 40:41], SMALL[:, 41:42], SMALL[:, 64:72], SMALL[:, 72:80], SMALL[:, 80:88]
            first_of(R, B1_, F1, W8, 1)
            line.step(v, v.scalar_tensor_tensor(R, F1, -2.0, R, ALU.mult, ALU.add))
            first_of(R, B2_, F2, W8, 1)
            for k, F in ((0, F1), (1, F2)):
                line.step(v, v.tensor_tensor(W8, F, IOTA[:, 0:8], ALU.mult))
                line.step(v, v.tensor_reduce(SMALL[:, 42 + k:43 + k], W8, AX.X, ALU.add))
            v.tensor_copy(CHOSEN[:, :], SMALL[0:1, 42:44]).then_inc(sem(f"{st}_chosen"), 1)
            v.tensor_scalar(SMALL[:, 48:49], B2_, B1_, None, ALU.subtract).then_inc(sem(f"{st}_sub"), 1)
            v.wait_ge(sem(f"{st}_exp"), 3)
            line.step(v, v.tensor_scalar(SMALL[:, 49:50], SMALL[:, 48:49], 1.0, None, ALU.add))
            line.step(v, v.reciprocal(SMALL[:, 50:51], SMALL[:, 49:50]))
            line.step(v, v.tensor_tensor(SMALL[:, 51:52], SMALL[:, 48:49], SMALL[:, 50:51], ALU.mult))
            for j in range(CH):
                ln_apply(st, 0, j, False)
            v.wait_ge(sem("ld_f3b"), 16 * 4)
            for k in range(2):
                w = WB[:, k * 1024:(k + 1) * 1024]
                line.mark(v.tensor_scalar(w, w, SMALL[:, 50 + k:51 + k], None, ALU.mult))
            line.step(v, v.tensor_scalar(CSTB[:, 0:D], CSTB[:, 0:D], SMALL[:, 50:51], None, ALU.mult))
            v.scalar_tensor_tensor(CSTB[:, 0:D], CSTB[:, D:2 * D], SMALL[:, 51:52], CSTB[:, 0:D], ALU.mult, ALU.add).then_inc(sem(f"{st}_weights"), 1)
            v.wait_ge(sem(f"{st}_weights"), 1)
            v.sem_inc(sem(f"{st}_out"), AHEAD)
            FIN = OH[:, 0:CH * D]
            M3, V3, S3, A3, C3 = (SMALL[:, 100 + 8 * k:100 + 8 * k + CH] for k in range(5))

            def out_moments(c):
                v.wait_ge(sem("bn"), tiles_before("n3") + (c + 1) * CH)
                s6 = ST6[:, ds(c * CH * 6, CH * 6)].rearrange("p (t k) -> p k t", k=6)
                line.mark(v.tensor_tensor(A3, s6[:, 1, :], s6[:, 4, :], ALU.subtract))
                line.mark(v.tensor_tensor(M3, s6[:, 1, :], s6[:, 4, :], ALU.add))
                line.step(v, v.tensor_tensor(C3, s6[:, 2, :], s6[:, 5, :], ALU.add))
                line.step(v, v.tensor_tensor(A3, A3, A3, ALU.mult))
                line.mark(v.tensor_scalar(M3, M3, 0.5, None, ALU.mult))
                line.step(v, v.tensor_scalar(A3, A3, 0.25, LN_EPS, ALU.mult, ALU.add))
                v.scalar_tensor_tensor(V3, C3, 1.0 / D, A3, ALU.mult, ALU.add).then_inc(sem("var"), 1)

            def finish(c):
                v.wait_ge(sem("std"), ORDER.index("n3") + c + 1)
                line.step(v, v.reciprocal(S3, S3))
                FINC = FIN.rearrange("p (t c) -> p t c", t=CH)
                wide = lambda n: CSTB[:, n * D:(n + 1) * D].unsqueeze(1).to_broadcast([P, CH, D])
                for j in range(CH):
                    line.mark(v.tensor_scalar(FIN[:, j * D:(j + 1) * D], tile(ACC, c * CH + j, D, ROW), M3[:, j:j + 1], S3[:, j:j + 1], ALU.subtract, ALU.mult))
                line.sync(v)
                line.step(v, v.tensor_tensor(FINC, FINC, wide(7), ALU.mult))
                line.step(v, v.tensor_tensor(FINC, FINC, wide(8), ALU.add))
                v.tensor_tensor(chunk(X, c), chunk(X, c), FINC, ALU.add).then_inc(sem("finished"), 1)
                v.wait_ge(sem("finished"), c + 1)

            def body(c, first, more):
                v.wait_ge(sem("xs"), tiles_before(st) + c * CH + CH)
                for j in range(CH):
                    line.mark(v.tensor_tensor(tile(ACC, c * CH + j, D, ROW), XS[:, j * D:(j + 1) * D], CSTB[:, 0:D], ALU.add))
                line.sync(v)
                if more:
                    for j in range(CH):
                        ln_apply(st, c + 1, j, False)
                if not first:
                    finish(c - 1)
                for j in range(CH):
                    t = c * CH + j
                    o = tile(ACC, t, D, ROW)
                    v.wait_ge(sem(f"{st}_y"), t + 1)
                    v.tensor_tensor(o, PB[6 + j % 2][:, 0:D], o, ALU.add).then_inc(sem(f"{st}_out"), 1)
                    v.wait_ge(sem(f"{st}_out"), AHEAD + t + 1)
                    v.bn_stats(tile(ST6, t, 6, 6), o).then_inc(sem("bn"), 1)
                out_moments(c)
            body(0, True, True)
            per = CH + 6 + 1 + CH + 2
            with v.Fori(0, NC - 2) as i:
                line.enter(i, per)
                body(i + 1, False, True)
            line.leave(NC - 2, per)
            body(NC - 1, False, False)
            finish(NC - 1)


def kernel(**inputs):
    import numpy as _np
    import concourse.bacc as _bacc
    from concourse import mybir as _mybir
    from concourse.bass_utils import run_bass_kernel_spmd as _run

    nc = _bacc.Bacc("TRN2", target_bir_lowering=False, num_devices=1)
    pad = ET * P - N_EDGES
    laid = dict(inputs)
    laid["src"] = _np.concatenate([inputs["src"], _np.zeros(pad, _np.int32)])
    laid["dst"] = _np.concatenate([inputs["dst"], _np.full(pad, 4095, _np.int32)])
    laid["L1_ffn_W_xT"] = _np.transpose(inputs["L1_ffn_W_x"])
    laid["L2_ffn_router_wT"] = _np.transpose(inputs["L2_ffn_router_w"])
    arrays, args = {}, {}
    for name in laid:
        x = _np.ascontiguousarray(laid[name])
        arrays[f"in_{name}"] = x
        args[name] = nc.dram_tensor(f"in_{name}", x.shape, _mybir.dt.from_np(x.dtype), kind="ExternalInput").ap()
    out = nc.dram_tensor("out_0", (N_NODES, D), F32, kind="ExternalOutput").ap()
    build(nc, args, out)
    r = _run(nc, [arrays], core_ids=[0])
    return r.results[0]["out_0"]
```
